# Optimizing a Trainium2 kernel written in Bass

```python
import numpy as np
import jax
import jax.numpy as jnp

def _softmax(x, axis=-1):
    return jax.nn.softmax(x, axis=axis)

def _gelu(x):
    return jax.nn.gelu(x, approximate=True)

def _silu(x):
    return jax.nn.silu(x)

def _sigmoid(x):
    return jax.nn.sigmoid(x)

def _layernorm(x, axis=-1, eps=1e-05):
    m = jnp.mean(x, axis=axis, keepdims=True)
    v = jnp.var(x, axis=axis, keepdims=True)
    return (x - m) / jnp.sqrt(v + eps)

def _scatter_add(tgt, idx, src, axis=0):
    return tgt.at[idx].add(src)

def _segment_sum(src, seg, n):
    return jax.ops.segment_sum(src, seg, n)
kernel_name = 'mk_seq_preln_d1_jaxref_r4_557a3c'

def setup_inputs(seed: int=0):
    np.random.seed(seed)
    _w = jnp.asarray

    def _L0_attn_setup():
        import jax, jax.numpy as jnp
        import numpy as np
        EMBED_DIM = 256
        N_HEADS = 16
        HEAD_DIM = EMBED_DIM // N_HEADS
        MAX_REL = 128
        B, S = (4, 256)
        key = jax.random.key(seed)
        ks = jax.random.split(key, 10)
        sc = 1.0 / np.sqrt(EMBED_DIM)
        return {'q': jax.random.normal(ks[0], (B, S, EMBED_DIM), jnp.float32), 'Wq': jax.random.normal(ks[1], (EMBED_DIM, EMBED_DIM), jnp.float32) * sc, 'bq': jax.random.normal(ks[2], (EMBED_DIM,), jnp.float32) * 0.02, 'Wk': jax.random.normal(ks[3], (EMBED_DIM, EMBED_DIM), jnp.float32) * sc, 'bk': jax.random.normal(ks[4], (EMBED_DIM,), jnp.float32) * 0.02, 'Wv': jax.random.normal(ks[5], (EMBED_DIM, EMBED_DIM), jnp.float32) * sc, 'bv': jax.random.normal(ks[6], (EMBED_DIM,), jnp.float32) * 0.02, 'Wo': jax.random.normal(ks[7], (EMBED_DIM, EMBED_DIM), jnp.float32) * sc, 'bo': jax.random.normal(ks[8], (EMBED_DIM,), jnp.float32) * 0.02, 'rel_table': jax.random.normal(ks[9], (2 * MAX_REL + 1, HEAD_DIM), jnp.float32) * 0.02}
    _L0_attn_in = _L0_attn_setup()

    def _L0_ffn_setup():
        import jax, jax.numpy as jnp
        import numpy as np
        E, H, I = (8, 256, 1024)
        B, S = (4, 512)
        key = jax.random.key(seed)
        k0, k1, k2, k3 = jax.random.split(key, 4)
        s = 0.02
        return {'hidden_states': jax.random.normal(k0, (B, S, H), dtype=jnp.float32), 'w1': jax.random.normal(k1, (E, H, I), dtype=jnp.float32) * s, 'b1': jnp.zeros((E, I), dtype=jnp.float32), 'w2': jax.random.normal(k2, (E, I, H), dtype=jnp.float32) * s, 'b2': jnp.zeros((E, H), dtype=jnp.float32), 'wr': jax.random.normal(k3, (H, E), dtype=jnp.float32) * s, 'br': jnp.zeros((E,), dtype=jnp.float32)}
    _L0_ffn_in = _L0_ffn_setup()
    _d = {'L0_attn_q': _L0_attn_in['q'], 'L0_attn_Wq': _L0_attn_in['Wq'], 'L0_attn_bq': _L0_attn_in['bq'], 'L0_attn_Wk': _L0_attn_in['Wk'], 'L0_attn_bk': _L0_attn_in['bk'], 'L0_attn_Wv': _L0_attn_in['Wv'], 'L0_attn_bv': _L0_attn_in['bv'], 'L0_attn_Wo': _L0_attn_in['Wo'], 'L0_attn_bo': _L0_attn_in['bo'], 'L0_attn_rel_table': _L0_attn_in['rel_table'], 'L0_ffn_w1': _L0_ffn_in['w1'], 'L0_ffn_b1': _L0_ffn_in['b1'], 'L0_ffn_w2': _L0_ffn_in['w2'], 'L0_ffn_b2': _L0_ffn_in['b2'], 'L0_ffn_wr': _L0_ffn_in['wr'], 'L0_ffn_br': _L0_ffn_in['br']}
    _x0 = _d['L0_attn_q']
    _d['L0_attn_q'] = jax.random.normal(jax.random.fold_in(jax.random.key(seed), 1), (2, 2048, 256), dtype=_x0.dtype)
    del _x0
    return _d

def reference(L0_attn_q, L0_attn_Wq, L0_attn_bq, L0_attn_Wk, L0_attn_bk, L0_attn_Wv, L0_attn_bv, L0_attn_Wo, L0_attn_bo, L0_attn_rel_table, L0_ffn_w1, L0_ffn_b1, L0_ffn_w2, L0_ffn_b2, L0_ffn_wr, L0_ffn_br):

    def _L0_attn_ref(q, Wq, bq, Wk, bk, Wv, bv, Wo, bo, rel_table):
        import jax, jax.numpy as jnp
        import numpy as np
        EMBED_DIM = 256
        N_HEADS = 16
        HEAD_DIM = EMBED_DIM // N_HEADS
        MAX_REL = 128
        B, S = (4, 256)
        b, s, e = q.shape
        h, d = (N_HEADS, HEAD_DIM)
        Q = (q @ Wq + bq).reshape(b, s, h, d).transpose(0, 2, 1, 3)
        K = (q @ Wk + bk).reshape(b, s, h, d).transpose(0, 2, 1, 3)
        V = (q @ Wv + bv).reshape(b, s, h, d).transpose(0, 2, 1, 3)
        scores = jnp.einsum('bhid,bhjd->bhij', Q, K) / jnp.sqrt(jnp.asarray(d, q.dtype))
        pos = jnp.arange(s)
        rel_idx = jnp.clip(pos[None, :] - pos[:, None] + MAX_REL, 0, 2 * MAX_REL)
        rel_emb = rel_table[rel_idx]
        scores = scores + jnp.einsum('bhid,ijd->bhij', Q, rel_emb)
        attn = jax.nn.softmax(scores, axis=-1)
        ctx = jnp.einsum('bhij,bhjd->bhid', attn, V)
        ctx = ctx.transpose(0, 2, 1, 3).reshape(b, s, e)
        return ctx @ Wo + bo

    def _L0_ffn_ref(hidden_states, w1, b1, w2, b2, wr, br):
        import jax, jax.numpy as jnp
        import numpy as np
        E, H, I = (8, 256, 1024)
        B, S = (4, 512)
        b, s, h = hidden_states.shape
        x = hidden_states.reshape(-1, h)
        logits = x @ wr + br
        probs = jax.nn.softmax(logits, axis=-1)
        top_p, top_i = jax.lax.top_k(probs, 2)
        gate = top_p[:, 0] / (top_p[:, 0] + top_p[:, 1])
        top1 = top_i[:, 0]
        out = jnp.zeros_like(x)
        n_experts = w1.shape[0]
        for e in range(n_experts):
            hmid = jax.nn.gelu(x @ w1[e] + b1[e], approximate=False)
            hout = hmid @ w2[e] + b2[e]
            mask = top1 == e
            out = out + jnp.where(mask[:, None], hout * gate[:, None], 0.0)
        return out.reshape(b, s, h)
    x = L0_attn_q
    x = x + _L0_attn_ref(_layernorm(x, axis=-1), L0_attn_Wq, L0_attn_bq, L0_attn_Wk, L0_attn_bk, L0_attn_Wv, L0_attn_bv, L0_attn_Wo, L0_attn_bo, L0_attn_rel_table)
    x = x + _L0_ffn_ref(_layernorm(x, axis=-1), L0_ffn_w1, L0_ffn_b1, L0_ffn_w2, L0_ffn_b2, L0_ffn_wr, L0_ffn_br)
    return x

_drawn_inputs = setup_inputs


def setup_inputs(seed=0):
    import zlib

    import numpy as np

    out = dict(_drawn_inputs(seed))
    spreads = {'L0_ffn_b1': (0.0, 0.409), 'L0_ffn_b2': (0.0, 0.1), 'L0_ffn_br': (0.0, 0.1)}
    factors = {'L0_attn_bq': 24.828, 'L0_attn_bk': 64.0, 'L0_attn_rel_table': 8.0}
    for name, (base, spread) in spreads.items():
        noise = np.random.default_rng([zlib.crc32(name.encode()), seed]).standard_normal(out[name].shape)
        drawn = base * np.exp(spread * noise) if base else spread * noise
        out[name] = jnp.asarray(drawn.astype(out[name].dtype))
    for name, factor in factors.items():
        out[name] = (out[name] * factor).astype(out[name].dtype)
    return out
```

```python
import concourse.bass as bass
from concourse import mybir
from contextlib import ExitStack

fp32 = mybir.dt.float32
bf16 = mybir.dt.bfloat16
fp16 = mybir.dt.float16
i32 = mybir.dt.int32
u32 = mybir.dt.uint32
ALU = mybir.AluOpType
ACT = mybir.ActivationFunctionType
AX = mybir.AxisListType
ds = bass.ds

P = 128
B, S, E = 2, 2048, 256
H, D = 16, 16
MAXREL = 128
NREL = 2 * MAXREL + 1
N = B * S
NT = N // P
ST = S // P
BH = B * H
NE, FI = 8, 1024
EPS = 1e-5

Q_PARTS = ("h", "m", "l", "h", "m", "h")
K_PARTS = ("h", "h", "h", "m", "m", "l")
PR = len(Q_PARTS) * D
R_LEFT, R_MAX, R_RIGHT = PR, PR + 3, PR + 5
QR = PR + 8
EXT = S // 4 - 1
VC = 32
EC = 4 * P
NC_ = N // EC

SLOT_TILES = NT + NE - 1
SLOTS = (SLOT_TILES + 1) * P


def sem_wait(eng, sem, value):
    if isinstance(value, int) and value <= 0:
        return
    eng.wait_ge(sem, value)


def wait_apart(eng, sem, value, tick):
    sem_wait(eng, sem, value)
    eng.sem_inc(tick, 1)


def rounds(eng, n, body):
    body(0)
    if n > 1:
        with eng.Fori(1, n) as i:
            body(i)


def project(nc, io, hbm):
    with ExitStack() as ctx:
        sb = lambda n, s, d=fp32: ctx.enter_context(nc.sbuf_tensor(n, s, d))
        sem = lambda n: ctx.enter_context(nc.semaphore(n))
        ident = sb("p_ident", [P, P])
        wq, wk, wv = (sb(f"p_w{n}", [P, 2, E]) for n in "qkv")
        bq, bk, bk4 = sb("p_bq", [P, 2]), sb("p_bk", [P, 2]), sb("p_bk4", [P, 2])
        bv = sb("p_bv", [P, E])
        eps = sb("p_eps", [P, 1])
        x = sb("p_x", [P, 2, 4, E])
        stats = sb("p_stats", [P, 2, 4, 6])
        mv = sb("p_mv", [P, 2, 4, 2])
        sd = sb("p_sd", [P, 2, 4])
        rs = sb("p_rs", [P, 2, 4])
        xn = sb("p_xn", [P, 2, 4, E])
        xt = sb("p_xt", [P, 2, 2, EC])
        full = {n: sb(f"p_{n}f", [P, 2, 2, EC]) for n in "qk"}
        rest = {n: sb(f"p_{n}r", [P, 2, EC]) for n in "qk"}
        part = {(n, w): sb(f"p_{n}{w}", [P, 2, 2, EC], bf16) for n in "qk" for w in "hml"}
        v = sb("p_v", [P, 2, H, 4, VC])
        relt = sb("p_relt", [D, NREL])
        rele = sb("p_rele", [D, EXT + 1])
        relz = sb("p_relz", [D, P])
        relr = sb("p_relr", [D, EXT + 1])
        relp = {w: sb(f"p_rel{w}", [D, EXT + 1], bf16) for w in "hml"}
        flags = sb("p_flags", [H, 2, N], bf16)
        zeros = sb("p_zeros", [P, 8 * E])
        pt = ctx.enter_context(nc.psum_tensor("p_pt", [P, 2, EC], fp32))
        pq = ctx.enter_context(nc.psum_tensor("p_pq", [P, 2, EC], fp32))
        pk = ctx.enter_context(nc.psum_tensor("p_pk", [P, 2, EC], fp32))
        pv = ctx.enter_context(nc.psum_tensor("p_pv", [P, 4, E], fp32))

        weights_in, rel_in = sem("p_weights_in"), sem("p_rel_in")
        x_in = [sem(f"p_x_in{k}") for k in range(2)]
        ident_done, init_done = sem("p_ident_done"), sem("p_init_done")
        tick_v, tick_p = sem("p_tick_v"), sem("p_tick_p")
        flags_done, flags_stored = sem("p_flags_done"), sem("p_flags_stored")
        eps_done, bk4_done = sem("p_eps_done"), sem("p_bk4_done")
        stats_done, mv_done, sd_done, rs_done, xn_done = (sem(f"p_{n}") for n in ("stats_d", "mv_d", "sd_d", "rs_d", "xn_d"))
        turned, xt_done = sem("p_turned"), sem("p_xt_done")
        q_done, k_done, v_done = sem("p_q_done"), sem("p_k_done"), sem("p_v_done")
        qf_done, kf_done = sem("p_qf_done"), sem("p_kf_done")
        q_split, k_split, vb_done = sem("p_q_split"), sem("p_k_split"), sem("p_vb_done")
        stored = [sem(f"p_stored{k}") for k in range(2)]
        rel_done, rel_stored = sem("p_rel_done"), sem("p_rel_stored")

        x_h = io["L0_attn_q"].rearrange("b (c t p) e -> p (b c) t e", p=P, t=4)
        STORES = 2 * 6 * 2 + 1

        with nc.Block() as block:

            @block.sync
            def _(sp):
                def load(k, c):
                    sp.dma_start(x[:, k], x_h[:, ds(c, 1)].rearrange("p c t e -> p (c t) e")).then_inc(x_in[k], 16)

                for k in range(2):
                    load(k, k)
                for w, name in ((wq, "Wq"), (wk, "Wk"), (wv, "Wv")):
                    sp.dma_start(w[:], io[f"L0_attn_{name}"].rearrange("(c p) n -> p c n", p=P)).then_inc(weights_in, 16)
                with nc.allow_non_contiguous_dma(reason="a bias to a column, once"):
                    for b_, name in ((bq, "bq"), (bk, "bk")):
                        sp.dma_start(b_[:], io[f"L0_attn_{name}"].rearrange("(c p) -> p c", p=P)).then_inc(weights_in, 16)
                sp.dma_start(bv[:], io["L0_attn_bv"].rearrange("(a n) -> a n", a=1).to_broadcast([P, E])).then_inc(weights_in, 16)

                def stores(i):
                    for k in range(2):
                        c = 2 * i + k
                        for n, split, rows in (("q", q_split, Q_PARTS), ("k", k_split, K_PARTS)):
                            for w, need in (("h", 1), ("m", 3), ("l", 4)):
                                sp.wait_ge(split, 4 * c + need)
                                for r, which in enumerate(rows):
                                    if which == w:
                                        to = hbm[n].rearrange("(m g) r t -> g r m t", m=2)[:, D * r:D * r + D, :, ds(c * EC, EC)]
                                        for m in range(2):
                                            sp.dma_start(to[:, :, m], part[n, w][:, k, m]).then_inc(stored[k], 16)
                        sp.wait_ge(vb_done, 4 * c + 4)
                        sp.dma_start(hbm["v"].rearrange("h p t c -> p h t c")[:, :, ds(c * 4, 4)],
                                     v[:, k]).then_inc(stored[k], 16)

                def loads(i):
                    for k in range(2):
                        sp.wait_ge(xn_done, 8 * i + 4 * k + 4)
                        load(k, 2 * i + k + 2)

                loads(0)
                stores(0)
                with sp.Fori(1, NC_ // 2 - 1) as i:
                    loads(i)
                    stores(i)
                stores(NC_ // 2 - 1)
                for k in range(2):
                    sp.wait_ge(stored[k], 16 * STORES * (NC_ // 2))

            @block.gpsimd
            def _(pool):
                pool.memset(ident[:], 0.0).then_inc(ident_done, 1)
                pool.memset(v[:], 0.0).then_inc(init_done, 1)
                pool.wait_ge(init_done, 1)
                pool.memset(v[:, :, :, :, D:D + 1], 1.0).then_inc(init_done, 1)
                pool.wait_ge(ident_done, 1)
                pool.affine_select(out=ident[:], in_=ident[:], compare_op=ALU.not_equal, fill=1.0, base=0,
                                   pattern=[[-1, P]], channel_multiplier=1).then_inc(ident_done, 1)
                with nc.allow_non_contiguous_dma(reason="a small table turned, once"):
                    pool.dma_start(relt[:], io["L0_attn_rel_table"].rearrange("r d -> d r")).then_inc(rel_in, 16)
                pool.memset(zeros[:], 0.0).then_inc(flags_done, 1)
                pool.wait_ge(flags_done, 1)
                for t in range(0, SLOTS, 8 * P):
                    pool.dma_start(hbm["xs"][t:t + 8 * P].rearrange("(p t) e -> p (t e)", p=P), zeros[:]).then_inc(flags_stored, 16)
                pool.memset(flags[:, 0], 0.0).then_inc(flags_done, 1)
                pool.memset(flags[:, 1], 1.0).then_inc(flags_done, 1)
                pool.wait_ge(flags_done, 3)
                for row in range(PR, QR):
                    pool.dma_start(hbm["k"][:, row, :], flags[:, int(R_MAX <= row < R_RIGHT)]).then_inc(flags_stored, 16)
                pool.wait_ge(init_done, 2)

                def split_keys(i):
                    for k in range(2):
                        c = 2 * i + k
                        f, r = full["k"][:, k], rest["k"]
                        h, m, l = (part["k", w][:, k] for w in "hml")
                        pool.wait_ge(kf_done, 2 * c + 2)
                        wait_apart(pool, stored[k], i * (16 * STORES), tick_p)
                        pool.tensor_copy(h, f).then_inc(k_split, 1)
                        pool.wait_ge(k_split, 4 * c + 1)
                        pool.tensor_tensor(r[:], f, h, ALU.subtract).then_inc(k_split, 1)
                        wait_apart(pool, k_split, 4 * c + 2, tick_p)
                        pool.tensor_copy(m, r[:]).then_inc(k_split, 1)
                        pool.wait_ge(k_split, 4 * c + 3)
                        pool.tensor_tensor(l, r[:], m, ALU.subtract).then_inc(k_split, 1)
                        pool.wait_ge(k_split, 4 * c + 4)

                rounds(pool, NC_ // 2, split_keys)
                pool.wait_ge(rel_done, 8)
                for r, w in enumerate(K_PARTS):
                    pool.dma_start(hbm["rel"][D * r:D * r + D, :], relp[w][:]).then_inc(rel_stored, 16)
                pool.wait_ge(rel_stored, 16 * len(K_PARTS))
                pool.wait_ge(flags_stored, 16 * (QR - PR + SLOTS // (8 * P)))

            @block.scalar
            def _(act):
                act.wait_ge(weights_in, 96)
                act.activation(bk4[:], bk[:], ACT.Copy, scale=D ** -0.5).then_inc(bk4_done, 1)
                act.wait_ge(bk4_done, 1)
                act.wait_ge(eps_done, 1)

                def chunk(i):
                    for k in range(2):
                        c = 2 * i + k
                        act.wait_ge(mv_done, 4 * c + 4)
                        act.activation(sd[:, k], mv[:, k, :, 1], ACT.Sqrt, bias=eps[:]).then_inc(sd_done, 1)
                        act.wait_ge(turned, c + 1)
                        act.activation(xt[:, k], pt[:], ACT.Copy).then_inc(xt_done, 1)
                        act.wait_ge(q_done, c + 1)
                        sem_wait(act, q_split, i * 8 + 4 * k - 4)
                        for m in range(2):
                            act.activation(full["q"][:, k, m], pq[:, m], ACT.Identity, bias=bq[:, m:m + 1]).then_inc(qf_done, 1)
                        act.wait_ge(k_done, c + 1)
                        sem_wait(act, k_split, i * 8 + 4 * k - 4)
                        for m in range(2):
                            act.activation(full["k"][:, k, m], pk[:, m], ACT.Identity, bias=bk4[:, m:m + 1],
                                           scale=D ** -0.5).then_inc(kf_done, 1)

                rounds(act, NC_ // 2, chunk)

            @block.tensor
            def _(pe):
                pe.wait_ge(ident_done, 2)
                pe.wait_ge(weights_in, 96)

                def chunk(i):
                    for k in range(2):
                        c = 2 * i + k
                        pe.wait_ge(xn_done, 4 * c + 4)
                        for t in range(4):
                            for e in range(2):
                                mm = pe.transpose(pt[:, e, t * P:(t + 1) * P], xn[:, k, t, e * P:(e + 1) * P], ident[:])
                        mm.then_inc(turned, 1)
                        pe.wait_ge(xt_done, c + 1)
                        for w, out, done, free, per in ((wq, pq, q_done, qf_done, 2), (wk, pk, k_done, kf_done, 2)):
                            sem_wait(pe, free, per * c)
                            for m in range(2):
                                for e in range(2):
                                    mm = pe.matmul(out[:, m], w[:, e, m * P:(m + 1) * P], xt[:, k, e], start=e == 0, stop=e == 1)
                            mm.then_inc(done, 1)
                        sem_wait(pe, vb_done, 4 * c)
                        for t in range(4):
                            for e in range(2):
                                mm = pe.matmul(pv[:, t], xt[:, k, e, t * P:(t + 1) * P], wv[:, e], start=e == 0, stop=e == 1)
                        mm.then_inc(v_done, 1)

                rounds(pe, NC_ // 2, chunk)

            @block.vector
            def _(dve):
                dve.memset(eps[:], EPS).then_inc(eps_done, 1)
                dve.memset(relz[:], 0.0).then_inc(rel_done, 1)

                def norm(k, c):
                    dve.wait_ge(x_in[k], 16 * (c // 2) + 16 if isinstance(c, int) else (c - k) * 8 + 16)
                    sem_wait(dve, turned, c - 1)
                    for t in range(4):
                        dve.bn_stats(stats[:, k, t], x[:, k, t]).then_inc(stats_done, 1)
                    wait_apart(dve, stats_done, 4 * c + 4, tick_v)
                    for t in range(4):
                        dve.bn_aggr(mv[:, k, t], stats[:, k, t]).then_inc(mv_done, 1)
                    dve.wait_ge(sd_done, c + 1)
                    dve.reciprocal(rs[:, k], sd[:, k]).then_inc(rs_done, 1)
                    dve.wait_ge(rs_done, c + 1)
                    for t in range(4):
                        dve.tensor_scalar(xn[:, k, t], x[:, k, t], mv[:, k, t, 0:1], rs[:, k, t:t + 1],
                                          ALU.subtract, ALU.mult).then_inc(xn_done, 1)

                def split(k, i):
                    c = 2 * i + k
                    f, r = full["q"][:, k], rest["q"]
                    h, m, l = (part["q", w][:, k] for w in "hml")
                    dve.wait_ge(qf_done, 2 * c + 2)
                    sem_wait(dve, stored[k], i * (16 * STORES))
                    dve.tensor_copy(h, f).then_inc(q_split, 1)
                    dve.wait_ge(q_split, 4 * c + 1)
                    dve.tensor_tensor(r[:], f, h, ALU.subtract).then_inc(q_split, 1)
                    dve.wait_ge(q_split, 4 * c + 2)
                    dve.tensor_copy(m, r[:]).then_inc(q_split, 1)
                    dve.wait_ge(q_split, 4 * c + 3)
                    dve.tensor_tensor(l, r[:], m, ALU.subtract).then_inc(q_split, 1)
                    dve.wait_ge(v_done, c + 1)
                    for t in range(4):
                        dve.tensor_tensor(v[:, k, :, t, 0:D], pv[:, t].rearrange("p (h d) -> p h d", d=D),
                                          bv[:].rearrange("p (h d) -> p h d", d=D), ALU.add).then_inc(vb_done, 1)
                    dve.wait_ge(q_split, 4 * c + 4)

                dve.wait_ge(rel_in, 16)
                dve.wait_ge(rel_done, 1)
                edge = MAXREL - 1
                dve.tensor_copy(rele[:, edge:edge + NREL], relt[:]).then_inc(rel_done, 1)
                dve.tensor_scalar(rele[:, 0:edge], relz[:, 0:edge], relt[:, 0:1], None, ALU.add).then_inc(rel_done, 1)
                dve.tensor_scalar(rele[:, edge + NREL:EXT + 1], relz[:, 0:EXT + 1 - edge - NREL],
                                  relt[:, NREL - 1:NREL], None, ALU.add).then_inc(rel_done, 1)
                dve.wait_ge(rel_done, 4)
                dve.tensor_copy(relp["h"][:], rele[:]).then_inc(rel_done, 1)
                dve.wait_ge(rel_done, 5)
                dve.tensor_tensor(relr[:], rele[:], relp["h"][:], ALU.subtract).then_inc(rel_done, 1)
                dve.wait_ge(rel_done, 6)
                dve.tensor_copy(relp["m"][:], relr[:]).then_inc(rel_done, 1)
                dve.wait_ge(rel_done, 7)
                dve.tensor_tensor(relp["l"][:], relr[:], relp["m"][:], ALU.subtract).then_inc(rel_done, 1)
                dve.wait_ge(weights_in, 96)
                dve.wait_ge(init_done, 2)

                def chunk(i):
                    for k in range(2):
                        norm(k, 2 * i + k)
                    for k in range(2):
                        split(k, i)

                rounds(dve, NC_ // 2, chunk)


def scratch(nc):
    def dram(name, shape, dt):
        return nc.dram_tensor(name, shape, dt, kind="Internal").ap()

    return {
        "q": dram("q_stack", [H, QR, N], bf16),
        "k": dram("k_stack", [H, QR, N], bf16),
        "v": dram("v_blocks", [H, P, NT, VC], fp32),
        "rel": dram("rel_stack", [PR, EXT + 1], bf16),
        "x1": dram("x_attended", [N, E], fp32),
        "xn": dram("x_normal", [N, E], fp32),
        "xs": dram("x_slots", [SLOTS, E], fp32),
        "y": dram("y_slots", [SLOTS, E], fp32),
    }


def maxima(nc, hbm):
    with ExitStack() as outer:
        terms = outer.enter_context(nc.sbuf_tensor("m_terms", [P, 3, H, B, ST], fp32))
        with ExitStack() as ctx:
            sb = lambda n, s, d=fp32: ctx.enter_context(nc.sbuf_tensor(n, s, d))
            sem = lambda n: ctx.enter_context(nc.semaphore(n))
            rel = sb("m_rel", [PR, EXT + 1], bf16)
            q = sb("m_q", [PR, 2, S], bf16)
            k_ = sb("m_k", [PR, 2, S], bf16)
            CB = 4
            copies = sb("m_copies", [P, CB, 4, 512], bf16)
            top, top_direct = sb("m_top", [P, 2, ST]), sb("m_top_direct", [P, 2, ST])
            top_rel = sb("m_top_rel", [P, 2, ST])
            ps = [ctx.enter_context(nc.psum_tensor(f"m_ps{i}", [P, 4, 512], fp32)) for i in range(2)]
            rel_in, stacks_in = sem("m_rel_in"), [sem(f"m_stacks_in{k}") for k in range(2)]
            to_copy, to_take, copied, taken, maxed, init_done, guard_done = (
                sem(f"m_{n}") for n in ("to_copy", "to_take", "copied", "taken", "maxed", "init_done", "guard_done"))
            steps = [("keys", t) for t in range(ST)] + [("rel", t) for t in range(0, ST, 4)]
            STEPS = len(steps)
            is_keys = lambda p: steps[p % STEPS][0] == "keys"
            copied_from = lambda p: 0 if steps[p % STEPS][1] % 4 == 3 else 1
            direct = lambda p: is_keys(p) and copied_from(p) > 0
            turns_before = lambda p: sum(not is_keys(x) or direct(x) for x in range(p))
            reads_before = lambda p: sum(1 if direct(x) else 0 if is_keys(x) else 2 for x in range(p))
            copies_before = lambda p: sum(is_keys(x) for x in range(p))
            TURNS, READS = turns_before(STEPS), reads_before(STEPS)

            with nc.Block() as block:

                @block.sync
                def _(sp):
                    def load(k, h):
                        for t, n in ((q, "q"), (k_, "k")):
                            sp.dma_start(t[:, k], hbm[n].rearrange("h r t -> r h t")[0:PR, ds(h, 1), k * S:(k + 1) * S]
                                         .rearrange("r h t -> r (h t)")).then_inc(stacks_in[k], 16)

                    sp.dma_start(rel[:], hbm["rel"]).then_inc(rel_in, 16)
                    for k in range(2):
                        load(k, 0)
                    with sp.Fori(1, H) as h:
                        for k in range(2):
                            sp.wait_ge(to_take, (2 * h - 1 + k) * TURNS)
                            load(k, h)

                @block.tensor
                def _(pe):
                    pe.wait_ge(rel_in, 16)

                    def head(h):
                        for k in range(2):
                            n = 2 * h + k
                            pe.wait_ge(stacks_in[k], 32 * h + 32)
                            for p, (kind, t) in enumerate(steps):
                                half = ps[p % 2]
                                product = lambda j: pe.matmul(half[:, j], q[:, k, t * P:(t + 1) * P], k_[:, k, j * 512:(j + 1) * 512],
                                                              start=True, stop=True)

                                def wait_copied():
                                    sem_wait(pe, copied, (n - 1) * ST + copies_before(p + STEPS - 1) if p < 2 else n * ST + copies_before(p - 1))

                                def wait_taken():
                                    sem_wait(pe, taken, (n - 1) * READS + reads_before(p + STEPS - 1) if p < 2 else n * READS + reads_before(p - 1))

                                late = direct(p) and direct(p - 2)
                                if is_keys(p - 2):
                                    wait_copied()
                                if not late and (direct(p - 2) or not is_keys(p - 2)):
                                    wait_taken()
                                if kind == "keys":
                                    for j in range(copied_from(p), 4):
                                        mm = product(j)
                                    mm.then_inc(to_copy, 1)
                                    if late:
                                        wait_taken()
                                    if direct(p):
                                        product(0).then_inc(to_take, 1)
                                else:
                                    for j in range(4):
                                        mm = pe.matmul(half[:, j, 0:NREL], q[:, k, (t + j) * P:(t + j + 1) * P],
                                                       rel[:, MAXREL - 1:MAXREL - 1 + NREL], start=True, stop=True)
                                    mm.then_inc(to_take, 1)

                    rounds(pe, H, head)

                @block.scalar
                def _(act):
                    def head(h):
                        for k in range(2):
                            for p, (kind, t) in enumerate(steps):
                                if kind == "keys":
                                    n = ST * (2 * h + k) + t
                                    act.wait_ge(to_copy, n + 1)
                                    sem_wait(act, maxed, n + 1 - CB)
                                    f = copied_from(p)
                                    act.activation(copies[:, t % CB, f:4], ps[p % 2][:, f:4], ACT.Copy).then_inc(copied, 1)

                    rounds(act, H, head)

                @block.vector
                def _(dve):
                    dve.memset(top_direct[:], -3.0e38).then_inc(init_done, 1)
                    dve.wait_ge(init_done, 1)

                    def head(h):
                        for k in range(2):
                            n = 2 * h + k

                            def max_of_copy(p):
                                t = steps[p][1]
                                dve.wait_ge(copied, n * ST + t + 1)
                                c = copies[:, t % CB, copied_from(p):4].rearrange("p j c -> p (j c)")
                                dve.tensor_scalar(c, c, -3.0e38, None, ALU.max, ALU.max, accum_out=top[:, k, t:t + 1]).then_inc(maxed, 1)

                            sem_wait(dve, guard_done, 2 * (n - 1))
                            for p, (kind, t) in enumerate(steps):
                                if kind == "rel" or direct(p):
                                    dve.wait_ge(to_take, n * TURNS + turns_before(p + 1))
                                if kind == "rel":
                                    half = ps[p % 2]
                                    dve.tensor_reduce(top_rel[:, k, t:t + 4], half[:, :, 0:NREL], AX.X, ALU.max).then_inc(taken, 1)
                                    dve.tensor_copy(terms[:, 0:3:2, ds(h, 1), k, t:t + 4].rearrange("p a h t -> p (a h) t"),
                                                    half[:, :, 0:NREL:NREL - 1].rearrange("p t a -> p a t")).then_inc(taken, 1)
                                elif direct(p):
                                    dve.tensor_reduce(top_direct[:, k, t:t + 1], ps[p % 2][:, 0], AX.X, ALU.max).then_inc(taken, 1)
                                if p and is_keys(p - 1):
                                    max_of_copy(p - 1)
                            dve.wait_ge(taken, n * READS + READS)
                            dve.wait_ge(maxed, n * ST + ST)
                            dve.tensor_tensor(top[:, k], top[:, k], top_direct[:, k], ALU.max).then_inc(guard_done, 1)
                            dve.wait_ge(guard_done, 2 * n + 1)
                            dve.scalar_tensor_tensor(out=terms[:, 1, ds(h, 1), k, :].rearrange("p h t -> p (h t)"), in0=top[:, k],
                                                     scalar=-1.0, in1=top_rel[:, k], op0=ALU.mult, op1=ALU.subtract)\
                               .then_inc(guard_done, 1)

                    rounds(dve, H, head)
                    dve.wait_ge(guard_done, 2 * BH)

        with ExitStack() as ctx:
            sb = lambda n, s, d=fp32: ctx.enter_context(nc.sbuf_tensor(n, s, d))
            sem = lambda n: ctx.enter_context(nc.semaphore(n))
            CC = BH * ST // P
            ident = sb("t_ident", [P, P])
            rest = sb("t_rest", [P, 3, CC, P])
            part = {w: sb(f"t_{w}", [P, 3, CC, P], bf16) for w in "hml"}
            ps = ctx.enter_context(nc.psum_tensor("t_ps", [P, 3, CC, P], fp32))
            ident_done, turned, split, stored = (sem(f"t_{n}") for n in ("ident_done", "turned", "split_d", "stored"))
            with nc.Block() as block:
                @block.gpsimd
                def _(pool):
                    pool.memset(ident[:], 0.0).then_inc(ident_done, 1)
                    pool.wait_ge(ident_done, 1)
                    pool.affine_select(out=ident[:], in_=ident[:], compare_op=ALU.not_equal, fill=1.0, base=0,
                                       pattern=[[-1, P]], channel_multiplier=1).then_inc(ident_done, 1)

                @block.tensor
                def _(pe):
                    pe.wait_ge(ident_done, 2)
                    flat = terms[:].rearrange("p a h b t -> p a (h b t)")
                    for a in range(3):
                        for c in range(CC):
                            mm = pe.transpose(ps[:, a, c], flat[:, a, c * P:(c + 1) * P], ident[:])
                    mm.then_inc(turned, 1)

                @block.vector
                def _(dve):
                    dve.wait_ge(turned, 1)
                    dve.tensor_copy(part["h"][:], ps[:]).then_inc(split, 1)
                    dve.wait_ge(split, 1)
                    dve.tensor_tensor(rest[:], ps[:], part["h"][:], ALU.subtract).then_inc(split, 1)
                    dve.wait_ge(split, 2)
                    dve.tensor_copy(part["m"][:], rest[:]).then_inc(split, 1)
                    dve.wait_ge(split, 3)
                    dve.tensor_tensor(part["l"][:], rest[:], part["m"][:], ALU.subtract).then_inc(split, 1)

                @block.sync
                def _(sp):
                    sp.wait_ge(split, 4)
                    hp = H // CC
                    n = 0
                    for a, row, parts in ((0, R_LEFT, "hml"), (1, R_MAX, "hm"), (2, R_RIGHT, "hml")):
                        for j, w in enumerate(parts):
                            for c in range(CC):
                                to = hbm["q"][c * hp:(c + 1) * hp, row + j, :].rearrange("h (t x) -> h t x", x=P)
                                sp.dma_start(to, part[w][:, a, c]).then_inc(stored, 16)
                                n += 1
                    sp.wait_ge(stored, 16 * n)


def near(nc, hbm, ctxn):
    with ExitStack() as ctx:
        sb = lambda n, s, d=fp32: ctx.enter_context(nc.sbuf_tensor(n, s, d))
        sem = lambda n: ctx.enter_context(nc.semaphore(n))
        ident = sb("n_ident", [P, P])
        rel = sb("n_rel", [PR, EXT + 1], bf16)
        kw = [sb(f"n_k{i}", [QR, H, B, 3 * P], bf16) for i in range(2)]
        qw = [sb(f"n_q{i}", [QR, H, B, P], bf16) for i in range(2)]
        vw = [sb(f"n_v{i}", [P, H, B, 3, VC]) for i in range(2)]
        HALF = P // 2
        HB, QB = BH // 2, HALF // 2
        pb = [sb(f"n_p{i}", [P, 2, 2, 2, HB, QB]) for i in range(2)]
        G = BH // 4
        os = sb("n_os", [P, G, P])
        sc = ctx.enter_context(nc.psum_tensor("n_sc", [P, 2, 2, HB, QB], fp32))
        o = ctx.enter_context(nc.psum_tensor("n_o", [P, G, P], fp32))
        ot = ctx.enter_context(nc.psum_tensor("n_ot", [P, G, P], fp32))
        ident_done, rel_in = sem("n_ident_done"), sem("n_rel_in")
        tile_in = [sem(f"n_tile_in{i}") for i in range(2)]
        scored, exps, summed, os_done, turned, ctx_done = (sem(f"n_{n}") for n in ("scored", "exps", "summed", "os_d", "turned", "ctx_d"))
        DMAS = 6
        SLOTS_OF = lambda edge: (1, 2) if edge == 0 else (0, 1) if edge == 1 else (0, 1, 2)
        first_step = lambda I: 0 if isinstance(I, int) and I == 0 else 3 * I - 1
        first_pb = lambda buf, edge: 1 if edge is None and buf == 0 else 0

        def tiles(eng, body):
            body(0, 0, 0)
            with eng.Fori(0, ST // 2 - 1) as i:
                for j in range(2):
                    body(2 * i + 1 + j, (1 + j) % 2, None)
            body(ST - 1, 1, 1)

        with nc.Block() as block:

            @block.sync
            def _(sp):
                def load(I, buf, edge):
                    lo = 1 if edge == 0 else 0
                    w = 2 if edge in (0, 1) else 3
                    t0 = I - 1 + lo
                    for b in range(B):
                        sp.dma_start(kw[buf][:, :, b, lo * P:(lo + w) * P],
                                     hbm["k"].rearrange("h r t -> r h t")[:, :, ds(t0 * P + b * S, w * P)]).then_inc(tile_in[buf], 16)
                        sp.dma_start(qw[buf][:, :, b],
                                     hbm["q"].rearrange("h r t -> r h t")[:, :, ds(I * P + b * S, P)]).then_inc(tile_in[buf], 16)
                        sp.dma_start(vw[buf][:, :, b, lo:lo + w],
                                     hbm["v"].rearrange("h p t c -> p h t c")[:, :, ds(t0 + b * ST, w)]).then_inc(tile_in[buf], 16)

                sp.dma_start(rel[:], hbm["rel"]).then_inc(rel_in, 16)
                load(0, 0, 0)
                load(1, 1, None)

                def next_load(I, buf, edge):
                    sp.wait_ge(summed, first_step(I - 1))
                    load(I, buf, edge)

                with sp.Fori(0, ST // 2 - 2) as i:
                    for j in range(2):
                        next_load(2 * i + 2 + j, j, None)
                next_load(ST - 2, 0, None)
                next_load(ST - 1, 1, 1)

            @block.gpsimd
            def _(pool):
                pool.memset(ident[:], 0.0).then_inc(ident_done, 1)
                pool.wait_ge(ident_done, 1)
                pool.affine_select(out=ident[:], in_=ident[:], compare_op=ALU.not_equal, fill=1.0, base=0,
                                   pattern=[[-1, P]], channel_multiplier=1).then_inc(ident_done, 1)

            @block.tensor
            def _(pe):
                pe.wait_ge(ident_done, 2)
                pe.wait_ge(rel_in, 16)

                def scores(buf, s, slot, u):
                    kb, qb = kw[buf], qw[buf]
                    for half in range(2):
                        sem_wait(pe, exps, 2 * u - 1 + half)
                        hs = slice(half * H // 2, (half + 1) * H // 2)
                        for x in range(HB):
                            h, b = (half * HB + x) // B, x % B
                            for y in range(2):
                                i0 = s * HALF + y * QB
                                pe.matmul(sc[:, half, y, x], kb[:, h, b, slot * P:(slot + 1) * P], qb[:, h, b, i0:i0 + QB],
                                          start=x == 0, stop=False, skip_group_check=True)
                        for i in range(HALF):
                            col = (slot - 1) * P - (s * HALF + i) + 2 * MAXREL - 1
                            mm = pe.matmul(sc[:, half, i // QB, :, i % QB], rel[:, col:col + P],
                                           qb[0:PR, hs, :, s * HALF + i].rearrange("r h b -> r (h b)"),
                                           start=False, stop=True, skip_group_check=True)
                        mm.then_inc(scored, 1)

                def products(I, buf, slot, n, which, step):
                    pe.wait_ge(exps, 4 * step + 4)
                    if n == 0:
                        sem_wait(pe, os_done, I)
                    for g in range(G):
                        for x in range(4):
                            bh = 4 * g + x
                            mm = pe.matmul(o[32 * x:32 * x + 32, g], vw[buf][:, bh // B, bh % B, slot],
                                           pb[which][:, bh // HB, :, :, bh % HB, :].rearrange("p s y q -> p (s y) q"),
                                           start=(n == 0 and g % 4 == 0), stop=True, skip_group_check=True)
                    mm.then_inc(summed, 1)

                def turn(I):
                    sem_wait(pe, os_done, I + 1)
                    sem_wait(pe, ctx_done, I)
                    for g in range(G):
                        mm = pe.transpose(ot[:, g], os[:, g], ident[:])
                    mm.then_inc(turned, 1)

                def tile(I, buf, edge):
                    pe.wait_ge(tile_in[buf], 16 * DMAS if isinstance(I, int) and I < 2 else (I - buf) * (8 * DMAS) + 16 * DMAS)
                    slots, step, p0 = SLOTS_OF(edge), first_step(I), first_pb(buf, edge)
                    for n, slot in enumerate(slots):
                        scores(buf, 0, slot, 2 * (step + n))
                        if n:
                            products(I, buf, slots[n - 1], n - 1, (p0 + n - 1) % 2, step + n - 1)
                        elif edge != 0:
                            products(I - 1, 1 - buf, 2, 2, (p0 + 1) % 2, step - 1)
                        if n == 1 and edge != 0:
                            turn(I - 1)
                        scores(buf, 1, slot, 2 * (step + n) + 1)

                tiles(pe, tile)

                products(ST - 1, 1, SLOTS_OF(1)[-1], 1, (first_pb(1, 1) + 1) % 2, first_step(ST - 1) + 1)
                turn(ST - 1)

            @block.scalar
            def _(act):
                def tile(I, buf, edge):
                    p0 = first_pb(buf, edge)
                    for n in range(len(SLOTS_OF(edge))):
                        step = first_step(I) + n
                        sem_wait(act, summed, step - 1)
                        for s in range(2):
                            for half in range(2):
                                act.wait_ge(scored, 4 * step + 2 * s + half + 1)
                                act.activation(pb[(p0 + n) % 2][:, half, s], sc[:, half], ACT.Exp).then_inc(exps, 1)

                tiles(act, tile)

            @block.vector
            def _(dve):
                def tile(I, buf, edge):
                    dve.wait_ge(summed, first_step(I) + len(SLOTS_OF(edge)))
                    sem_wait(dve, turned, I)
                    dve.tensor_copy(os[:], o[:]).then_inc(os_done, 1)
                    dve.wait_ge(turned, I + 1)
                    dve.tensor_copy(ctxn[:, :, :, ds(I, 1), :].rearrange("p h b t c -> p (h b t) c"),
                                    ot[:].rearrange("p g (x c) -> p (g x) c", c=VC)[:, :, 0:D + 1]).then_inc(ctx_done, 1)

                tiles(dve, tile)
                dve.wait_ge(ctx_done, ST)


def far(nc, hbm, ctxn):
    with ExitStack() as ctx:
        sb = lambda n, s, d=fp32: ctx.enter_context(nc.sbuf_tensor(n, s, d))
        sem = lambda n: ctx.enter_context(nc.semaphore(n))
        UT = 12
        pairs = [(j, i) for j in range(ST) for i in range(ST) if abs(i - j) > 1]
        units = [pairs[n:n + UT] for n in range(0, len(pairs), UT)]
        NU = len(units)
        assert NU % 6 == 0

        def runs(unit, size):
            out = []
            for n, (j, i) in enumerate(unit):
                if out:
                    pj, pi, w, at = out[-1]
                    if pj == j and pi + w == i and (i < j) == (pi < j) and not size(n, i):
                        out[-1] = (pj, pi, w + 1, at)
                        continue
                out.append((j, i, 1, n))
            return out

        bank = lambda n, i: n % 4 == 0
        quad = lambda n, i: i % 4 == 0

        ident = sb("f_ident", [P, P])
        q = sb("f_q", [QR, B, S], bf16)
        kl = sb("f_kl", [QR, B, S], bf16)
        kr = sb("f_kr", [QR, B, S], bf16)
        v = sb("f_v", [P, B, ST, VC])
        pb = [sb(f"f_p{i}", [P, UT * P]) for i in range(3)]
        os = sb("f_os", [P, 4, P])
        sc = [ctx.enter_context(nc.psum_tensor(f"f_sc{i}", [P, UT * P], fp32)) for i in range(2)]
        o = ctx.enter_context(nc.psum_tensor("f_o", [P, 4, P], fp32))
        ot = ctx.enter_context(nc.psum_tensor("f_ot", [P, 4, P], fp32))
        ident_done, ones_done = sem("f_ident_done"), sem("f_ones_done")
        stacks_in = [sem(f"f_in{k}") for k in range(B)]
        scored, exps, summed, os_done, turned, ctx_done = (sem(f"f_{n}") for n in ("scored", "exps", "summed", "os_d", "turned", "ctx_d"))
        DMAS = 4

        with nc.Block() as block:

            @block.sync
            def _(sp):
                def load(k, h):
                    flat = lambda ap: ap.rearrange("r h t -> r (h t)")
                    at = lambda n, rows: flat(hbm[n].rearrange("h r t -> r h t")[0:rows, ds(h, 1), k * S:(k + 1) * S])
                    sp.dma_start(q[:, k], at("q", QR)).then_inc(stacks_in[k], 16)
                    sp.dma_start(kl[0:PR, k], at("k", PR)).then_inc(stacks_in[k], 16)
                    sp.dma_start(kr[0:PR, k], at("k", PR)).then_inc(stacks_in[k], 16)
                    sp.dma_start(v[:, k], hbm["v"].rearrange("h p t c -> p h t c")[:, ds(h, 1), k * ST:(k + 1) * ST]
                                 .rearrange("p h t c -> p (h t) c")).then_inc(stacks_in[k], 16)

                for k in range(B):
                    load(k, 0)
                with sp.Fori(1, H) as h:
                    for k in range(B):
                        sp.wait_ge(summed, (2 * h + k - 1) * NU)
                        load(k, h)

            @block.gpsimd
            def _(pool):
                pool.memset(ident[:], 0.0).then_inc(ident_done, 1)
                pool.wait_ge(ident_done, 1)
                pool.affine_select(out=ident[:], in_=ident[:], compare_op=ALU.not_equal, fill=1.0, base=0,
                                   pattern=[[-1, P]], channel_multiplier=1).then_inc(ident_done, 1)

            @block.tensor
            def _(pe):
                pe.wait_ge(ident_done, 2)
                pe.wait_ge(ones_done, 4)

                def scores(k, n, u):
                    sem_wait(pe, exps, u - 1)
                    for j, i, w, at in runs(units[n], bank):
                        side = kl if j < i else kr
                        mm = pe.matmul(sc[n % 2][:, at * P:(at + w) * P], side[:, k, j * P:(j + 1) * P], q[:, k, i * P:(i + w) * P],
                                       start=True, stop=True)
                    mm.then_inc(scored, 1)

                def products(k, n, u):
                    pe.wait_ge(exps, u + 1)
                    for j, i, w, at in runs(units[n], quad):
                        g, c = i // 4, i % 4
                        first = not any(x // 4 == g for un in units[:n] for _, x in un) and \
                            not any(x // 4 == g for _, x in units[n][:at])
                        mm = pe.matmul(o[32 * g:32 * g + 32, c:c + w], v[:, k, j], pb[n % 3][:, at * P:(at + w) * P],
                                       start=first, stop=True, skip_group_check=True)
                    mm.then_inc(summed, 1)

                def turn(pair):
                    pe.wait_ge(os_done, pair + 1)
                    sem_wait(pe, ctx_done, pair)
                    for c in range(4):
                        mm = pe.transpose(ot[:, c], os[:, c], ident[:])
                    mm.then_inc(turned, 1)

                def head(h):
                    for k in range(B):
                        pair = B * h + k
                        u = pair * NU
                        pe.wait_ge(stacks_in[k], 16 * DMAS * h + 16 * DMAS)
                        for n in range(NU):
                            scores(k, n, u + n)
                            if n < 2:
                                if not (isinstance(pair, int) and pair == 0):
                                    products((k - 1) % B, NU - 2 + n, u - 2 + n)
                            else:
                                if n == 2:
                                    sem_wait(pe, os_done, pair)
                                products(k, n - 2, u + n - 2)
                            if n == 3 and not (isinstance(pair, int) and pair == 0):
                                turn(pair - 1)

                rounds(pe, H, head)
                for n in (NU - 2, NU - 1):
                    products(B - 1, n, (BH - 1) * NU + n)
                turn(BH - 1)

            @block.scalar
            def _(act):
                def head(h):
                    for k in range(B):
                        for n in range(NU):
                            u = (B * h + k) * NU + n
                            w = len(units[n]) * P
                            act.wait_ge(scored, u + 1)
                            sem_wait(act, summed, u - 2)
                            act.activation(pb[n % 3][:, 0:w], sc[n % 2][:, 0:w], ACT.Exp).then_inc(exps, 1)

                rounds(act, H, head)

            @block.vector
            def _(dve):
                dve.memset(kl[PR:QR], 0.0).then_inc(ones_done, 1)
                dve.memset(kr[PR:QR], 1.0).then_inc(ones_done, 1)
                dve.wait_ge(ones_done, 2)
                dve.memset(kl[PR:R_RIGHT], 1.0).then_inc(ones_done, 1)
                dve.memset(kr[PR:R_MAX], 0.0).then_inc(ones_done, 1)

                def head(h):
                    for k in range(B):
                        pair = B * h + k
                        dve.wait_ge(summed, pair * NU + NU)
                        sem_wait(dve, turned, pair)
                        dve.tensor_copy(os[:], o[:]).then_inc(os_done, 1)
                        dve.wait_ge(turned, pair + 1)
                        c = ctxn[:, ds(h, 1), k].rearrange("p h (g c) x -> p (h g) c x", c=4)
                        dve.tensor_tensor(c, ot[:].rearrange("p c (g x) -> p g c x", g=4)[:, :, :, 0:D + 1], c, ALU.add)\
                           .then_inc(ctx_done, 1)

                rounds(dve, H, head)
                dve.wait_ge(ctx_done, BH)


WS = 64.0


def make_ident(pool, ident, done):
    pool.memset(ident[:], 0.0).then_inc(done, 1)
    pool.wait_ge(done, 1)
    pool.affine_select(out=ident[:], in_=ident[:], compare_op=ALU.not_equal, fill=1.0, base=0,
                       pattern=[[-1, P]], channel_multiplier=1).then_inc(done, 1)


def combine(nc, io, hbm, ctxn, w1, w2, logits):
    with ExitStack() as ctx:
        sb = lambda n, s, d=fp32: ctx.enter_context(nc.sbuf_tensor(n, s, d))
        sem = lambda n: ctx.enter_context(nc.semaphore(n))
        ident = sb("c_ident", [P, P])
        wo, wr = sb("c_wo", [P, 2, E]), sb("c_wr", [P, 2, NE])
        bo, br, eps = sb("c_bo", [P, E]), sb("c_br", [P, NE]), sb("c_eps", [P, 1])
        raw = [sb(f"c_raw{i}", [P, 2 * FI]) for i in range(2)]
        x = sb("c_x", [P, B, E])
        xb = sb("c_xb", [P, B, E])
        rden = sb("c_rden", [P, B, H])
        c = sb("c_c", [P, B, E])
        ct = sb("c_ct", [P, B, 2, P])
        x1 = sb("c_x1", [P, B, E])
        stats, mv, sd, rs = sb("c_stats", [P, B, 6]), sb("c_mv", [P, B, 2]), sb("c_sd", [P, B]), sb("c_rs", [P, B])
        xn = sb("c_xn", [P, B, E])
        xnt = sb("c_xnt", [P, B, 2, P])
        ps = lambda n, s: ctx.enter_context(nc.psum_tensor(n, s, fp32))
        pc = [ps(f"c_pc{b}", [P, 2, P]) for b in range(B)]
        po = [ps(f"c_po{b}", [P, E]) for b in range(B)]
        pn = [ps(f"c_pn{b}", [P, 2, P]) for b in range(B)]
        pl = [ps(f"c_pl{b}", [P, NE]) for b in range(B)]
        ident_done, consts_in, eps_done = sem("c_ident_done"), sem("c_consts_in"), sem("c_eps_done")
        raw_in, hi_done, lo_done = [sem(f"c_raw_in{i}") for i in range(2)], sem("c_hi_done"), sem("c_lo_done")
        x_in, stored = [sem(f"c_x_in{b}") for b in range(B)], [sem(f"c_stored{b}") for b in range(B)]
        names = ("xb", "rden", "c", "ctp", "ct", "o", "x1", "stats", "mv", "sd", "rs", "xn", "xnp", "xnt", "lp", "l", "tick")
        done = {n: sem(f"c_{n}_done") for n in names}
        x_h = io["L0_attn_q"].rearrange("b (t p) e -> p b t e", p=P)

        with nc.Block() as block:

            @block.sync
            def _(sp):
                sp.dma_start(wo[:], io["L0_attn_Wo"].rearrange("(c p) n -> p c n", p=P)).then_inc(consts_in, 16)
                sp.dma_start(wr[:], io["L0_ffn_wr"].rearrange("(c p) n -> p c n", p=P)).then_inc(consts_in, 16)
                sp.dma_start(bo[:], io["L0_attn_bo"].rearrange("(a n) -> a n", a=1).to_broadcast([P, E])).then_inc(consts_in, 16)
                sp.dma_start(br[:], io["L0_ffn_br"].rearrange("(a n) -> a n", a=1).to_broadcast([P, NE])).then_inc(consts_in, 16)

                def tile(i):
                    for b in range(B):
                        sem_wait(sp, done["xb"], B * i - 1 + b if not isinstance(i, int) else 0)
                        sp.dma_start(x[:, b], x_h[:, b, ds(i, 1)].rearrange("p t e -> p (t e)")).then_inc(x_in[b], 16)
                    for b in range(B):
                        sp.wait_ge(done["x1"], B * i + b + 1)
                        sp.dma_start(hbm["x1"].rearrange("(b t p) e -> p b t e", p=P, b=B)[:, b, ds(i, 1)].rearrange("p t e -> p (t e)"),
                                     x1[:, b]).then_inc(stored[b], 16)
                        sp.wait_ge(done["xn"], B * i + b + 1)
                        sp.dma_start(hbm["xn"].rearrange("(b t p) e -> p b t e", p=P, b=B)[:, b, ds(i, 1)].rearrange("p t e -> p (t e)"),
                                     xn[:, b]).then_inc(stored[b], 16)

                rounds(sp, ST, tile)
                for b in range(B):
                    sp.wait_ge(stored[b], 32 * ST)

            @block.gpsimd
            def _(pool):
                make_ident(pool, ident, ident_done)
                pool.wait_ge(ident_done, 2)

                pool.wait_ge(consts_in, 64)

                def tile(i):
                    for b in range(B):
                        pool.wait_ge(x_in[b], 16 * i + 16)
                        sem_wait(pool, done["x1"], B * i + b - 1 if not isinstance(i, int) else 0)
                        pool.tensor_tensor(xb[:, b], x[:, b], bo[:], ALU.add).then_inc(done["xb"], 1)

                rounds(pool, ST, tile)

            @block.scalar
            def _(act):
                act.wait_ge(eps_done, 1)

                def load(e, k):
                    act.dma_start(raw[0][:].rearrange("p (c n) -> p c n", c=2) if k == 0 else raw[1][:].rearrange("p (c n) -> p c n", c=8),
                                  io["L0_ffn_w1" if k == 0 else "L0_ffn_w2"][ds(e, 1)].rearrange("a (c p) n -> p (a c) n", p=P))\
                       .then_inc(raw_in[k], 16)

                for k in range(2):
                    load(0, k)

                def tile(i):
                    for b in range(B):
                        act.wait_ge(done["ctp"], B * i + b + 1)
                        act.activation(ct[:, b], pc[b][:], ACT.Copy).then_inc(done["ct"], 1)
                    for b in range(B):
                        act.wait_ge(done["mv"], B * i + b + 1)
                        act.activation(sd[:, b:b + 1], mv[:, b, 1:2], ACT.Sqrt, bias=eps[:]).then_inc(done["sd"], 1)
                    for b in range(B):
                        act.wait_ge(done["xnp"], B * i + b + 1)
                        act.activation(xnt[:, b], pn[b][:], ACT.Copy).then_inc(done["xnt"], 1)

                def weights(e, k):
                    act.wait_ge(raw_in[k], 16 * e + 16)
                    w = (w1, w2)[k][0]
                    act.activation(w[:, ds(e, 1)].rearrange("p a n -> p (a n)"), raw[k][:], ACT.Copy, scale=WS).then_inc(hi_done, 1)

                def pair(e):
                    tile(2 * e)
                    weights(e, 0)
                    tile(2 * e + 1)
                    weights(e, 1)

                pair(0)
                with act.Fori(1, NE) as e:
                    for k in range(2):
                        act.wait_ge(lo_done, 2 * e - 1 + k)
                        load(e, k)
                    pair(e)

            @block.tensor
            def _(pe):
                pe.wait_ge(ident_done, 2)
                pe.wait_ge(consts_in, 64)

                def tile(i):
                    for b in range(B):
                        pe.wait_ge(done["c"], B * i + b + 1)
                        for e in range(2):
                            mm = pe.transpose(pc[b][:, e], c[:, b, e * P:(e + 1) * P], ident[:])
                        mm.then_inc(done["ctp"], 1)
                    for b in range(B):
                        pe.wait_ge(done["ct"], B * i + b + 1)
                        for e in range(2):
                            mm = pe.matmul(po[b][:], ct[:, b, e], wo[:, e], start=e == 0, stop=e == 1)
                        mm.then_inc(done["o"], 1)
                    for b in range(B):
                        pe.wait_ge(done["xn"], B * i + b + 1)
                        for e in range(2):
                            mm = pe.transpose(pn[b][:, e], xn[:, b, e * P:(e + 1) * P], ident[:])
                        mm.then_inc(done["xnp"], 1)
                    for b in range(B):
                        pe.wait_ge(done["xnt"], B * i + b + 1)
                        for e in range(2):
                            mm = pe.matmul(pl[b][:], xnt[:, b, e], wr[:, e], start=e == 0, stop=e == 1)
                        mm.then_inc(done["lp"], 1)

                rounds(pe, ST, tile)

            @block.vector
            def _(dve):
                dve.memset(eps[:], EPS).then_inc(eps_done, 1)
                dve.wait_ge(consts_in, 64)

                def tile(i):
                    n = lambda b: B * i + b + 1
                    for b in range(B):
                        sem_wait(dve, done["ctp"], n(b) - B)
                        dve.reciprocal(rden[:, b], ctxn[:, :, b, ds(i, 1), D].rearrange("p h t -> p (h t)")).then_inc(done["rden"], 1)
                    for b in range(B):
                        dve.wait_ge(done["rden"], n(b))
                        dve.tensor_tensor(c[:, b].rearrange("p (h d) -> p h d", d=D),
                                          ctxn[:, :, b, ds(i, 1), 0:D].rearrange("p h t d -> p (h t) d"),
                                          rden[:, b].rearrange("p (h a) -> p h a", a=1).to_broadcast([P, H, D]), ALU.mult)\
                           .then_inc(done["c"], 1)
                    for b in range(B):
                        dve.wait_ge(done["o"], n(b))
                        sem_wait(dve, stored[b], 32 * i)
                        dve.wait_ge(done["xb"], n(b))
                        dve.tensor_tensor(x1[:, b], po[b][:], xb[:, b], ALU.add).then_inc(done["x1"], 1)
                    for b in range(B):
                        dve.wait_ge(done["x1"], n(b))
                        dve.bn_stats(stats[:, b], x1[:, b]).then_inc(done["stats"], 1)
                    for b in range(B):
                        wait_apart(dve, done["stats"], n(b), done["tick"])
                        dve.bn_aggr(mv[:, b], stats[:, b]).then_inc(done["mv"], 1)
                    for b in range(B):
                        dve.wait_ge(done["sd"], n(b))
                        dve.reciprocal(rs[:, b:b + 1], sd[:, b:b + 1]).then_inc(done["rs"], 1)
                    for b in range(B):
                        dve.wait_ge(done["rs"], n(b))
                        dve.tensor_scalar(xn[:, b], x1[:, b], mv[:, b, 0:1], rs[:, b:b + 1], ALU.subtract, ALU.mult)\
                           .then_inc(done["xn"], 1)
                    for b in range(B):
                        dve.wait_ge(done["lp"], n(b))
                        dve.tensor_tensor(logits[:, b, ds(i, 1)].rearrange("p t e -> p (t e)"), pl[b][:], br[:], ALU.add)\
                           .then_inc(done["l"], 1)

                def weights(e, k):
                    hi, lo = (w1, w2)[k]
                    dve.wait_ge(hi_done, 2 * e + k + 1)
                    dve.scalar_tensor_tensor(out=lo[:, ds(e, 1)].rearrange("p a n -> p (a n)"), in0=raw[k][:], scalar=WS,
                                             in1=hi[:, ds(e, 1)].rearrange("p a n -> p (a n)"), op0=ALU.mult, op1=ALU.subtract)\
                       .then_inc(lo_done, 1)

                def pair(e):
                    tile(2 * e)
                    weights(e, 0)
                    tile(2 * e + 1)
                    weights(e, 1)

                rounds(dve, NE, pair)
                dve.wait_ge(done["l"], NT)
                dve.wait_ge(lo_done, 2 * NE)


def route(nc, io, hbm, logits, gate, slot, owner):
    with ExitStack() as ctx:
        sb = lambda n, s, d=fp32: ctx.enter_context(nc.sbuf_tensor(n, s, d))
        sem = lambda n: ctx.enter_context(nc.semaphore(n))
        xn = sb("r_xn", [P, NT, E])
        ones, below = sb("r_ones", [P, P], bf16), sb("r_below", [P, P], bf16)
        e_of, e_less, starts_at = sb("r_e_of", [P, NT, NE]), sb("r_e_less", [P, NT, NE]), sb("r_starts", [P, SLOT_TILES + 1, NE])
        ione = sb("r_ione", [P, NT])
        best, second, gap, ex = (sb(f"r_{n}", [P, NT]) for n in ("best", "second", "gap", "ex"))
        top = sb("r_top", [P, NT])
        a = [sb(f"r_a{i}", [P, NT, NE]) for i in range(4)]
        oh, ohb = sb("r_oh", [P, NT, NE]), sb("r_ohb", [P, NT, NE], bf16)
        tot, inc, base = (sb(f"r_{n}", [P, NE, NT]) for n in ("tot", "inc", "base"))
        cnt, rem, room, end, start = (sb(f"r_{n}", [P, NE]) for n in ("cnt", "rem", "room", "end", "start"))
        cnti, remi = sb("r_cnti", [P, NE], i32), sb("r_remi", [P, NE], i32)
        slotf = sb("r_slotf", [P, NT])
        own, ownf = sb("r_own", [P, SLOT_TILES + 1, NE]), sb("r_ownf", [P, SLOT_TILES + 1])
        pp = ctx.enter_context(nc.psum_tensor("r_pp", [P, NT * NE], fp32))
        pt = ctx.enter_context(nc.psum_tensor("r_pt", [P, NT * NE], fp32))
        consts, ones_done, below_done, oh_done, ranked = (sem(f"r_{n}") for n in ("consts", "ones_done", "below_done", "oh_done", "ranked"))
        step, gap_done, ex_done, slot_done, xn_in, sent = (sem(f"r_{n}") for n in ("step", "gap_done", "ex_done", "slot_done", "xn_in", "sent"))

        with nc.Block() as block:

            @block.sync
            def _(sp):
                sp.dma_start(xn[:], hbm["xn"].rearrange("(t p) e -> p t e", p=P)).then_inc(xn_in, 16)
                sp.wait_ge(xn_in, 16)

            @block.gpsimd
            def _(pool):
                pool.iota(e_of[:], pattern=[[0, NT], [1, NE]], base=0, channel_multiplier=0, allow_small_or_imprecise_dtypes=True).then_inc(consts, 1)
                pool.iota(e_less[:], pattern=[[0, NT], [1, NE]], base=-NE, channel_multiplier=0, allow_small_or_imprecise_dtypes=True).then_inc(consts, 1)
                pool.iota(starts_at[:], pattern=[[P, SLOT_TILES + 1], [0, NE]], base=0, channel_multiplier=0, allow_small_or_imprecise_dtypes=True).then_inc(consts, 1)
                pool.memset(ione[:], 1.0).then_inc(consts, 1)
                pool.memset(ones[:], 1.0).then_inc(ones_done, 1)
                pool.wait_ge(ones_done, 1)
                pool.affine_select(out=below[:], in_=ones[:], compare_op=ALU.is_gt, fill=0.0, base=0,
                                   pattern=[[1, P]], channel_multiplier=-1).then_inc(below_done, 1)
                pool.wait_ge(below_done, 1)
                pool.wait_ge(slot_done, 1)
                pool.wait_ge(xn_in, 16)
                for t in range(NT):
                    pool.indirect_dma_start(out=hbm["xs"], out_offset=bass.IndirectOffsetOnAxis(ap=slot[:, t:t + 1], axis=0),
                                            in_=xn[:, t], in_offset=None, bounds_check=SLOTS - 1, oob_is_err=True).then_inc(sent, 16)
                pool.wait_ge(sent, 16 * NT)

            @block.scalar
            def _(act):
                act.wait_ge(gap_done, 1)
                act.activation(ex[:], gap[:], ACT.Exp).then_inc(ex_done, 1)

            @block.tensor
            def _(pe):
                pe.wait_ge(below_done, 1)
                pe.wait_ge(oh_done, 1)
                flat = ohb[:].rearrange("p t e -> p (t e)")
                pe.matmul(pp[:], below[:], flat, start=True, stop=True).then_inc(ranked, 1)
                pe.matmul(pt[:], ones[:], flat, start=True, stop=True).then_inc(ranked, 1)

            @block.vector
            def _(dve):
                n = [0]

                def then(ins):
                    n[0] += 1
                    ins.then_inc(step, 1)
                    dve.wait_ge(step, n[0])

                wide = lambda ap, m=NE: ap.rearrange("p (t a) -> p t a", a=1).to_broadcast([P, ap.shape[1], m])
                l = logits[:].rearrange("p b t e -> p (b t) e")
                dve.wait_ge(consts, 4)
                then(dve.tensor_reduce(best[:], l, AX.X, ALU.max))
                then(dve.tensor_tensor(a[0][:], l, wide(best[:]), ALU.is_equal))
                then(dve.tensor_tensor(a[1][:], a[0][:], e_less[:], ALU.mult))
                then(dve.tensor_reduce(top[:], a[1][:], AX.X, ALU.min))
                then(dve.tensor_tensor(oh[:], e_less[:], wide(top[:]), ALU.is_equal))
                dve.tensor_copy(ohb[:], oh[:]).then_inc(oh_done, 1)
                then(dve.scalar_tensor_tensor(out=a[2][:], in0=oh[:], scalar=-3.0e38, in1=l, op0=ALU.mult, op1=ALU.add))
                then(dve.tensor_reduce(second[:], a[2][:], AX.X, ALU.max))
                dve.tensor_tensor(gap[:], second[:], best[:], ALU.subtract).then_inc(gap_done, 1)
                dve.wait_ge(ranked, 2)
                then(dve.tensor_copy(tot[:], pt[:].rearrange("p (t e) -> p e t", e=NE)))
                for e in range(NE):
                    ins = dve.tensor_tensor_scan(inc[:, e], ione[:], tot[:, e], 0.0, ALU.mult, ALU.add)
                    n[0] += 1
                    ins.then_inc(step, 1)
                dve.wait_ge(step, n[0])
                then(dve.tensor_scalar(cnt[:], inc[:, :, NT - 1], float(P - 1), None, ALU.add))
                then(dve.tensor_copy(cnti[:], cnt[:]))
                then(dve.tensor_scalar(remi[:], cnti[:], P - 1, None, ALU.bitwise_and))
                then(dve.tensor_copy(rem[:], remi[:]))
                then(dve.tensor_tensor(room[:], cnt[:], rem[:], ALU.subtract))
                then(dve.tensor_tensor_scan(end[:], ione[:, 0:NE], room[:], 0.0, ALU.mult, ALU.add))
                then(dve.tensor_tensor(start[:], end[:], room[:], ALU.subtract))
                then(dve.tensor_tensor(base[:], inc[:], tot[:], ALU.subtract))
                then(dve.tensor_tensor(tot[:], base[:], wide(start[:], NT), ALU.add))
                then(dve.tensor_tensor(a[3][:], pp[:].rearrange("p (t e) -> p t e", e=NE), tot[:].rearrange("p e t -> p t e"), ALU.add))
                then(dve.tensor_tensor(a[0][:], a[3][:], oh[:], ALU.mult))
                then(dve.tensor_reduce(slotf[:], a[0][:], AX.X, ALU.add))
                dve.tensor_copy(slot[:], slotf[:]).then_inc(slot_done, 1)
                then(dve.tensor_tensor(own[:], starts_at[:], end[:].rearrange("p (a e) -> p a e", a=1).to_broadcast([P, SLOT_TILES + 1, NE]), ALU.is_ge))
                then(dve.tensor_reduce(ownf[:], own[:], AX.X, ALU.add))
                then(dve.tensor_scalar(ownf[:], ownf[:], float(NE - 1), None, ALU.min))
                then(dve.tensor_copy(owner[:], ownf[:]))
                dve.wait_ge(ex_done, 1)
                then(dve.tensor_scalar(ex[:], ex[:], 1.0, None, ALU.add))
                then(dve.reciprocal(gate[:], ex[:]))


def experts(nc, io, hbm, w1, w2, owner):
    with ExitStack() as ctx:
        sb = lambda n, s, d=fp32: ctx.enter_context(nc.sbuf_tensor(n, s, d))
        sem = lambda n: ctx.enter_context(nc.semaphore(n))
        (w1h, w1l), (w2h, w2l) = w1, w2
        KC, IC = E // P, FI // P
        HC = IC // 2
        ident = sb("e_ident", [P, P])
        b1r, b1 = sb("e_b1r", [NE * IC, P]), sb("e_b1", [P, NE * IC])
        b2 = sb("e_b2", [P, NE, E])
        xs = sb("e_xs", [P, 2, E])
        xh, xl = sb("e_xh", [P, 2, KC, P], fp16), sb("e_xl", [P, 2, KC, P], fp16)
        g = sb("e_g", [P, 2, IC, P])
        gh, gl = sb("e_gh", [P, 2, IC, P], fp16), sb("e_gl", [P, 2, IC, P], fp16)
        ys = sb("e_ys", [P, 2, E])
        px = [ctx.enter_context(nc.psum_tensor(f"e_px{k}", [P, KC, P], fp32)) for k in range(2)]
        ph = [ctx.enter_context(nc.psum_tensor(f"e_ph{k}", [P, IC, P], fp32)) for k in range(2)]
        py = [ctx.enter_context(nc.psum_tensor(f"e_py{k}", [P, E], fp32)) for k in range(2)]
        ident_done, b_in, b1_done = sem("e_ident_done"), sem("e_b_in"), sem("e_b1_done")
        b1_turned = sem("e_b1_turned")
        x_in, stored = [sem(f"e_x_in{k}") for k in range(2)], [sem(f"e_stored{k}") for k in range(2)]
        xt_done, xh_done, xl_done, h_done, g_done, gh_done, gl_done, y_done, ys_done = (
            sem(f"e_{n}_done") for n in ("xt", "xh", "xl", "h", "g", "gh", "gl", "y", "ys"))
        xs_h = hbm["xs"].rearrange("(t p) e -> p t e", p=P)
        y_h = hbm["y"].rearrange("(t p) e -> p t e", p=P)
        T2 = (SLOT_TILES + 1) // 2

        with nc.Block() as block:

            @block.sync
            def _(sp):
                sp.dma_start(b1r[:], io["L0_ffn_b1"].rearrange("e (c p) -> (e c) p", p=P)).then_inc(b_in, 16)
                sp.dma_start(b2[:], io["L0_ffn_b2"].rearrange("(a e) n -> a e n", a=1).to_broadcast([P, NE, E])).then_inc(b_in, 16)

                def load(t, k):
                    sp.dma_start(xs[:, k], xs_h[:, ds(t, 1)].rearrange("p t e -> p (t e)")).then_inc(x_in[k], 16)

                def store(t, k):
                    sp.wait_ge(ys_done, t + 1)
                    sp.dma_start(y_h[:, ds(t, 1)].rearrange("p t e -> p (t e)"), ys[:, k]).then_inc(stored[k], 16)

                for k in range(2):
                    load(k, k)
                with sp.Fori(0, T2 - 1) as i:
                    for k in range(2):
                        sp.wait_ge(xt_done, 2 * i + k + 1)
                        load(2 * i + k + 2, k)
                    for k in range(2):
                        store(2 * i + k, k)
                for k in range(2):
                    store(2 * T2 - 2 + k, k)
                for k in range(2):
                    sp.wait_ge(stored[k], 16 * T2)

            @block.gpsimd
            def _(pool):
                make_ident(pool, ident, ident_done)

            @block.tensor
            def _(pe):
                pe.wait_ge(ident_done, 2)
                pe.wait_ge(b_in, 32)
                pe.transpose(px[0][:, 0, 0:NE * IC], b1r[:], ident[0:NE * IC, 0:NE * IC]).then_inc(b1_turned, 1)
                pe.wait_ge(b1_done, 1)

                def turn(i, k):
                    t = 2 * i + k
                    pe.wait_ge(x_in[k], 16 * i + 16)
                    sem_wait(pe, xl_done, t - 1)
                    for c in range(KC):
                        mm = pe.transpose(px[k][:, c], xs[:, k, c * P:(c + 1) * P], ident[:])
                    mm.then_inc(xt_done, 1)

                def up(i, k, e):
                    t = 2 * i + k
                    pe.wait_ge(xl_done, t + 1)
                    sem_wait(pe, g_done, IC * (t - 1))
                    for n in range(IC):
                        terms = [(w, x, c) for w, x in ((w1h, xh), (w1h, xl), (w1l, xh)) for c in range(KC)]
                        for m, (w, x, c) in enumerate(terms):
                            mm = pe.matmul(ph[k][:, n], w[:, ds(e, 1), c * FI + n * P:c * FI + (n + 1) * P].rearrange("p a n -> p (a n)"),
                                           x[:, k, c], start=m == 0, stop=m == len(terms) - 1)
                        if n % HC == HC - 1:
                            mm.then_inc(h_done, 1)

                def down(i, k, e):
                    t = 2 * i + k
                    pe.wait_ge(gl_done, t + 1)
                    sem_wait(pe, ys_done, t - 1)
                    terms = [(x, w, n) for n in range(IC) for x, w in ((gh, w2h), (gl, w2h), (gh, w2l))]
                    for m, (x, w, n) in enumerate(terms):
                        mm = pe.matmul(py[k][:], x[:, k, n], w[:, ds(e, 1), n * E:(n + 1) * E].rearrange("p a n -> p (a n)"),
                                       start=m == 0, stop=m == len(terms) - 1)
                    mm.then_inc(y_done, 1)

                def tiles(i):
                    e = [pe.value_load(owner[0:1, ds(2 * i + k, 1)], min_val=0, max_val=NE - 1) for k in range(2)]
                    for k in range(2):
                        turn(i, k)
                    for k in range(2):
                        up(i, k, e[k])
                    for k in range(2):
                        down(i, k, e[k])

                rounds(pe, T2, tiles)

            @block.scalar
            def _(act):
                act.wait_ge(b1_turned, 1)
                act.activation(b1[:], px[0][:, 0, 0:NE * IC], ACT.Copy).then_inc(b1_done, 1)
                act.wait_ge(b1_done, 1)

                def tiles(i):
                    e = [act.value_load(owner[0:1, ds(2 * i + k, 1)], min_val=0, max_val=NE - 1) for k in range(2)]
                    for k in range(2):
                        t = 2 * i + k
                        act.wait_ge(xt_done, t + 1)
                        sem_wait(act, h_done, 2 * (t - 1))
                        act.activation(xh[:, k], px[k][:], ACT.Copy).then_inc(xh_done, 1)
                    for k in range(2):
                        t = 2 * i + k
                        sem_wait(act, gl_done, t - 1)
                        for n in range(IC):
                            if n % HC == 0:
                                act.wait_ge(h_done, 2 * t + n // HC + 1)
                            act.activation(g[:, k, n], ph[k][:, n], ACT.Gelu, bias=b1[:, ds(e[k] * IC + n, 1)], scale=1.0 / WS)\
                               .then_inc(g_done, 1)

                rounds(act, T2, tiles)

            @block.vector
            def _(dve):
                def tiles(i):
                    e = [dve.value_load(owner[0:1, ds(2 * i + k, 1)], min_val=0, max_val=NE - 1) for k in range(2)]
                    for k in range(2):
                        t = 2 * i + k
                        dve.wait_ge(xh_done, t + 1)
                        dve.tensor_tensor(xl[:, k], px[k][:], xh[:, k], ALU.subtract).then_inc(xl_done, 1)
                    for k in range(2):
                        t = 2 * i + k
                        dve.wait_ge(g_done, IC * (t + 1))
                        sem_wait(dve, y_done, t - 1)
                        dve.tensor_copy(gh[:, k], g[:, k]).then_inc(gh_done, 1)
                        dve.wait_ge(gh_done, t + 1)
                        dve.tensor_tensor(gl[:, k], g[:, k], gh[:, k], ALU.subtract).then_inc(gl_done, 1)
                    for k in range(2):
                        t = 2 * i + k
                        dve.wait_ge(y_done, t + 1)
                        sem_wait(dve, stored[k], 16 * i)
                        dve.scalar_tensor_tensor(out=ys[:, k], in0=py[k][:], scalar=1.0 / WS,
                                                 in1=b2[:, ds(e[k], 1)].rearrange("p a n -> p (a n)"), op0=ALU.mult, op1=ALU.add)\
                           .then_inc(ys_done, 1)

                dve.wait_ge(b_in, 32)
                rounds(dve, T2, tiles)


def gather(nc, hbm, out, gate, slot):
    with ExitStack() as ctx:
        sb = lambda n, s, d=fp32: ctx.enter_context(nc.sbuf_tensor(n, s, d))
        sem = lambda n: ctx.enter_context(nc.semaphore(n))
        CH = 8
        y, x1 = sb("g_y", [P, NT, E]), sb("g_x1", [P, NT, E])
        y_in = [sem(f"g_y_in{i}") for i in range(NT // CH)]
        x_in, done, stored = sem("g_x_in"), sem("g_done"), sem("g_stored")
        out_h = out.rearrange("b (t p) e -> p (b t) e", p=P)

        with nc.Block() as block:

            @block.gpsimd
            def _(pool):
                for t in range(NT):
                    pool.indirect_dma_start(out=y[:, t], out_offset=None, in_=hbm["y"],
                                            in_offset=bass.IndirectOffsetOnAxis(ap=slot[:, t:t + 1], axis=0),
                                            bounds_check=SLOTS - 1, oob_is_err=True).then_inc(y_in[t // CH], 16)

            @block.vector
            def _(dve):
                dve.wait_ge(x_in, 16)
                for t in range(NT):
                    dve.wait_ge(y_in[t // CH], 16 * CH)
                    dve.scalar_tensor_tensor(out=x1[:, t], in0=y[:, t], scalar=gate[:, t:t + 1], in1=x1[:, t], op0=ALU.mult, op1=ALU.add)\
                       .then_inc(done, 1)

            @block.sync
            def _(sp):
                sp.dma_start(x1[:], hbm["x1"].rearrange("(t p) e -> p t e", p=P)).then_inc(x_in, 16)
                for c in range(NT // CH):
                    sp.wait_ge(done, CH * (c + 1))
                    sp.dma_start(out_h[:, c * CH:(c + 1) * CH], x1[:, c * CH:(c + 1) * CH]).then_inc(stored, 16)
                sp.wait_ge(stored, 16 * (NT // CH))


def build(nc, io, out):
    hbm = scratch(nc)
    project(nc, io, hbm)
    maxima(nc, hbm)
    with ExitStack() as ctx:
        sb = lambda n, s, d=fp32: ctx.enter_context(nc.sbuf_tensor(n, s, d))
        logits = sb("logits", [P, B, ST, NE])
        gate, slot, owner = sb("gate", [P, NT]), sb("slot", [P, NT], u32), sb("owner", [P, SLOT_TILES + 1], i32)
        with ExitStack() as attention:
            ctxn = attention.enter_context(nc.sbuf_tensor("ctxn", [P, H, B, ST, D + 1], fp32, side="right"))
            near(nc, hbm, ctxn)
            far(nc, hbm, ctxn)
            w1 = [sb(f"w1{n}", [P, NE, 2 * FI], fp16) for n in "hl"]
            w2 = [sb(f"w2{n}", [P, NE, 2 * FI], fp16) for n in "hl"]
            combine(nc, io, hbm, ctxn, w1, w2, logits)
        route(nc, io, hbm, logits, gate, slot, owner)
        experts(nc, io, hbm, w1, w2, owner)
        gather(nc, hbm, out, gate, slot)


def kernel(**inputs):
    import numpy as np
    import concourse.bacc as bacc
    from concourse.bass_utils import run_bass_kernel_spmd

    nc = bacc.Bacc("TRN2", target_bir_lowering=False, num_devices=1)
    arrays, io = {}, {}
    for name, value in inputs.items():
        a = np.ascontiguousarray(value)
        arrays[f"in_{name}"] = a
        io[name] = nc.dram_tensor(f"in_{name}", a.shape, mybir.dt.from_np(a.dtype), kind="ExternalInput").ap()
    out = nc.dram_tensor("out", (B, S, E), fp32, kind="ExternalOutput").ap()
    build(nc, io, out)
    r = run_bass_kernel_spmd(nc, [arrays], core_ids=[0])
    return r.results[0]["out"]
```

```python
import concourse.bass as bass
from concourse import mybir
from contextlib import ExitStack

fp32 = mybir.dt.float32
bf16 = mybir.dt.bfloat16
fp16 = mybir.dt.float16
i32 = mybir.dt.int32
u32 = mybir.dt.uint32
ALU = mybir.AluOpType
ACT = mybir.ActivationFunctionType
AX = mybir.AxisListType
ds = bass.ds

P = 128
B, S, E = 2, 2048, 256
H, D = 16, 16
MAXREL = 128
NREL = 2 * MAXREL + 1
N = B * S
NT = N // P
ST = S // P
BH = B * H
NE, FI = 8, 1024
EPS = 1e-5

Q_PARTS = ("h", "m", "l", "h", "m", "h")
K_PARTS = ("h", "h", "h", "m", "m", "l")
PR = len(Q_PARTS) * D
R_LEFT, R_MAX, R_RIGHT = PR, PR + 3, PR + 5
QR = PR + 8
EXT = S // 4 - 1
VC = 32
EC = 4 * P
NC_ = N // EC

SLOT_TILES = NT + NE - 1
SLOTS = (SLOT_TILES + 1) * P


def sem_wait(eng, sem, value):
    if isinstance(value, int) and value <= 0:
        return
    eng.wait_ge(sem, value)


def wait_apart(eng, sem, value, tick):
    sem_wait(eng, sem, value)
    eng.sem_inc(tick, 1)


def rounds(eng, n, body):
    body(0)
    if n > 1:
        with eng.Fori(1, n) as i:
            body(i)


def project(nc, io, hbm):
    with ExitStack() as ctx:
        sb = lambda n, s, d=fp32: ctx.enter_context(nc.sbuf_tensor(n, s, d))
        sem = lambda n: ctx.enter_context(nc.semaphore(n))
        ident = sb("p_ident", [P, P])
        wq, wk, wv = (sb(f"p_w{n}", [P, 2, E]) for n in "qkv")
        bq, bk, bk4 = sb("p_bq", [P, 2]), sb("p_bk", [P, 2]), sb("p_bk4", [P, 2])
        bv = sb("p_bv", [P, E])
        eps = sb("p_eps", [P, 1])
        x = sb("p_x", [P, 2, 4, E])
        stats = sb("p_stats", [P, 2, 4, 6])
        mv = sb("p_mv", [P, 2, 4, 2])
        sd = sb("p_sd", [P, 2, 4])
        rs = sb("p_rs", [P, 2, 4])
        xn = sb("p_xn", [P, 2, 4, E])
        xt = sb("p_xt", [P, 2, 2, EC])
        full = {n: sb(f"p_{n}f", [P, 2, 2, EC]) for n in "qk"}
        rest = {n: sb(f"p_{n}r", [P, 2, EC]) for n in "qk"}
        part = {(n, w): sb(f"p_{n}{w}", [P, 2, 2, EC], bf16) for n in "qk" for w in "hml"}
        v = sb("p_v", [P, 2, H, 4, VC])
        relt = sb("p_relt", [D, NREL])
        rele = sb("p_rele", [D, EXT + 1])
        relz = sb("p_relz", [D, P])
        relr = sb("p_relr", [D, EXT + 1])
        relp = {w: sb(f"p_rel{w}", [D, EXT + 1], bf16) for w in "hml"}
        flags = sb("p_flags", [H, 2, N], bf16)
        zeros = sb("p_zeros", [P, 8 * E])
        pt = ctx.enter_context(nc.psum_tensor("p_pt", [P, 2, EC], fp32))
        pq = ctx.enter_context(nc.psum_tensor("p_pq", [P, 2, EC], fp32))
        pk = ctx.enter_context(nc.psum_tensor("p_pk", [P, 2, EC], fp32))
        pv = ctx.enter_context(nc.psum_tensor("p_pv", [P, 4, E], fp32))

        weights_in, rel_in = sem("p_weights_in"), sem("p_rel_in")
        x_in = [sem(f"p_x_in{k}") for k in range(2)]
        ident_done, init_done = sem("p_ident_done"), sem("p_init_done")
        tick_v, tick_p = sem("p_tick_v"), sem("p_tick_p")
        flags_done, flags_stored = sem("p_flags_done"), sem("p_flags_stored")
        eps_done, bk4_done = sem("p_eps_done"), sem("p_bk4_done")
        stats_done, mv_done, sd_done, rs_done, xn_done = (sem(f"p_{n}") for n in ("stats_d", "mv_d", "sd_d", "rs_d", "xn_d"))
        turned, xt_done = sem("p_turned"), sem("p_xt_done")
        q_done, k_done, v_done = sem("p_q_done"), sem("p_k_done"), sem("p_v_done")
        qf_done, kf_done = sem("p_qf_done"), sem("p_kf_done")
        q_split, k_split, vb_done = sem("p_q_split"), sem("p_k_split"), sem("p_vb_done")
        stored = [sem(f"p_stored{k}") for k in range(2)]
        rel_done, rel_stored = sem("p_rel_done"), sem("p_rel_stored")

        x_h = io["L0_attn_q"].rearrange("b (c t p) e -> p (b c) t e", p=P, t=4)
        STORES = 2 * 6 * 2 + 1

        with nc.Block() as block:

            @block.sync
            def _(sp):
                def load(k, c):
                    sp.dma_start(x[:, k], x_h[:, ds(c, 1)].rearrange("p c t e -> p (c t) e")).then_inc(x_in[k], 16)

                for k in range(2):
                    load(k, k)
                for w, name in ((wq, "Wq"), (wk, "Wk"), (wv, "Wv")):
                    sp.dma_start(w[:], io[f"L0_attn_{name}"].rearrange("(c p) n -> p c n", p=P)).then_inc(weights_in, 16)
                with nc.allow_non_contiguous_dma(reason="a bias to a column, once"):
                    for b_, name in ((bq, "bq"), (bk, "bk")):
                        sp.dma_start(b_[:], io[f"L0_attn_{name}"].rearrange("(c p) -> p c", p=P)).then_inc(weights_in, 16)
                sp.dma_start(bv[:], io["L0_attn_bv"].rearrange("(a n) -> a n", a=1).to_broadcast([P, E])).then_inc(weights_in, 16)

                def stores(i):
                    for k in range(2):
                        c = 2 * i + k
                        for n, split, rows in (("q", q_split, Q_PARTS), ("k", k_split, K_PARTS)):
                            for w, need in (("h", 1), ("m", 3), ("l", 4)):
                                sp.wait_ge(split, 4 * c + need)
                                for r, which in enumerate(rows):
                                    if which == w:
                                        to = hbm[n].rearrange("(m g) r t -> g r m t", m=2)[:, D * r:D * r + D, :, ds(c * EC, EC)]
                                        for m in range(2):
                                            sp.dma_start(to[:, :, m], part[n, w][:, k, m]).then_inc(stored[k], 16)
                        sp.wait_ge(vb_done, 4 * c + 4)
                        sp.dma_start(hbm["v"].rearrange("h p t c -> p h t c")[:, :, ds(c * 4, 4)],
                                     v[:, k]).then_inc(stored[k], 16)

                def loads(i):
                    for k in range(2):
                        sp.wait_ge(xn_done, 8 * i + 4 * k + 4)
                        load(k, 2 * i + k + 2)

                loads(0)
                stores(0)
                with sp.Fori(1, NC_ // 2 - 1) as i:
                    loads(i)
                    stores(i)
                stores(NC_ // 2 - 1)
                for k in range(2):
                    sp.wait_ge(stored[k], 16 * STORES * (NC_ // 2))

            @block.gpsimd
            def _(pool):
                pool.memset(ident[:], 0.0).then_inc(ident_done, 1)
                pool.memset(v[:], 0.0).then_inc(init_done, 1)
                pool.wait_ge(init_done, 1)
                pool.memset(v[:, :, :, :, D:D + 1], 1.0).then_inc(init_done, 1)
                pool.wait_ge(ident_done, 1)
                pool.affine_select(out=ident[:], in_=ident[:], compare_op=ALU.not_equal, fill=1.0, base=0,
                                   pattern=[[-1, P]], channel_multiplier=1).then_inc(ident_done, 1)
                with nc.allow_non_contiguous_dma(reason="a small table turned, once"):
                    pool.dma_start(relt[:], io["L0_attn_rel_table"].rearrange("r d -> d r")).then_inc(rel_in, 16)
                pool.memset(zeros[:], 0.0).then_inc(flags_done, 1)
                pool.wait_ge(flags_done, 1)
                for t in range(0, SLOTS, 8 * P):
                    pool.dma_start(hbm["xs"][t:t + 8 * P].rearrange("(p t) e -> p (t e)", p=P), zeros[:]).then_inc(flags_stored, 16)
                pool.memset(flags[:, 0], 0.0).then_inc(flags_done, 1)
                pool.memset(flags[:, 1], 1.0).then_inc(flags_done, 1)
                pool.wait_ge(flags_done, 3)
                for row in range(PR, QR):
                    pool.dma_start(hbm["k"][:, row, :], flags[:, int(R_MAX <= row < R_RIGHT)]).then_inc(flags_stored, 16)
                pool.wait_ge(init_done, 2)

                def split_keys(i):
                    for k in range(2):
                        c = 2 * i + k
                        f, r = full["k"][:, k], rest["k"]
                        h, m, l = (part["k", w][:, k] for w in "hml")
                        pool.wait_ge(kf_done, 2 * c + 2)
                        wait_apart(pool, stored[k], i * (16 * STORES), tick_p)
                        pool.tensor_copy(h, f).then_inc(k_split, 1)
                        pool.wait_ge(k_split, 4 * c + 1)
                        pool.tensor_tensor(r[:], f, h, ALU.subtract).then_inc(k_split, 1)
                        wait_apart(pool, k_split, 4 * c + 2, tick_p)
                        pool.tensor_copy(m, r[:]).then_inc(k_split, 1)
                        pool.wait_ge(k_split, 4 * c + 3)
                        pool.tensor_tensor(l, r[:], m, ALU.subtract).then_inc(k_split, 1)
                        pool.wait_ge(k_split, 4 * c + 4)

                rounds(pool, NC_ // 2, split_keys)
                pool.wait_ge(rel_done, 8)
                for r, w in enumerate(K_PARTS):
                    pool.dma_start(hbm["rel"][D * r:D * r + D, :], relp[w][:]).then_inc(rel_stored, 16)
                pool.wait_ge(rel_stored, 16 * len(K_PARTS))
                pool.wait_ge(flags_stored, 16 * (QR - PR + SLOTS // (8 * P)))

            @block.scalar
            def _(act):
                act.wait_ge(weights_in, 96)
                act.activation(bk4[:], bk[:], ACT.Copy, scale=D ** -0.5).then_inc(bk4_done, 1)
                act.wait_ge(bk4_done, 1)
                act.wait_ge(eps_done, 1)

                def chunk(i):
                    for k in range(2):
                        c = 2 * i + k
                        act.wait_ge(mv_done, 4 * c + 4)
                        act.activation(sd[:, k], mv[:, k, :, 1], ACT.Sqrt, bias=eps[:]).then_inc(sd_done, 1)
                        act.wait_ge(turned, c + 1)
                        act.activation(xt[:, k], pt[:], ACT.Copy).then_inc(xt_done, 1)
                        act.wait_ge(q_done, c + 1)
                        sem_wait(act, q_split, i * 8 + 4 * k - 4)
                        for m in range(2):
                            act.activation(full["q"][:, k, m], pq[:, m], ACT.Identity, bias=bq[:, m:m + 1]).then_inc(qf_done, 1)
                        act.wait_ge(k_done, c + 1)
                        sem_wait(act, k_split, i * 8 + 4 * k - 4)
                        for m in range(2):
                            act.activation(full["k"][:, k, m], pk[:, m], ACT.Identity, bias=bk4[:, m:m + 1],
                                           scale=D ** -0.5).then_inc(kf_done, 1)

                rounds(act, NC_ // 2, chunk)

            @block.tensor
            def _(pe):
                pe.wait_ge(ident_done, 2)
                pe.wait_ge(weights_in, 96)

                def chunk(i):
                    for k in range(2):
                        c = 2 * i + k
                        pe.wait_ge(xn_done, 4 * c + 4)
                        for t in range(4):
                            for e in range(2):
                                mm = pe.transpose(pt[:, e, t * P:(t + 1) * P], xn[:, k, t, e * P:(e + 1) * P], ident[:])
                        mm.then_inc(turned, 1)
                        pe.wait_ge(xt_done, c + 1)
                        for w, out, done, free, per in ((wq, pq, q_done, qf_done, 2), (wk, pk, k_done, kf_done, 2)):
                            sem_wait(pe, free, per * c)
                            for m in range(2):
                                for e in range(2):
                                    mm = pe.matmul(out[:, m], w[:, e, m * P:(m + 1) * P], xt[:, k, e], start=e == 0, stop=e == 1)
                            mm.then_inc(done, 1)
                        sem_wait(pe, vb_done, 4 * c)
                        for t in range(4):
                            for e in range(2):
                                mm = pe.matmul(pv[:, t], xt[:, k, e, t * P:(t + 1) * P], wv[:, e], start=e == 0, stop=e == 1)
                        mm.then_inc(v_done, 1)

                rounds(pe, NC_ // 2, chunk)

            @block.vector
            def _(dve):
                dve.memset(eps[:], EPS).then_inc(eps_done, 1)
                dve.memset(relz[:], 0.0).then_inc(rel_done, 1)

                def norm(k, c):
                    dve.wait_ge(x_in[k], 16 * (c // 2) + 16 if isinstance(c, int) else (c - k) * 8 + 16)
                    sem_wait(dve, turned, c - 1)
                    for t in range(4):
                        dve.bn_stats(stats[:, k, t], x[:, k, t]).then_inc(stats_done, 1)
                    wait_apart(dve, stats_done, 4 * c + 4, tick_v)
                    for t in range(4):
                        dve.bn_aggr(mv[:, k, t], stats[:, k, t]).then_inc(mv_done, 1)
                    dve.wait_ge(sd_done, c + 1)
                    dve.reciprocal(rs[:, k], sd[:, k]).then_inc(rs_done, 1)
                    dve.wait_ge(rs_done, c + 1)
                    for t in range(4):
                        dve.tensor_scalar(xn[:, k, t], x[:, k, t], mv[:, k, t, 0:1], rs[:, k, t:t + 1],
                                          ALU.subtract, ALU.mult).then_inc(xn_done, 1)

                def split(k, i):
                    c = 2 * i + k
                    f, r = full["q"][:, k], rest["q"]
                    h, m, l = (part["q", w][:, k] for w in "hml")
                    dve.wait_ge(qf_done, 2 * c + 2)
                    sem_wait(dve, stored[k], i * (16 * STORES))
                    dve.tensor_copy(h, f).then_inc(q_split, 1)
                    dve.wait_ge(q_split, 4 * c + 1)
                    dve.tensor_tensor(r[:], f, h, ALU.subtract).then_inc(q_split, 1)
                    dve.wait_ge(q_split, 4 * c + 2)
                    dve.tensor_copy(m, r[:]).then_inc(q_split, 1)
                    dve.wait_ge(q_split, 4 * c + 3)
                    dve.tensor_tensor(l, r[:], m, ALU.subtract).then_inc(q_split, 1)
                    dve.wait_ge(v_done, c + 1)
                    for t in range(4):
                        dve.tensor_tensor(v[:, k, :, t, 0:D], pv[:, t].rearrange("p (h d) -> p h d", d=D),
                                          bv[:].rearrange("p (h d) -> p h d", d=D), ALU.add).then_inc(vb_done, 1)
                    dve.wait_ge(q_split, 4 * c + 4)

                dve.wait_ge(rel_in, 16)
                dve.wait_ge(rel_done, 1)
                edge = MAXREL - 1
                dve.tensor_copy(rele[:, edge:edge + NREL], relt[:]).then_inc(rel_done, 1)
                dve.tensor_scalar(rele[:, 0:edge], relz[:, 0:edge], relt[:, 0:1], None, ALU.add).then_inc(rel_done, 1)
                dve.tensor_scalar(rele[:, edge + NREL:EXT + 1], relz[:, 0:EXT + 1 - edge - NREL],
                                  relt[:, NREL - 1:NREL], None, ALU.add).then_inc(rel_done, 1)
                dve.wait_ge(rel_done, 4)
                dve.tensor_copy(relp["h"][:], rele[:]).then_inc(rel_done, 1)
                dve.wait_ge(rel_done, 5)
                dve.tensor_tensor(relr[:], rele[:], relp["h"][:], ALU.subtract).then_inc(rel_done, 1)
                dve.wait_ge(rel_done, 6)
                dve.tensor_copy(relp["m"][:], relr[:]).then_inc(rel_done, 1)
                dve.wait_ge(rel_done, 7)
                dve.tensor_tensor(relp["l"][:], relr[:], relp["m"][:], ALU.subtract).then_inc(rel_done, 1)
                dve.wait_ge(weights_in, 96)
                dve.wait_ge(init_done, 2)

                def chunk(i):
                    for k in range(2):
                        norm(k, 2 * i + k)
                    for k in range(2):
                        split(k, i)

                rounds(dve, NC_ // 2, chunk)


def scratch(nc):
    def dram(name, shape, dt):
        return nc.dram_tensor(name, shape, dt, kind="Internal").ap()

    return {
        "q": dram("q_stack", [H, QR, N], bf16),
        "k": dram("k_stack", [H, QR, N], bf16),
        "v": dram("v_blocks", [H, P, NT, VC], fp32),
        "rel": dram("rel_stack", [PR, EXT + 1], bf16),
        "x1": dram("x_attended", [N, E], fp32),
        "xn": dram("x_normal", [N, E], fp32),
        "xs": dram("x_slots", [SLOTS, E], fp32),
        "y": dram("y_slots", [SLOTS, E], fp32),
    }


def far(nc, hbm, ctxn):
    with ExitStack() as ctx:
        sb = lambda n, s, d=fp32: ctx.enter_context(nc.sbuf_tensor(n, s, d))
        sem = lambda n: ctx.enter_context(nc.semaphore(n))
        def row_units(j):
            tiles = [i for i in range(ST) if abs(i - j) > 1]
            n = len(tiles)
            cuts = [round(x * n / 4) for x in range(5)]
            return [tiles[a:b] for a, b in zip(cuts, cuts[1:])]

        def runs(tiles, brk):
            out = []
            for at, i in enumerate(tiles):
                if out and out[-1][0] + out[-1][1] == i and not brk(i):
                    out[-1] = (out[-1][0], out[-1][1] + 1, out[-1][2])
                else:
                    out.append((i, 1, at))
            return out

        ROWT = ST - 2
        NU = 4 * ST
        ident = sb("f_ident", [P, P])
        rel = sb("f_rel", [PR, EXT + 1], bf16)
        q = sb("f_q", [QR, B, S], bf16)
        kl = sb("f_kl", [QR, B, S], bf16)
        kr = sb("f_kr", [QR, B, S], bf16)
        v = sb("f_v", [P, B, ST, VC])
        mq, mk = sb("f_mq", [PR, B, S], bf16), sb("f_mk", [PR, B, S], bf16)
        pb = [sb(f"f_p{i}", [P, ROWT * P]) for i in range(2)]
        os = sb("f_os", [P, 4, P])
        top, top_all, top_rel = sb("f_top", [P, B, 4, ST]), sb("f_top_all", [P, B, ST]), sb("f_top_rel", [P, B, ST])
        terms = sb("f_terms", [P, B, 3, ST])
        GR = 3 * ST
        rest = sb("f_rest", [GR, P])
        part = {w: sb(f"f_t{w}", [GR, B, P], bf16) for w in "hml"}
        sc = [ctx.enter_context(nc.psum_tensor(f"f_sc{i}", [P, 4 * P], fp32)) for i in range(2)]
        m = [ctx.enter_context(nc.psum_tensor(f"f_m{i}", [P, 512], fp32)) for i in range(4)]
        o = ctx.enter_context(nc.psum_tensor("f_o", [P, 4, P], fp32))
        ot = ctx.enter_context(nc.psum_tensor("f_ot", [P, 4, P], fp32))
        ident_done, ones_done, rel_in = sem("f_ident_done"), sem("f_ones_done"), sem("f_rel_in")
        stacks_in, guards_in, m_in, stored = ([sem(f"f_{n}{k}") for k in range(B)] for n in ("in", "guards_in", "m_in", "stored"))
        scored, exps, summed, os_done, turned, ctx_done = (sem(f"f_{n}") for n in ("scored", "exps", "summed", "os_d", "turned", "ctx_d"))
        tick_pe, tick_sp = sem("f_tick_pe"), sem("f_tick_sp")
        to_take, taken, guard_done, guard_turned, split = (
            sem(f"f_{n}") for n in ("to_take", "taken", "guard_d", "guard_turned", "split_d"))

        steps = [st for j in range(ST) for st in [("keys", j, x) for x in range(4)] + [("rel", j, 0)]]
        step_of = {st: i for i, st in enumerate(steps)}
        STEPS = len(steps)
        RING = 4
        reads_before = lambda i: i + sum(kind == "rel" for kind, *_ in steps[:i])
        READS = reads_before(STEPS)

        def heads(body):
            def passes(eng):
                body(None, 0, 0, None)
                body(None, 1, 1, 0)
                for k in range(B):
                    body(k, k, k + 2, k + 1)
                with eng.Fori(1, H - 1) as h:
                    for k in range(B):
                        body(2 * h + k, k, 2 * h + k + 2, 2 * h + k + 1)
                body(BH - 2, 0, None, BH - 1)
                body(BH - 1, 1, None, None)
            return passes

        def rounds_of(pair, k):
            return pair // 2 + 1 if isinstance(pair, int) else (pair - k) // 2 + 1

        with nc.Block() as block:

            @block.sync
            def _(sp):
                flat = lambda ap: ap.rearrange("r h t -> r (h t)")
                at = lambda n, rows, h, k: flat(hbm[n].rearrange("h r t -> r h t")[rows, ds(h, 1), k * S:(k + 1) * S])

                def load_m(h, k):
                    sp.dma_start(mq[:, k], at("q", slice(0, PR), h, k)).then_inc(m_in[k], 16)
                    sp.dma_start(mk[:, k], at("k", slice(0, PR), h, k)).then_inc(m_in[k], 16)

                def load_far(h, k):
                    sp.dma_start(kl[0:PR, k], at("k", slice(0, PR), h, k)).then_inc(stacks_in[k], 16)
                    sp.dma_start(kr[0:PR, k], at("k", slice(0, PR), h, k)).then_inc(stacks_in[k], 16)
                    sp.dma_start(q[0:PR, k], at("q", slice(0, PR), h, k)).then_inc(stacks_in[k], 16)
                    sp.dma_start(v[:, k], hbm["v"].rearrange("h p t c -> p h t c")[:, ds(h, 1), k * ST:(k + 1) * ST]
                                 .rearrange("p h t c -> p (h t) c")).then_inc(stacks_in[k], 16)

                def guards(h, k, pair):
                    wait_apart(sp, split, 4 * pair + 4, tick_sp)
                    for a, row, parts in ((0, R_LEFT, "hml"), (1, R_MAX, "hm"), (2, R_RIGHT, "hml")):
                        for y, w in enumerate(parts):
                            to = hbm["q"][ds(h, 1), row + y, k * S:(k + 1) * S].rearrange("h (t x) -> (h t) x", x=P)
                            sp.dma_start(to, part[w][a * ST:(a + 1) * ST, k]).then_inc(stored[k], 16)
                    wait_apart(sp, stored[k], 16 * GUARD_DMAS * (h + 1), tick_sp)
                    sp.dma_start(q[PR:QR, k], at("q", slice(PR, QR), h, k)).then_inc(guards_in[k], 16)

                GUARD_DMAS = 8
                sp.dma_start(rel[:], hbm["rel"]).then_inc(rel_in, 16)
                load_m(0, 0)
                load_m(0, 1)
                load_far(0, 0)
                sp.wait_ge(to_take, STEPS)
                load_m(1, 0)
                guards(0, 0, 0)

                def during(h, k, m_next=True, far_next=True):
                    n = 2 * h + k
                    nk, nh = 1 - k, h + k
                    if m_next:
                        wait_apart(sp, to_take, STEPS * (n + 2), tick_sp)
                        load_m(nh + 1, nk)
                    if far_next:
                        wait_apart(sp, summed, ST * n, tick_sp)
                        load_far(nh, nk)
                        guards(nh, nk, n + 1)

                for k in range(B):
                    during(0, k)
                with sp.Fori(1, H - 2) as h:
                    for k in range(B):
                        during(h, k)
                during(H - 2, 0)
                during(H - 2, 1, m_next=False)
                during(H - 1, 0, m_next=False)
                for k in range(B):
                    sp.wait_ge(guards_in[k], 16 * H)

            @block.gpsimd
            def _(pool):
                make_ident(pool, ident, ident_done)

            @block.tensor
            def _(pe):
                pe.wait_ge(ident_done, 2)
                pe.wait_ge(ones_done, 4)
                pe.wait_ge(rel_in, 16)

                def scores(n, k, j, x):
                    u = 4 * j + x
                    sem_wait(pe, exps, NU * n + u - 1)
                    for i, w, place in runs(row_units(j)[x], lambda i: False):
                        side = kl if j < i else kr
                        mm = pe.matmul(sc[u % 2][:, place * P:(place + w) * P], side[:, k, j * P:(j + 1) * P],
                                       q[:, k, i * P:(i + w) * P], start=True, stop=True)
                    mm.then_inc(scored, 1)

                def products(n, k, j):
                    pe.wait_ge(exps, NU * n + 4 * j + 4)
                    if j == 0:
                        sem_wait(pe, os_done, n)
                    for i, w, place in runs([i for i in range(ST) if abs(i - j) > 1], lambda i: i % 4 == 0):
                        g, c = i // 4, i % 4
                        mm = pe.matmul(o[32 * g:32 * g + 32, c:c + w], v[:, k, j], pb[j % 2][:, place * P:(place + w) * P],
                                       start=j == 0, stop=True, skip_group_check=True)
                    mm.then_inc(summed, 1)

                def turn(n):
                    pe.wait_ge(os_done, n + 1)
                    if not isinstance(n, int) or n < BH - 1:
                        sem_wait(pe, split, 4 * (n + 1) + 2)
                    sem_wait(pe, ctx_done, n)
                    for c in range(4):
                        mm = pe.transpose(ot[:, c], os[:, c], ident[:])
                    mm.then_inc(turned, 1)

                def turn_guards(g, k, n):
                    if n is not None:
                        sem_wait(pe, ctx_done, n)
                    wait_apart(pe, guard_done, 2 * g + 2, tick_pe)
                    pe.transpose(ot[0:GR, 0], terms[:, k].rearrange("p a t -> p (a t)"), ident[:])\
                        .then_inc(guard_turned, 1)

                def step(g, k, st):
                    i = step_of[st]
                    kind, t, quarter = st
                    sem_wait(pe, taken, READS * (g - 1) + reads_before(i - RING + 1 + STEPS) if i < RING else READS * g + reads_before(i - RING + 1))
                    if kind == "keys":
                        mm = pe.matmul(m[i % RING][:], mq[:, k, t * P:(t + 1) * P], mk[:, k, quarter * 512:(quarter + 1) * 512], start=True, stop=True)
                    else:
                        mm = pe.matmul(m[i % RING][:, 0:NREL], mq[:, k, t * P:(t + 1) * P],
                                       rel[:, MAXREL - 1:MAXREL - 1 + NREL], start=True, stop=True)
                    mm.then_inc(to_take, 1)

                def body(n, k, g, gs):
                    if n is not None:
                        pe.wait_ge(stacks_in[k], 64 * rounds_of(n, k))
                        pe.wait_ge(guards_in[k], 16 * rounds_of(n, k))
                    if g is not None:
                        pe.wait_ge(m_in[k], 32 * rounds_of(g, k))
                    for j in range(ST):
                        def keys_steps(*quarters):
                            if g is not None:
                                for x in quarters:
                                    step(g, k, ("keys", j, x))

                        if n is not None:
                            scores(n, k, j, 0)
                            if j == 1 and not (isinstance(n, int) and n == 0):
                                turn(n - 1)
                            if j == 4 and gs is not None:
                                turn_guards(gs, 1 - k, n)
                        elif j == 4 and gs is not None:
                            turn_guards(gs, 1 - k, n)
                        keys_steps(0, 1)
                        if n is not None:
                            scores(n, k, j, 1)
                            if j:
                                products(n, k, j - 1)
                            elif not (isinstance(n, int) and n == 0):
                                products(n - 1, 1 - k, ST - 1)
                            scores(n, k, j, 2)
                        keys_steps(2, 3)
                        if n is not None:
                            scores(n, k, j, 3)
                        if g is not None:
                            step(g, k, ("rel", j, 0))

                heads(body)(pe)
                products(BH - 1, 1, ST - 1)
                turn(BH - 1)

            @block.scalar
            def _(act):
                def copy_sums(n):
                    act.wait_ge(summed, ST * n + ST)
                    sem_wait(act, turned, n)
                    act.activation(os[:], o[:], ACT.Copy).then_inc(os_done, 1)

                def body(n, k, g, gs):
                    for j in range(ST):
                        if n is not None:
                            sem_wait(act, summed, ST * n + j - 1)
                        at = 0
                        for x in range(4):
                            if n is not None:
                                u = 4 * j + x
                                w = len(row_units(j)[x]) * P
                                act.wait_ge(scored, NU * n + u + 1)
                                act.activation(pb[j % 2][:, at:at + w], sc[u % 2][:, 0:w], ACT.Exp).then_inc(exps, 1)
                                at += w
                        if j == 0 and n is not None and not (isinstance(n, int) and n == 0):
                            copy_sums(n - 1)

                heads(body)(act)
                copy_sums(BH - 1)

            @block.vector
            def _(dve):
                dve.memset(kl[PR:QR], 0.0).then_inc(ones_done, 1)
                dve.memset(kr[PR:QR], 1.0).then_inc(ones_done, 1)
                dve.wait_ge(ones_done, 2)
                dve.memset(kl[PR:R_RIGHT], 1.0).then_inc(ones_done, 1)
                dve.memset(kr[PR:R_MAX], 0.0).then_inc(ones_done, 1)

                def step(g, k, st):
                    i = step_of[st]
                    kind, t, quarter = st
                    dve.wait_ge(to_take, STEPS * g + i + 1)
                    if kind == "keys":
                        dve.tensor_reduce(top[:, k, quarter, t:t + 1], m[i % RING][:], AX.X, ALU.max).then_inc(taken, 1)
                    else:
                        dve.tensor_reduce(top_rel[:, k, t:t + 1], m[i % RING][:, 0:NREL], AX.X, ALU.max).then_inc(taken, 1)
                        dve.tensor_copy(terms[:, k, 0:3:2, t], m[i % RING][:, 0:NREL:NREL - 1]).then_inc(taken, 1)

                def guard(g, k, stage):
                    if stage == 0:
                        dve.wait_ge(taken, READS * g + READS)
                        dve.tensor_reduce(top_all[:, k], top[:, k].rearrange("p q t -> p t q"), AX.X, ALU.max).then_inc(guard_done, 1)
                    else:
                        dve.wait_ge(guard_done, 2 * g + 1)
                        dve.scalar_tensor_tensor(out=terms[:, k, 1], in0=top_all[:, k], scalar=-1.0, in1=top_rel[:, k],
                                                 op0=ALU.mult, op1=ALU.subtract).then_inc(guard_done, 1)

                def split_guard(g, k, stage):
                    h, mid, low = (part[w][:, k] for w in "hml")
                    if stage == 0:
                        dve.wait_ge(guard_turned, g + 1)
                        sem_wait(dve, stored[k], 128 * (rounds_of(g, k) - 1))
                        dve.tensor_copy(h, ot[0:GR, 0]).then_inc(split, 1)
                        return
                    dve.wait_ge(split, 4 * g + stage)
                    if stage == 1:
                        dve.tensor_tensor(rest[:], ot[0:GR, 0], h, ALU.subtract).then_inc(split, 1)
                    elif stage == 2:
                        dve.tensor_copy(mid, rest[:]).then_inc(split, 1)
                    else:
                        dve.tensor_tensor(low, rest[:], mid, ALU.subtract).then_inc(split, 1)

                def sums(h, k, n):
                    dve.wait_ge(turned, n + 1)
                    c = ctxn[:, ds(h, 1), k].rearrange("p h (g c) x -> p (h g) c x", c=4)
                    dve.tensor_copy(c, ot[:].rearrange("p c (g x) -> p g c x", g=4)[:, :, :, 0:D + 1]).then_inc(ctx_done, 1)

                def body(n, k, g, gs):
                    if g is not None:
                        sem_wait(dve, guard_turned, g - 1)
                    for j in range(ST):
                        if g is not None:
                            for x in range(4):
                                step(g, k, ("keys", j, x))
                                if x == 1 and j == 0 and gs is not None:
                                    guard(gs, 1 - k, 0)
                            step(g, k, ("rel", j, 0))
                        elif j == 0 and gs is not None:
                            guard(gs, 1 - k, 0)
                        if j == 0 and gs is not None:
                            guard(gs, 1 - k, 1)
                        if j == 2 and n is not None and not (isinstance(n, int) and n == 0):
                            prev = (n - 1) // 2 if isinstance(n, int) else ((n - k) // 2 if k else (n - 2) // 2)
                            sums(prev, 1 - k, n - 1)
                        if gs is not None and 5 <= j <= 8:
                            split_guard(gs, 1 - k, j - 5)

                heads(body)(dve)
                sums(H - 1, 1, BH - 1)
                dve.wait_ge(ctx_done, BH)


def near(nc, hbm, ctxn):
    with ExitStack() as ctx:
        sb = lambda n, s, d=fp32: ctx.enter_context(nc.sbuf_tensor(n, s, d))
        sem = lambda n: ctx.enter_context(nc.semaphore(n))
        ident = sb("n_ident", [P, P])
        rel = sb("n_rel", [PR, EXT + 1], bf16)
        kw = [sb(f"n_k{i}", [QR, H, B, 3 * P], bf16) for i in range(2)]
        qw = [sb(f"n_q{i}", [QR, H, B, P], bf16) for i in range(2)]
        vw = [sb(f"n_v{i}", [P, H, B, 3, VC]) for i in range(2)]
        HALF = P // 2
        HB, QB = BH // 2, HALF // 2
        pb = [sb(f"n_p{i}", [P, 2, 2, 2, HB, QB]) for i in range(2)]
        G = BH // 4
        os = sb("n_os", [P, G, P])
        sc = ctx.enter_context(nc.psum_tensor("n_sc", [P, 2, 2, HB, QB], fp32))
        o = ctx.enter_context(nc.psum_tensor("n_o", [P, G, P], fp32))
        ot = ctx.enter_context(nc.psum_tensor("n_ot", [P, G, P], fp32))
        ident_done, rel_in = sem("n_ident_done"), sem("n_rel_in")
        tile_in = [sem(f"n_tile_in{i}") for i in range(2)]
        scored, exps, summed, os_done, turned, ctx_done = (sem(f"n_{n}") for n in ("scored", "exps", "summed", "os_d", "turned", "ctx_d"))
        DMAS = 6
        SLOTS_OF = lambda edge: (1, 2) if edge == 0 else (0, 1) if edge == 1 else (0, 1, 2)
        first_step = lambda I: 0 if isinstance(I, int) and I == 0 else 3 * I - 1
        first_pb = lambda buf, edge: 1 if edge is None and buf == 0 else 0

        def tiles(eng, body):
            body(0, 0, 0)
            with eng.Fori(0, ST // 2 - 1) as i:
                for j in range(2):
                    body(2 * i + 1 + j, (1 + j) % 2, None)
            body(ST - 1, 1, 1)

        with nc.Block() as block:

            @block.sync
            def _(sp):
                def load(I, buf, edge):
                    lo = 1 if edge == 0 else 0
                    w = 2 if edge in (0, 1) else 3
                    t0 = I - 1 + lo
                    for b in range(B):
                        sp.dma_start(kw[buf][:, :, b, lo * P:(lo + w) * P],
                                     hbm["k"].rearrange("h r t -> r h t")[:, :, ds(t0 * P + b * S, w * P)]).then_inc(tile_in[buf], 16)
                        sp.dma_start(qw[buf][:, :, b],
                                     hbm["q"].rearrange("h r t -> r h t")[:, :, ds(I * P + b * S, P)]).then_inc(tile_in[buf], 16)
                        sp.dma_start(vw[buf][:, :, b, lo:lo + w],
                                     hbm["v"].rearrange("h p t c -> p h t c")[:, :, ds(t0 + b * ST, w)]).then_inc(tile_in[buf], 16)

                sp.dma_start(rel[:], hbm["rel"]).then_inc(rel_in, 16)
                load(0, 0, 0)
                load(1, 1, None)

                def next_load(I, buf, edge):
                    sp.wait_ge(summed, first_step(I - 1))
                    load(I, buf, edge)

                with sp.Fori(0, ST // 2 - 2) as i:
                    for j in range(2):
                        next_load(2 * i + 2 + j, j, None)
                next_load(ST - 2, 0, None)
                next_load(ST - 1, 1, 1)

            @block.gpsimd
            def _(pool):
                pool.memset(ident[:], 0.0).then_inc(ident_done, 1)
                pool.wait_ge(ident_done, 1)
                pool.affine_select(out=ident[:], in_=ident[:], compare_op=ALU.not_equal, fill=1.0, base=0,
                                   pattern=[[-1, P]], channel_multiplier=1).then_inc(ident_done, 1)

            @block.tensor
            def _(pe):
                pe.wait_ge(ident_done, 2)
                pe.wait_ge(rel_in, 16)

                def scores(buf, s, slot, u):
                    kb, qb = kw[buf], qw[buf]
                    for half in range(2):
                        sem_wait(pe, exps, 2 * u - 1 + half)
                        hs = slice(half * H // 2, (half + 1) * H // 2)
                        for x in range(HB):
                            h, b = (half * HB + x) // B, x % B
                            for y in range(2):
                                i0 = s * HALF + y * QB
                                pe.matmul(sc[:, half, y, x], kb[:, h, b, slot * P:(slot + 1) * P], qb[:, h, b, i0:i0 + QB],
                                          start=x == 0, stop=False, skip_group_check=True)
                        for i in range(HALF):
                            col = (slot - 1) * P - (s * HALF + i) + 2 * MAXREL - 1
                            mm = pe.matmul(sc[:, half, i // QB, :, i % QB], rel[:, col:col + P],
                                           qb[0:PR, hs, :, s * HALF + i].rearrange("r h b -> r (h b)"),
                                           start=False, stop=True, skip_group_check=True)
                        mm.then_inc(scored, 1)

                def products(I, buf, slot, n, which, step):
                    pe.wait_ge(exps, 4 * step + 4)
                    if n == 0:
                        sem_wait(pe, os_done, I)
                    for g in range(G):
                        for x in range(4):
                            bh = 4 * g + x
                            mm = pe.matmul(o[32 * x:32 * x + 32, g], vw[buf][:, bh // B, bh % B, slot],
                                           pb[which][:, bh // HB, :, :, bh % HB, :].rearrange("p s y q -> p (s y) q"),
                                           start=(n == 0 and g % 4 == 0), stop=True, skip_group_check=True)
                    mm.then_inc(summed, 1)

                def turn(I):
                    sem_wait(pe, os_done, I + 1)
                    sem_wait(pe, ctx_done, I)
                    for g in range(G):
                        mm = pe.transpose(ot[:, g], os[:, g], ident[:])
                    mm.then_inc(turned, 1)

                def tile(I, buf, edge):
                    pe.wait_ge(tile_in[buf], 16 * DMAS if isinstance(I, int) and I < 2 else (I - buf) * (8 * DMAS) + 16 * DMAS)
                    slots, step, p0 = SLOTS_OF(edge), first_step(I), first_pb(buf, edge)
                    for n, slot in enumerate(slots):
                        scores(buf, 0, slot, 2 * (step + n))
                        if n:
                            products(I, buf, slots[n - 1], n - 1, (p0 + n - 1) % 2, step + n - 1)
                        elif edge != 0:
                            products(I - 1, 1 - buf, 2, 2, (p0 + 1) % 2, step - 1)
                        if n == 1 and edge != 0:
                            turn(I - 1)
                        scores(buf, 1, slot, 2 * (step + n) + 1)

                tiles(pe, tile)

                products(ST - 1, 1, SLOTS_OF(1)[-1], 1, (first_pb(1, 1) + 1) % 2, first_step(ST - 1) + 1)
                turn(ST - 1)

            @block.scalar
            def _(act):
                def tile(I, buf, edge):
                    p0 = first_pb(buf, edge)
                    for n in range(len(SLOTS_OF(edge))):
                        step = first_step(I) + n
                        sem_wait(act, summed, step - 1)
                        for s in range(2):
                            for half in range(2):
                                act.wait_ge(scored, 4 * step + 2 * s + half + 1)
                                act.activation(pb[(p0 + n) % 2][:, half, s], sc[:, half], ACT.Exp).then_inc(exps, 1)

                tiles(act, tile)

            @block.vector
            def _(dve):
                def tile(I, buf, edge):
                    dve.wait_ge(summed, first_step(I) + len(SLOTS_OF(edge)))
                    sem_wait(dve, turned, I)
                    dve.tensor_copy(os[:], o[:]).then_inc(os_done, 1)
                    dve.wait_ge(turned, I + 1)
                    c = ctxn[:, :, :, ds(I, 1), :].rearrange("p h b t c -> p (h b t) c")
                    dve.tensor_tensor(c, ot[:].rearrange("p g (x c) -> p (g x) c", c=VC)[:, :, 0:D + 1], c, ALU.add).then_inc(ctx_done, 1)

                tiles(dve, tile)
                dve.wait_ge(ctx_done, ST)


WS = 64.0


def make_ident(pool, ident, done):
    pool.memset(ident[:], 0.0).then_inc(done, 1)
    pool.wait_ge(done, 1)
    pool.affine_select(out=ident[:], in_=ident[:], compare_op=ALU.not_equal, fill=1.0, base=0,
                       pattern=[[-1, P]], channel_multiplier=1).then_inc(done, 1)


def combine(nc, io, hbm, ctxn, w1, w2, logits):
    with ExitStack() as ctx:
        sb = lambda n, s, d=fp32: ctx.enter_context(nc.sbuf_tensor(n, s, d))
        sem = lambda n: ctx.enter_context(nc.semaphore(n))
        ident = sb("c_ident", [P, P])
        wo, wr = sb("c_wo", [P, 2, E]), sb("c_wr", [P, 2, NE])
        bo, br, eps = sb("c_bo", [P, E]), sb("c_br", [P, NE]), sb("c_eps", [P, 1])
        raw = [sb(f"c_raw{i}", [P, 2 * FI]) for i in range(2)]
        x = sb("c_x", [P, B, E])
        xb = sb("c_xb", [P, B, E])
        rden = sb("c_rden", [P, B, H])
        c = sb("c_c", [P, B, E])
        ct = sb("c_ct", [P, B, 2, P])
        x1 = sb("c_x1", [P, B, E])
        stats, mv, sd, rs = sb("c_stats", [P, B, 6]), sb("c_mv", [P, B, 2]), sb("c_sd", [P, B]), sb("c_rs", [P, B])
        xn = sb("c_xn", [P, B, E])
        xnt = sb("c_xnt", [P, B, 2, P])
        ps = lambda n, s: ctx.enter_context(nc.psum_tensor(n, s, fp32))
        pc = [ps(f"c_pc{b}", [P, 2, P]) for b in range(B)]
        po = [ps(f"c_po{b}", [P, E]) for b in range(B)]
        pn = [ps(f"c_pn{b}", [P, 2, P]) for b in range(B)]
        pl = [ps(f"c_pl{b}", [P, NE]) for b in range(B)]
        ident_done, consts_in, eps_done = sem("c_ident_done"), sem("c_consts_in"), sem("c_eps_done")
        raw_in, hi_done, lo_done = [sem(f"c_raw_in{i}") for i in range(2)], sem("c_hi_done"), sem("c_lo_done")
        x_in, stored = [sem(f"c_x_in{b}") for b in range(B)], [sem(f"c_stored{b}") for b in range(B)]
        names = ("xb", "rden", "c", "ctp", "ct", "o", "x1", "stats", "mv", "sd", "rs", "xn", "xnp", "xnt", "lp", "l", "tick")
        done = {n: sem(f"c_{n}_done") for n in names}
        x_h = io["L0_attn_q"].rearrange("b (t p) e -> p b t e", p=P)

        with nc.Block() as block:

            @block.sync
            def _(sp):
                sp.dma_start(wo[:], io["L0_attn_Wo"].rearrange("(c p) n -> p c n", p=P)).then_inc(consts_in, 16)
                sp.dma_start(wr[:], io["L0_ffn_wr"].rearrange("(c p) n -> p c n", p=P)).then_inc(consts_in, 16)
                sp.dma_start(bo[:], io["L0_attn_bo"].rearrange("(a n) -> a n", a=1).to_broadcast([P, E])).then_inc(consts_in, 16)
                sp.dma_start(br[:], io["L0_ffn_br"].rearrange("(a n) -> a n", a=1).to_broadcast([P, NE])).then_inc(consts_in, 16)

                def tile(i):
                    for b in range(B):
                        sem_wait(sp, done["xb"], B * i - 1 + b if not isinstance(i, int) else 0)
                        sp.dma_start(x[:, b], x_h[:, b, ds(i, 1)].rearrange("p t e -> p (t e)")).then_inc(x_in[b], 16)
                    for b in range(B):
                        sp.wait_ge(done["x1"], B * i + b + 1)
                        sp.dma_start(hbm["x1"].rearrange("(b t p) e -> p b t e", p=P, b=B)[:, b, ds(i, 1)].rearrange("p t e -> p (t e)"),
                                     x1[:, b]).then_inc(stored[b], 16)
                        sp.wait_ge(done["xn"], B * i + b + 1)
                        sp.dma_start(hbm["xn"].rearrange("(b t p) e -> p b t e", p=P, b=B)[:, b, ds(i, 1)].rearrange("p t e -> p (t e)"),
                                     xn[:, b]).then_inc(stored[b], 16)

                rounds(sp, ST, tile)
                for b in range(B):
                    sp.wait_ge(stored[b], 32 * ST)

            @block.gpsimd
            def _(pool):
                make_ident(pool, ident, ident_done)
                pool.wait_ge(ident_done, 2)

                pool.wait_ge(consts_in, 64)

                def tile(i):
                    for b in range(B):
                        pool.wait_ge(x_in[b], 16 * i + 16)
                        sem_wait(pool, done["x1"], B * i + b - 1 if not isinstance(i, int) else 0)
                        pool.tensor_tensor(xb[:, b], x[:, b], bo[:], ALU.add).then_inc(done["xb"], 1)

                rounds(pool, ST, tile)

            @block.scalar
            def _(act):
                act.wait_ge(eps_done, 1)

                def load(e, k):
                    act.dma_start(raw[0][:].rearrange("p (c n) -> p c n", c=2) if k == 0 else raw[1][:].rearrange("p (c n) -> p c n", c=8),
                                  io["L0_ffn_w1" if k == 0 else "L0_ffn_w2"][ds(e, 1)].rearrange("a (c p) n -> p (a c) n", p=P))\
                       .then_inc(raw_in[k], 16)

                for k in range(2):
                    load(0, k)

                def tile(i):
                    for b in range(B):
                        act.wait_ge(done["ctp"], B * i + b + 1)
                        act.activation(ct[:, b], pc[b][:], ACT.Copy).then_inc(done["ct"], 1)
                    for b in range(B):
                        act.wait_ge(done["mv"], B * i + b + 1)
                        act.activation(sd[:, b:b + 1], mv[:, b, 1:2], ACT.Sqrt, bias=eps[:]).then_inc(done["sd"], 1)
                    for b in range(B):
                        act.wait_ge(done["xnp"], B * i + b + 1)
                        act.activation(xnt[:, b], pn[b][:], ACT.Copy).then_inc(done["xnt"], 1)

                def weights(e, k):
                    act.wait_ge(raw_in[k], 16 * e + 16)
                    w = (w1, w2)[k][0]
                    act.activation(w[:, ds(e, 1)].rearrange("p a n -> p (a n)"), raw[k][:], ACT.Copy, scale=WS).then_inc(hi_done, 1)

                def pair(e):
                    tile(2 * e)
                    weights(e, 0)
                    tile(2 * e + 1)
                    weights(e, 1)

                pair(0)
                with act.Fori(1, NE) as e:
                    for k in range(2):
                        act.wait_ge(lo_done, 2 * e - 1 + k)
                        load(e, k)
                    pair(e)

            @block.tensor
            def _(pe):
                pe.wait_ge(ident_done, 2)
                pe.wait_ge(consts_in, 64)

                def tile(i):
                    for b in range(B):
                        pe.wait_ge(done["c"], B * i + b + 1)
                        for e in range(2):
                            mm = pe.transpose(pc[b][:, e], c[:, b, e * P:(e + 1) * P], ident[:])
                        mm.then_inc(done["ctp"], 1)
                    for b in range(B):
                        pe.wait_ge(done["ct"], B * i + b + 1)
                        for e in range(2):
                            mm = pe.matmul(po[b][:], ct[:, b, e], wo[:, e], start=e == 0, stop=e == 1)
                        mm.then_inc(done["o"], 1)
                    for b in range(B):
                        pe.wait_ge(done["xn"], B * i + b + 1)
                        for e in range(2):
                            mm = pe.transpose(pn[b][:, e], xn[:, b, e * P:(e + 1) * P], ident[:])
                        mm.then_inc(done["xnp"], 1)
                    for b in range(B):
                        pe.wait_ge(done["xnt"], B * i + b + 1)
                        for e in range(2):
                            mm = pe.matmul(pl[b][:], xnt[:, b, e], wr[:, e], start=e == 0, stop=e == 1)
                        mm.then_inc(done["lp"], 1)

                rounds(pe, ST, tile)

            @block.vector
            def _(dve):
                dve.memset(eps[:], EPS).then_inc(eps_done, 1)
                dve.wait_ge(consts_in, 64)

                def tile(i):
                    n = lambda b: B * i + b + 1
                    for b in range(B):
                        sem_wait(dve, done["ctp"], n(b) - B)
                        dve.reciprocal(rden[:, b], ctxn[:, :, b, ds(i, 1), D].rearrange("p h t -> p (h t)")).then_inc(done["rden"], 1)
                    for b in range(B):
                        dve.wait_ge(done["rden"], n(b))
                        dve.tensor_tensor(c[:, b].rearrange("p (h d) -> p h d", d=D),
                                          ctxn[:, :, b, ds(i, 1), 0:D].rearrange("p h t d -> p (h t) d"),
                                          rden[:, b].rearrange("p (h a) -> p h a", a=1).to_broadcast([P, H, D]), ALU.mult)\
                           .then_inc(done["c"], 1)
                    for b in range(B):
                        dve.wait_ge(done["o"], n(b))
                        sem_wait(dve, stored[b], 32 * i)
                        dve.wait_ge(done["xb"], n(b))
                        dve.tensor_tensor(x1[:, b], po[b][:], xb[:, b], ALU.add).then_inc(done["x1"], 1)
                    for b in range(B):
                        dve.wait_ge(done["x1"], n(b))
                        dve.bn_stats(stats[:, b], x1[:, b]).then_inc(done["stats"], 1)
                    for b in range(B):
                        wait_apart(dve, done["stats"], n(b), done["tick"])
                        dve.bn_aggr(mv[:, b], stats[:, b]).then_inc(done["mv"], 1)
                    for b in range(B):
                        dve.wait_ge(done["sd"], n(b))
                        dve.reciprocal(rs[:, b:b + 1], sd[:, b:b + 1]).then_inc(done["rs"], 1)
                    for b in range(B):
                        dve.wait_ge(done["rs"], n(b))
                        dve.tensor_scalar(xn[:, b], x1[:, b], mv[:, b, 0:1], rs[:, b:b + 1], ALU.subtract, ALU.mult)\
                           .then_inc(done["xn"], 1)
                    for b in range(B):
                        dve.wait_ge(done["lp"], n(b))
                        dve.tensor_tensor(logits[:, b, ds(i, 1)].rearrange("p t e -> p (t e)"), pl[b][:], br[:], ALU.add)\
                           .then_inc(done["l"], 1)

                def weights(e, k):
                    hi, lo = (w1, w2)[k]
                    dve.wait_ge(hi_done, 2 * e + k + 1)
                    dve.scalar_tensor_tensor(out=lo[:, ds(e, 1)].rearrange("p a n -> p (a n)"), in0=raw[k][:], scalar=WS,
                                             in1=hi[:, ds(e, 1)].rearrange("p a n -> p (a n)"), op0=ALU.mult, op1=ALU.subtract)\
                       .then_inc(lo_done, 1)

                def pair(e):
                    tile(2 * e)
                    weights(e, 0)
                    tile(2 * e + 1)
                    weights(e, 1)

                rounds(dve, NE, pair)
                dve.wait_ge(done["l"], NT)
                dve.wait_ge(lo_done, 2 * NE)


def route(nc, io, hbm, logits, gate, slot, owner):
    with ExitStack() as ctx:
        sb = lambda n, s, d=fp32: ctx.enter_context(nc.sbuf_tensor(n, s, d))
        sem = lambda n: ctx.enter_context(nc.semaphore(n))
        xn = sb("r_xn", [P, NT, E])
        ones, below = sb("r_ones", [P, P], bf16), sb("r_below", [P, P], bf16)
        e_of, e_less, starts_at = sb("r_e_of", [P, NT, NE]), sb("r_e_less", [P, NT, NE]), sb("r_starts", [P, SLOT_TILES + 1, NE])
        ione = sb("r_ione", [P, NT])
        best, second, gap, ex = (sb(f"r_{n}", [P, NT]) for n in ("best", "second", "gap", "ex"))
        top = sb("r_top", [P, NT])
        a = [sb(f"r_a{i}", [P, NT, NE]) for i in range(4)]
        oh, ohb = sb("r_oh", [P, NT, NE]), sb("r_ohb", [P, NT, NE], bf16)
        tot, inc, base = (sb(f"r_{n}", [P, NE, NT]) for n in ("tot", "inc", "base"))
        cnt, rem, room, end, start = (sb(f"r_{n}", [P, NE]) for n in ("cnt", "rem", "room", "end", "start"))
        cnti, remi = sb("r_cnti", [P, NE], i32), sb("r_remi", [P, NE], i32)
        slotf = sb("r_slotf", [P, NT])
        own, ownf = sb("r_own", [P, SLOT_TILES + 1, NE]), sb("r_ownf", [P, SLOT_TILES + 1])
        pp = ctx.enter_context(nc.psum_tensor("r_pp", [P, NT * NE], fp32))
        pt = ctx.enter_context(nc.psum_tensor("r_pt", [P, NT * NE], fp32))
        consts, ones_done, below_done, oh_done, ranked = (sem(f"r_{n}") for n in ("consts", "ones_done", "below_done", "oh_done", "ranked"))
        step, gap_done, ex_done, slot_done, xn_in, sent = (sem(f"r_{n}") for n in ("step", "gap_done", "ex_done", "slot_done", "xn_in", "sent"))

        with nc.Block() as block:

            @block.sync
            def _(sp):
                sp.dma_start(xn[:], hbm["xn"].rearrange("(t p) e -> p t e", p=P)).then_inc(xn_in, 16)
                sp.wait_ge(xn_in, 16)

            @block.gpsimd
            def _(pool):
                pool.iota(e_of[:], pattern=[[0, NT], [1, NE]], base=0, channel_multiplier=0, allow_small_or_imprecise_dtypes=True).then_inc(consts, 1)
                pool.iota(e_less[:], pattern=[[0, NT], [1, NE]], base=-NE, channel_multiplier=0, allow_small_or_imprecise_dtypes=True).then_inc(consts, 1)
                pool.iota(starts_at[:], pattern=[[P, SLOT_TILES + 1], [0, NE]], base=0, channel_multiplier=0, allow_small_or_imprecise_dtypes=True).then_inc(consts, 1)
                pool.memset(ione[:], 1.0).then_inc(consts, 1)
                pool.memset(ones[:], 1.0).then_inc(ones_done, 1)
                pool.wait_ge(ones_done, 1)
                pool.affine_select(out=below[:], in_=ones[:], compare_op=ALU.is_gt, fill=0.0, base=0,
                                   pattern=[[1, P]], channel_multiplier=-1).then_inc(below_done, 1)
                pool.wait_ge(below_done, 1)
                pool.wait_ge(slot_done, 1)
                pool.wait_ge(xn_in, 16)
                for t in range(NT):
                    pool.indirect_dma_start(out=hbm["xs"], out_offset=bass.IndirectOffsetOnAxis(ap=slot[:, t:t + 1], axis=0),
                                            in_=xn[:, t], in_offset=None, bounds_check=SLOTS - 1, oob_is_err=True).then_inc(sent, 16)
                pool.wait_ge(sent, 16 * NT)

            @block.scalar
            def _(act):
                act.wait_ge(gap_done, 1)
                act.activation(ex[:], gap[:], ACT.Exp).then_inc(ex_done, 1)

            @block.tensor
            def _(pe):
                pe.wait_ge(below_done, 1)
                pe.wait_ge(oh_done, 1)
                flat = ohb[:].rearrange("p t e -> p (t e)")
                pe.matmul(pp[:], below[:], flat, start=True, stop=True).then_inc(ranked, 1)
                pe.matmul(pt[:], ones[:], flat, start=True, stop=True).then_inc(ranked, 1)

            @block.vector
            def _(dve):
                n = [0]

                def then(ins):
                    n[0] += 1
                    ins.then_inc(step, 1)
                    dve.wait_ge(step, n[0])

                wide = lambda ap, m=NE: ap.rearrange("p (t a) -> p t a", a=1).to_broadcast([P, ap.shape[1], m])
                l = logits[:].rearrange("p b t e -> p (b t) e")
                dve.wait_ge(consts, 4)
                then(dve.tensor_reduce(best[:], l, AX.X, ALU.max))
                then(dve.tensor_tensor(a[0][:], l, wide(best[:]), ALU.is_equal))
                then(dve.tensor_tensor(a[1][:], a[0][:], e_less[:], ALU.mult))
                then(dve.tensor_reduce(top[:], a[1][:], AX.X, ALU.min))
                then(dve.tensor_tensor(oh[:], e_less[:], wide(top[:]), ALU.is_equal))
                dve.tensor_copy(ohb[:], oh[:]).then_inc(oh_done, 1)
                then(dve.scalar_tensor_tensor(out=a[2][:], in0=oh[:], scalar=-3.0e38, in1=l, op0=ALU.mult, op1=ALU.add))
                then(dve.tensor_reduce(second[:], a[2][:], AX.X, ALU.max))
                dve.tensor_tensor(gap[:], second[:], best[:], ALU.subtract).then_inc(gap_done, 1)
                dve.wait_ge(ranked, 2)
                then(dve.tensor_copy(tot[:], pt[:].rearrange("p (t e) -> p e t", e=NE)))
                for e in range(NE):
                    ins = dve.tensor_tensor_scan(inc[:, e], ione[:], tot[:, e], 0.0, ALU.mult, ALU.add)
                    n[0] += 1
                    ins.then_inc(step, 1)
                dve.wait_ge(step, n[0])
                then(dve.tensor_scalar(cnt[:], inc[:, :, NT - 1], float(P - 1), None, ALU.add))
                then(dve.tensor_copy(cnti[:], cnt[:]))
                then(dve.tensor_scalar(remi[:], cnti[:], P - 1, None, ALU.bitwise_and))
                then(dve.tensor_copy(rem[:], remi[:]))
                then(dve.tensor_tensor(room[:], cnt[:], rem[:], ALU.subtract))
                then(dve.tensor_tensor_scan(end[:], ione[:, 0:NE], room[:], 0.0, ALU.mult, ALU.add))
                then(dve.tensor_tensor(start[:], end[:], room[:], ALU.subtract))
                then(dve.tensor_tensor(base[:], inc[:], tot[:], ALU.subtract))
                then(dve.tensor_tensor(tot[:], base[:], wide(start[:], NT), ALU.add))
                then(dve.tensor_tensor(a[3][:], pp[:].rearrange("p (t e) -> p t e", e=NE), tot[:].rearrange("p e t -> p t e"), ALU.add))
                then(dve.tensor_tensor(a[0][:], a[3][:], oh[:], ALU.mult))
                then(dve.tensor_reduce(slotf[:], a[0][:], AX.X, ALU.add))
                dve.tensor_copy(slot[:], slotf[:]).then_inc(slot_done, 1)
                then(dve.tensor_tensor(own[:], starts_at[:], end[:].rearrange("p (a e) -> p a e", a=1).to_broadcast([P, SLOT_TILES + 1, NE]), ALU.is_ge))
                then(dve.tensor_reduce(ownf[:], own[:], AX.X, ALU.add))
                then(dve.tensor_scalar(ownf[:], ownf[:], float(NE - 1), None, ALU.min))
                then(dve.tensor_copy(owner[:], ownf[:]))
                dve.wait_ge(ex_done, 1)
                then(dve.tensor_scalar(ex[:], ex[:], 1.0, None, ALU.add))
                then(dve.reciprocal(gate[:], ex[:]))


def experts(nc, io, hbm, w1, w2, owner):
    with ExitStack() as ctx:
        sb = lambda n, s, d=fp32: ctx.enter_context(nc.sbuf_tensor(n, s, d))
        sem = lambda n: ctx.enter_context(nc.semaphore(n))
        (w1h, w1l), (w2h, w2l) = w1, w2
        KC, IC = E // P, FI // P
        HC = IC // 2
        ident = sb("e_ident", [P, P])
        b1r, b1 = sb("e_b1r", [NE * IC, P]), sb("e_b1", [P, NE * IC])
        b2 = sb("e_b2", [P, NE, E])
        xs = sb("e_xs", [P, 2, E])
        xh, xl = sb("e_xh", [P, 2, KC, P], fp16), sb("e_xl", [P, 2, KC, P], fp16)
        g = sb("e_g", [P, 2, IC, P])
        gh, gl = sb("e_gh", [P, 2, IC, P], fp16), sb("e_gl", [P, 2, IC, P], fp16)
        ys = sb("e_ys", [P, 2, E])
        px = [ctx.enter_context(nc.psum_tensor(f"e_px{k}", [P, KC, P], fp32)) for k in range(2)]
        ph = [ctx.enter_context(nc.psum_tensor(f"e_ph{k}", [P, IC, P], fp32)) for k in range(2)]
        py = [ctx.enter_context(nc.psum_tensor(f"e_py{k}", [P, E], fp32)) for k in range(2)]
        ident_done, b_in, b1_done = sem("e_ident_done"), sem("e_b_in"), sem("e_b1_done")
        b1_turned = sem("e_b1_turned")
        x_in, stored = [sem(f"e_x_in{k}") for k in range(2)], [sem(f"e_stored{k}") for k in range(2)]
        xt_done, xh_done, xl_done, h_done, g_done, gh_done, gl_done, y_done, ys_done = (
            sem(f"e_{n}_done") for n in ("xt", "xh", "xl", "h", "g", "gh", "gl", "y", "ys"))
        xs_h = hbm["xs"].rearrange("(t p) e -> p t e", p=P)
        y_h = hbm["y"].rearrange("(t p) e -> p t e", p=P)
        T2 = (SLOT_TILES + 1) // 2

        with nc.Block() as block:

            @block.sync
            def _(sp):
                sp.dma_start(b1r[:], io["L0_ffn_b1"].rearrange("e (c p) -> (e c) p", p=P)).then_inc(b_in, 16)
                sp.dma_start(b2[:], io["L0_ffn_b2"].rearrange("(a e) n -> a e n", a=1).to_broadcast([P, NE, E])).then_inc(b_in, 16)

                def load(t, k):
                    sp.dma_start(xs[:, k], xs_h[:, ds(t, 1)].rearrange("p t e -> p (t e)")).then_inc(x_in[k], 16)

                def store(t, k):
                    sp.wait_ge(ys_done, t + 1)
                    sp.dma_start(y_h[:, ds(t, 1)].rearrange("p t e -> p (t e)"), ys[:, k]).then_inc(stored[k], 16)

                for k in range(2):
                    load(k, k)
                with sp.Fori(0, T2 - 1) as i:
                    for k in range(2):
                        sp.wait_ge(xt_done, 2 * i + k + 1)
                        load(2 * i + k + 2, k)
                    for k in range(2):
                        store(2 * i + k, k)
                for k in range(2):
                    store(2 * T2 - 2 + k, k)
                for k in range(2):
                    sp.wait_ge(stored[k], 16 * T2)

            @block.gpsimd
            def _(pool):
                make_ident(pool, ident, ident_done)

            @block.tensor
            def _(pe):
                pe.wait_ge(ident_done, 2)
                pe.wait_ge(b_in, 32)
                pe.transpose(px[0][:, 0, 0:NE * IC], b1r[:], ident[0:NE * IC, 0:NE * IC]).then_inc(b1_turned, 1)
                pe.wait_ge(b1_done, 1)

                def turn(i, k):
                    t = 2 * i + k
                    pe.wait_ge(x_in[k], 16 * i + 16)
                    sem_wait(pe, xl_done, t - 1)
                    for c in range(KC):
                        mm = pe.transpose(px[k][:, c], xs[:, k, c * P:(c + 1) * P], ident[:])
                    mm.then_inc(xt_done, 1)

                def up(i, k, e):
                    t = 2 * i + k
                    pe.wait_ge(xl_done, t + 1)
                    sem_wait(pe, g_done, IC * (t - 1))
                    for n in range(IC):
                        terms = [(w, x, c) for w, x in ((w1h, xh), (w1h, xl), (w1l, xh)) for c in range(KC)]
                        for m, (w, x, c) in enumerate(terms):
                            mm = pe.matmul(ph[k][:, n], w[:, ds(e, 1), c * FI + n * P:c * FI + (n + 1) * P].rearrange("p a n -> p (a n)"),
                                           x[:, k, c], start=m == 0, stop=m == len(terms) - 1)
                        if n % HC == HC - 1:
                            mm.then_inc(h_done, 1)

                def down(i, k, e):
                    t = 2 * i + k
                    pe.wait_ge(gl_done, t + 1)
                    sem_wait(pe, ys_done, t - 1)
                    terms = [(x, w, n) for n in range(IC) for x, w in ((gh, w2h), (gl, w2h), (gh, w2l))]
                    for m, (x, w, n) in enumerate(terms):
                        mm = pe.matmul(py[k][:], x[:, k, n], w[:, ds(e, 1), n * E:(n + 1) * E].rearrange("p a n -> p (a n)"),
                                       start=m == 0, stop=m == len(terms) - 1)
                    mm.then_inc(y_done, 1)

                def tiles(i):
                    e = [pe.value_load(owner[0:1, ds(2 * i + k, 1)], min_val=0, max_val=NE - 1) for k in range(2)]
                    for k in range(2):
                        turn(i, k)
                    for k in range(2):
                        up(i, k, e[k])
                    for k in range(2):
                        down(i, k, e[k])

                rounds(pe, T2, tiles)

            @block.scalar
            def _(act):
                act.wait_ge(b1_turned, 1)
                act.activation(b1[:], px[0][:, 0, 0:NE * IC], ACT.Copy).then_inc(b1_done, 1)
                act.wait_ge(b1_done, 1)

                def tiles(i):
                    e = [act.value_load(owner[0:1, ds(2 * i + k, 1)], min_val=0, max_val=NE - 1) for k in range(2)]
                    for k in range(2):
                        t = 2 * i + k
                        act.wait_ge(xt_done, t + 1)
                        sem_wait(act, h_done, 2 * (t - 1))
                        act.activation(xh[:, k], px[k][:], ACT.Copy).then_inc(xh_done, 1)
                    for k in range(2):
                        t = 2 * i + k
                        sem_wait(act, gl_done, t - 1)
                        for n in range(IC):
                            if n % HC == 0:
                                act.wait_ge(h_done, 2 * t + n // HC + 1)
                            act.activation(g[:, k, n], ph[k][:, n], ACT.Gelu, bias=b1[:, ds(e[k] * IC + n, 1)], scale=1.0 / WS)\
                               .then_inc(g_done, 1)

                rounds(act, T2, tiles)

            @block.vector
            def _(dve):
                def tiles(i):
                    e = [dve.value_load(owner[0:1, ds(2 * i + k, 1)], min_val=0, max_val=NE - 1) for k in range(2)]
                    for k in range(2):
                        t = 2 * i + k
                        dve.wait_ge(xh_done, t + 1)
                        dve.tensor_tensor(xl[:, k], px[k][:], xh[:, k], ALU.subtract).then_inc(xl_done, 1)
                    for k in range(2):
                        t = 2 * i + k
                        dve.wait_ge(g_done, IC * (t + 1))
                        sem_wait(dve, y_done, t - 1)
                        dve.tensor_copy(gh[:, k], g[:, k]).then_inc(gh_done, 1)
                        dve.wait_ge(gh_done, t + 1)
                        dve.tensor_tensor(gl[:, k], g[:, k], gh[:, k], ALU.subtract).then_inc(gl_done, 1)
                    for k in range(2):
                        t = 2 * i + k
                        dve.wait_ge(y_done, t + 1)
                        sem_wait(dve, stored[k], 16 * i)
                        dve.scalar_tensor_tensor(out=ys[:, k], in0=py[k][:], scalar=1.0 / WS,
                                                 in1=b2[:, ds(e[k], 1)].rearrange("p a n -> p (a n)"), op0=ALU.mult, op1=ALU.add)\
                           .then_inc(ys_done, 1)

                dve.wait_ge(b_in, 32)
                rounds(dve, T2, tiles)


def gather(nc, hbm, out, gate, slot):
    with ExitStack() as ctx:
        sb = lambda n, s, d=fp32: ctx.enter_context(nc.sbuf_tensor(n, s, d))
        sem = lambda n: ctx.enter_context(nc.semaphore(n))
        CH = 8
        y, x1 = sb("g_y", [P, NT, E]), sb("g_x1", [P, NT, E])
        y_in = [sem(f"g_y_in{i}") for i in range(NT // CH)]
        x_in, done, stored = sem("g_x_in"), sem("g_done"), sem("g_stored")
        out_h = out.rearrange("b (t p) e -> p (b t) e", p=P)

        with nc.Block() as block:

            @block.gpsimd
            def _(pool):
                for t in range(NT):
                    pool.indirect_dma_start(out=y[:, t], out_offset=None, in_=hbm["y"],
                                            in_offset=bass.IndirectOffsetOnAxis(ap=slot[:, t:t + 1], axis=0),
                                            bounds_check=SLOTS - 1, oob_is_err=True).then_inc(y_in[t // CH], 16)

            @block.vector
            def _(dve):
                dve.wait_ge(x_in, 16)
                for t in range(NT):
                    dve.wait_ge(y_in[t // CH], 16 * CH)
                    dve.scalar_tensor_tensor(out=x1[:, t], in0=y[:, t], scalar=gate[:, t:t + 1], in1=x1[:, t], op0=ALU.mult, op1=ALU.add)\
                       .then_inc(done, 1)

            @block.sync
            def _(sp):
                sp.dma_start(x1[:], hbm["x1"].rearrange("(t p) e -> p t e", p=P)).then_inc(x_in, 16)
                for c in range(NT // CH):
                    sp.wait_ge(done, CH * (c + 1))
                    sp.dma_start(out_h[:, c * CH:(c + 1) * CH], x1[:, c * CH:(c + 1) * CH]).then_inc(stored, 16)
                sp.wait_ge(stored, 16 * (NT // CH))


def build(nc, io, out):
    hbm = scratch(nc)
    project(nc, io, hbm)
    with ExitStack() as ctx:
        sb = lambda n, s, d=fp32: ctx.enter_context(nc.sbuf_tensor(n, s, d))
        logits = sb("logits", [P, B, ST, NE])
        gate, slot, owner = sb("gate", [P, NT]), sb("slot", [P, NT], u32), sb("owner", [P, SLOT_TILES + 1], i32)
        with ExitStack() as attention:
            ctxn = attention.enter_context(nc.sbuf_tensor("ctxn", [P, H, B, ST, D + 1], fp32, side="right"))
            far(nc, hbm, ctxn)
            near(nc, hbm, ctxn)
            w1 = [sb(f"w1{n}", [P, NE, 2 * FI], fp16) for n in "hl"]
            w2 = [sb(f"w2{n}", [P, NE, 2 * FI], fp16) for n in "hl"]
            combine(nc, io, hbm, ctxn, w1, w2, logits)
        route(nc, io, hbm, logits, gate, slot, owner)
        experts(nc, io, hbm, w1, w2, owner)
        gather(nc, hbm, out, gate, slot)


def kernel(**inputs):
    import numpy as np
    import concourse.bacc as bacc
    from concourse.bass_utils import run_bass_kernel_spmd

    nc = bacc.Bacc("TRN2", target_bir_lowering=False, num_devices=1)
    arrays, io = {}, {}
    for name, value in inputs.items():
        a = np.ascontiguousarray(value)
        arrays[f"in_{name}"] = a
        io[name] = nc.dram_tensor(f"in_{name}", a.shape, mybir.dt.from_np(a.dtype), kind="ExternalInput").ap()
    out = nc.dram_tensor("out", (B, S, E), fp32, kind="ExternalOutput").ap()
    build(nc, io, out)
    r = run_bass_kernel_spmd(nc, [arrays], core_ids=[0])
    return r.results[0]["out"]
```

```python
import concourse.bass as bass
from concourse import mybir
from contextlib import ExitStack

fp32 = mybir.dt.float32
bf16 = mybir.dt.bfloat16
fp16 = mybir.dt.float16
i32 = mybir.dt.int32
u32 = mybir.dt.uint32
ALU = mybir.AluOpType
ACT = mybir.ActivationFunctionType
AX = mybir.AxisListType
ds = bass.ds

P = 128
B, S, E = 2, 2048, 256
H, D = 16, 16
MAXREL = 128
NREL = 2 * MAXREL + 1
N = B * S
NT = N // P
ST = S // P
BH = B * H
NE, FI = 8, 1024
EPS = 1e-5

Q_PARTS = ("h", "h", "h", "m", "m", "l")
K_PARTS = ("m", "h", "l", "h", "m", "h")
PR = len(Q_PARTS) * D
R_MAX, R_LEFT, R_RIGHT = PR, PR + 2, PR + 5
QR = PR + 8
EXT = S // 4 - 1
VC = 32
EC = 4 * P
NC_ = N // EC


def places(parts, which):
    at = [r for r, w in enumerate(parts) if w == which]
    step = at[1] - at[0] if len(at) > 1 else 1
    assert at == list(range(at[0], at[-1] + 1, step))
    return slice(at[0], at[-1] + 1, step)


SLOT_TILES = NT + NE - 1
SLOTS = (SLOT_TILES + 1) * P


def sem_wait(eng, sem, value):
    if isinstance(value, int) and value <= 0:
        return
    eng.wait_ge(sem, value)


def wait_apart(eng, sem, value, tick):
    sem_wait(eng, sem, value)
    eng.sem_inc(tick, 1)


def rounds(eng, n, body):
    body(0)
    if n > 1:
        with eng.Fori(1, n) as i:
            body(i)


def project(nc, io, hbm):
    with ExitStack() as ctx:
        sb = lambda n, s, d=fp32: ctx.enter_context(nc.sbuf_tensor(n, s, d))
        sem = lambda n: ctx.enter_context(nc.semaphore(n))
        ident = sb("p_ident", [P, P])
        wq, wk, wv = (sb(f"p_w{n}", [P, 2, E]) for n in "qkv")
        bq, bk, bk4 = sb("p_bq", [P, 2]), sb("p_bk", [P, 2]), sb("p_bk4", [P, 2])
        bv = sb("p_bv", [P, E])
        eps = sb("p_eps", [P, 1])
        x = sb("p_x", [P, 2, 4, E])
        stats = sb("p_stats", [P, 2, 4, 6])
        mv = sb("p_mv", [P, 2, 4, 2])
        sd = sb("p_sd", [P, 2, 4])
        rs = sb("p_rs", [P, 2, 4])
        xn = sb("p_xn", [P, 2, 4, E])
        xt = sb("p_xt", [P, 2, 2, EC])
        full = {n: sb(f"p_{n}f", [P, 2, 2, EC]) for n in "qk"}
        rest = {n: sb(f"p_{n}r", [P, 2, EC]) for n in "qk"}
        part = {(n, w): sb(f"p_{n}{w}", [P, 2, 2, EC], bf16) for n in "qk" for w in "hml"}
        v = sb("p_v", [P, 2, H, 4, VC])
        relt = sb("p_relt", [D, NREL])
        rele = sb("p_rele", [D, EXT + 1])
        relz = sb("p_relz", [D, P])
        relr = sb("p_relr", [D, EXT + 1])
        relp = {w: sb(f"p_rel{w}", [D, EXT + 1], bf16) for w in "hml"}
        zeros = sb("p_zeros", [P, 8 * E])
        pt = ctx.enter_context(nc.psum_tensor("p_pt", [P, 2, EC], fp32))
        pq = ctx.enter_context(nc.psum_tensor("p_pq", [P, 2, EC], fp32))
        pk = ctx.enter_context(nc.psum_tensor("p_pk", [P, 2, EC], fp32))
        pv = ctx.enter_context(nc.psum_tensor("p_pv", [P, 4, E], fp32))

        weights_in, rel_in = sem("p_weights_in"), sem("p_rel_in")
        x_in = [sem(f"p_x_in{k}") for k in range(2)]
        ident_done, init_done = sem("p_ident_done"), sem("p_init_done")
        tick_v, tick_p = sem("p_tick_v"), sem("p_tick_p")
        zeros_done, zeros_stored = sem("p_zeros_done"), sem("p_zeros_stored")
        eps_done, bk4_done = sem("p_eps_done"), sem("p_bk4_done")
        stats_done, mv_done, sd_done, rs_done, xn_done = (sem(f"p_{n}") for n in ("stats_d", "mv_d", "sd_d", "rs_d", "xn_d"))
        turned, xt_done = sem("p_turned"), sem("p_xt_done")
        q_done, k_done, v_done = sem("p_q_done"), sem("p_k_done"), sem("p_v_done")
        qf_done, kf_done = sem("p_qf_done"), sem("p_kf_done")
        q_split, k_split, vb_done = sem("p_q_split"), sem("p_k_split"), sem("p_vb_done")
        stored = [sem(f"p_stored{k}") for k in range(2)]
        rel_done, rel_stored = sem("p_rel_done"), sem("p_rel_stored")

        x_h = io["L0_attn_q"].rearrange("b (c t p) e -> p (b c) t e", p=P, t=4)
        STORES = 2 * 3 * 2 + 1

        def chunk_pairs(eng, body):
            body(0, True)
            with eng.Fori(1, NC_ // 2 - 1) as i:
                body(i, True)
            body(NC_ // 2 - 1, False)

        with nc.Block() as block:

            @block.sync
            def _(sp):
                def load(k, c):
                    sp.dma_start(x[:, k], x_h[:, ds(c, 1)].rearrange("p c t e -> p (c t) e")).then_inc(x_in[k], 16)

                for k in range(2):
                    load(k, k)
                for w, name in ((wq, "Wq"), (wk, "Wk"), (wv, "Wv")):
                    sp.dma_start(w[:], io[f"L0_attn_{name}"].rearrange("(c p) n -> p c n", p=P)).then_inc(weights_in, 16)
                with nc.allow_non_contiguous_dma(reason="a bias to a column, once"):
                    for b_, name in ((bq, "bq"), (bk, "bk")):
                        sp.dma_start(b_[:], io[f"L0_attn_{name}"].rearrange("(c p) -> p c", p=P)).then_inc(weights_in, 16)
                sp.dma_start(bv[:], io["L0_attn_bv"].rearrange("(a n) -> a n", a=1).to_broadcast([P, E])).then_inc(weights_in, 16)

                def stores(i):
                    for k in range(2):
                        c = 2 * i + k
                        for n, split, rows in (("q", q_split, Q_PARTS), ("k", k_split, K_PARTS)):
                            for w, need in (("h", 1), ("m", 3), ("l", 4)):
                                sp.wait_ge(split, 4 * c + need)
                                at = places(rows, w)
                                copies = rows.count(w)
                                for m in range(2):
                                    to = hbm[n].rearrange("(m g) (d r) t -> m (g d) r t", m=2, r=len(rows))[m, :, at, ds(c * EC, EC)]
                                    sp.dma_start(to, part[n, w][:, k, m].rearrange("p (a t) -> p a t", a=1).to_broadcast([P, copies, EC]))\
                                        .then_inc(stored[k], 16)
                        sp.wait_ge(vb_done, 4 * c + 4)
                        sp.dma_start(hbm["v"].rearrange("h p t c -> p h t c")[:, :, ds(c * 4, 4)],
                                     v[:, k]).then_inc(stored[k], 16)

                def loads(i):
                    for k in range(2):
                        sp.wait_ge(xn_done, 8 * i + 4 * k + 4)
                        load(k, 2 * i + k + 2)

                loads(0)
                stores(0)
                with sp.Fori(1, NC_ // 2 - 1) as i:
                    loads(i)
                    stores(i)
                stores(NC_ // 2 - 1)
                for k in range(2):
                    sp.wait_ge(stored[k], 16 * STORES * (NC_ // 2))

            @block.gpsimd
            def _(pool):
                pool.memset(ident[:], 0.0).then_inc(ident_done, 1)
                pool.memset(v[:], 0.0).then_inc(init_done, 1)
                pool.wait_ge(init_done, 1)
                pool.memset(v[:, :, :, :, D:D + 1], 1.0).then_inc(init_done, 1)
                pool.wait_ge(ident_done, 1)
                pool.affine_select(out=ident[:], in_=ident[:], compare_op=ALU.not_equal, fill=1.0, base=0,
                                   pattern=[[-1, P]], channel_multiplier=1).then_inc(ident_done, 1)
                with nc.allow_non_contiguous_dma(reason="a small table turned, once"):
                    pool.dma_start(relt[:], io["L0_attn_rel_table"].rearrange("r d -> d r")).then_inc(rel_in, 16)
                pool.memset(zeros[:], 0.0).then_inc(zeros_done, 1)
                pool.wait_ge(zeros_done, 1)
                for t in range(0, SLOTS, 8 * P):
                    pool.dma_start(hbm["xs"][t:t + 8 * P].rearrange("(p t) e -> p (t e)", p=P), zeros[:]).then_inc(zeros_stored, 16)
                pool.wait_ge(init_done, 2)

                def split_keys(i):
                    for k in range(2):
                        c = 2 * i + k
                        f, r = full["k"][:, k], rest["k"]
                        h, m, l = (part["k", w][:, k] for w in "hml")
                        pool.wait_ge(kf_done, 2 * c + 2)
                        wait_apart(pool, stored[k], i * (16 * STORES), tick_p)
                        pool.tensor_copy(h, f).then_inc(k_split, 1)
                        pool.wait_ge(k_split, 4 * c + 1)
                        pool.tensor_tensor(r[:], f, h, ALU.subtract).then_inc(k_split, 1)
                        wait_apart(pool, k_split, 4 * c + 2, tick_p)
                        pool.tensor_copy(m, r[:]).then_inc(k_split, 1)
                        pool.wait_ge(k_split, 4 * c + 3)
                        pool.tensor_tensor(l, r[:], m, ALU.subtract).then_inc(k_split, 1)
                        pool.wait_ge(k_split, 4 * c + 4)

                rounds(pool, NC_ // 2, split_keys)
                pool.wait_ge(rel_done, 8)
                for r, w in enumerate(K_PARTS):
                    pool.dma_start(hbm["rel"].rearrange("(d r) c -> r d c", r=len(K_PARTS))[r], relp[w][:]).then_inc(rel_stored, 16)
                pool.wait_ge(rel_stored, 16 * len(K_PARTS))
                pool.wait_ge(zeros_stored, 16 * (SLOTS // (8 * P)))

            @block.scalar
            def _(act):
                act.wait_ge(weights_in, 96)
                act.activation(bk4[:], bk[:], ACT.Copy, scale=D ** -0.5).then_inc(bk4_done, 1)
                act.wait_ge(bk4_done, 1)
                act.wait_ge(eps_done, 1)

                def deviation(c, k):
                    act.wait_ge(mv_done, 4 * c + 4)
                    act.activation(sd[:, k], mv[:, k, :, 1], ACT.Sqrt, bias=eps[:]).then_inc(sd_done, 1)

                def turned_out(c, k):
                    act.wait_ge(turned, c + 1)
                    act.activation(xt[:, k], pt[:], ACT.Copy).then_inc(xt_done, 1)

                def chunk(i, more):
                    for k in range(2):
                        c = 2 * i + k
                        act.wait_ge(q_done, c + 1)
                        sem_wait(act, q_split, i * 8 + 4 * k - 4)
                        for m in range(2):
                            act.activation(full["q"][:, k, m], pq[:, m], ACT.Identity, bias=bq[:, m:m + 1]).then_inc(qf_done, 1)
                        act.wait_ge(k_done, c + 1)
                        sem_wait(act, k_split, i * 8 + 4 * k - 4)
                        for m in range(2):
                            act.activation(full["k"][:, k, m], pk[:, m], ACT.Identity, bias=bk4[:, m:m + 1],
                                           scale=D ** -0.5).then_inc(kf_done, 1)
                        if k == 0 or more:
                            turned_out(c + 1, 1 - k)
                        if more:
                            deviation(c + 2, k)

                for k in range(2):
                    deviation(k, k)
                turned_out(0, 0)
                chunk_pairs(act, chunk)

            @block.tensor
            def _(pe):
                pe.wait_ge(ident_done, 2)
                pe.wait_ge(weights_in, 96)

                def turn(c, k):
                    pe.wait_ge(xn_done, 4 * c + 4)
                    for t in range(4):
                        for e in range(2):
                            mm = pe.transpose(pt[:, e, t * P:(t + 1) * P], xn[:, k, t, e * P:(e + 1) * P], ident[:])
                    mm.then_inc(turned, 1)

                def chunk(i, more):
                    for k in range(2):
                        c = 2 * i + k
                        pe.wait_ge(xt_done, c + 1)
                        for w, out, done, free, per in ((wq, pq, q_done, qf_done, 2), (wk, pk, k_done, kf_done, 2)):
                            sem_wait(pe, free, per * c)
                            for m in range(2):
                                for e in range(2):
                                    mm = pe.matmul(out[:, m], w[:, e, m * P:(m + 1) * P], xt[:, k, e], start=e == 0, stop=e == 1)
                            mm.then_inc(done, 1)
                        if k == 0 or more:
                            turn(c + 1, 1 - k)
                        sem_wait(pe, vb_done, 4 * c)
                        for t in range(4):
                            for e in range(2):
                                mm = pe.matmul(pv[:, t], xt[:, k, e, t * P:(t + 1) * P], wv[:, e], start=e == 0, stop=e == 1)
                        mm.then_inc(v_done, 1)

                turn(0, 0)
                chunk_pairs(pe, chunk)

            @block.vector
            def _(dve):
                dve.memset(eps[:], EPS).then_inc(eps_done, 1)
                dve.memset(relz[:], 0.0).then_inc(rel_done, 1)

                def norm(k, c):
                    dve.wait_ge(x_in[k], 16 * (c // 2) + 16 if isinstance(c, int) else (c - k) * 8 + 16)
                    sem_wait(dve, turned, c - 1)
                    for t in range(4):
                        dve.bn_stats(stats[:, k, t], x[:, k, t]).then_inc(stats_done, 1)
                    wait_apart(dve, stats_done, 4 * c + 4, tick_v)
                    for t in range(4):
                        dve.bn_aggr(mv[:, k, t], stats[:, k, t]).then_inc(mv_done, 1)
                    dve.wait_ge(sd_done, c + 1)
                    dve.reciprocal(rs[:, k], sd[:, k]).then_inc(rs_done, 1)
                    dve.wait_ge(rs_done, c + 1)
                    for t in range(4):
                        dve.tensor_scalar(xn[:, k, t], x[:, k, t], mv[:, k, t, 0:1], rs[:, k, t:t + 1],
                                          ALU.subtract, ALU.mult).then_inc(xn_done, 1)

                def split(k, i):
                    c = 2 * i + k
                    f, r = full["q"][:, k], rest["q"]
                    h, m, l = (part["q", w][:, k] for w in "hml")
                    dve.wait_ge(qf_done, 2 * c + 2)
                    sem_wait(dve, stored[k], i * (16 * STORES))
                    dve.tensor_copy(h, f).then_inc(q_split, 1)
                    dve.wait_ge(q_split, 4 * c + 1)
                    dve.tensor_tensor(r[:], f, h, ALU.subtract).then_inc(q_split, 1)
                    dve.wait_ge(q_split, 4 * c + 2)
                    dve.tensor_copy(m, r[:]).then_inc(q_split, 1)
                    dve.wait_ge(q_split, 4 * c + 3)
                    dve.tensor_tensor(l, r[:], m, ALU.subtract).then_inc(q_split, 1)
                    dve.wait_ge(v_done, c + 1)
                    for t in range(4):
                        dve.tensor_tensor(v[:, k, :, t, 0:D], pv[:, t].rearrange("p (h d) -> p h d", d=D),
                                          bv[:].rearrange("p (h d) -> p h d", d=D), ALU.add).then_inc(vb_done, 1)
                    dve.wait_ge(q_split, 4 * c + 4)

                dve.wait_ge(rel_in, 16)
                dve.wait_ge(rel_done, 1)
                edge = MAXREL - 1
                dve.tensor_copy(rele[:, edge:edge + NREL], relt[:]).then_inc(rel_done, 1)
                dve.tensor_scalar(rele[:, 0:edge], relz[:, 0:edge], relt[:, 0:1], None, ALU.add).then_inc(rel_done, 1)
                dve.tensor_scalar(rele[:, edge + NREL:EXT + 1], relz[:, 0:EXT + 1 - edge - NREL],
                                  relt[:, NREL - 1:NREL], None, ALU.add).then_inc(rel_done, 1)
                dve.wait_ge(rel_done, 4)
                dve.tensor_copy(relp["h"][:], rele[:]).then_inc(rel_done, 1)
                dve.wait_ge(rel_done, 5)
                dve.tensor_tensor(relr[:], rele[:], relp["h"][:], ALU.subtract).then_inc(rel_done, 1)
                dve.wait_ge(rel_done, 6)
                dve.tensor_copy(relp["m"][:], relr[:]).then_inc(rel_done, 1)
                dve.wait_ge(rel_done, 7)
                dve.tensor_tensor(relp["l"][:], relr[:], relp["m"][:], ALU.subtract).then_inc(rel_done, 1)
                dve.wait_ge(weights_in, 96)
                dve.wait_ge(init_done, 2)

                def chunk(i, more):
                    for k in range(2):
                        split(k, i)
                        if more:
                            norm(k, 2 * i + k + 2)

                for k in range(2):
                    norm(k, k)
                chunk_pairs(dve, chunk)


def scratch(nc):
    def dram(name, shape, dt):
        return nc.dram_tensor(name, shape, dt, kind="Internal").ap()

    return {
        "q": dram("q_stack", [H, PR, N], bf16),
        "k": dram("k_stack", [H, PR, N], bf16),
        "terms": dram("q_terms", [H, QR - PR, N], bf16),
        "v": dram("v_blocks", [H, P, NT, VC], fp32),
        "rel": dram("rel_stack", [PR, EXT + 1], bf16),
        "x1": dram("x_attended", [N, E], fp32),
        "xn": dram("x_normal", [N, E], fp32),
        "xs": dram("x_slots", [SLOTS, E], fp32),
        "y": dram("y_slots", [SLOTS, E], fp32),
    }


def far(nc, hbm, ctxn):
    with ExitStack() as ctx:
        sb = lambda n, s, d=fp32: ctx.enter_context(nc.sbuf_tensor(n, s, d))
        sem = lambda n: ctx.enter_context(nc.semaphore(n))
        def row_units(j):
            tiles = [i for i in range(ST) if abs(i - j) > 1]
            n = len(tiles)
            cuts = [round(x * n / 4) for x in range(5)]
            return [tiles[a:b] for a, b in zip(cuts, cuts[1:])]

        def runs(tiles, brk):
            out = []
            for at, i in enumerate(tiles):
                if out and out[-1][0] + out[-1][1] == i and not brk(i):
                    out[-1] = (out[-1][0], out[-1][1] + 1, out[-1][2])
                else:
                    out.append((i, 1, at))
            return out

        ROWT = ST - 2
        NU = 4 * ST
        ident = sb("f_ident", [P, P])
        rel = sb("f_rel", [PR, EXT + 1], bf16)
        q = sb("f_q", [QR, B, S], bf16)
        kl = sb("f_kl", [QR, B, S], bf16)
        kr = sb("f_kr", [QR, B, S], bf16)
        v = sb("f_v", [P, B, ST, VC])
        mq, mk = sb("f_mq", [PR, B, S], bf16), sb("f_mk", [PR, B, S], bf16)
        pb = [sb(f"f_p{i}", [P, ROWT * P]) for i in range(2)]
        os = sb("f_os", [P, 4, P])
        top, top_all, top_rel = sb("f_top", [P, B, 4, ST]), sb("f_top_all", [P, B, ST]), sb("f_top_rel", [P, B, ST])
        terms = sb("f_terms", [P, B, 3, ST])
        GR = 3 * ST
        rest = sb("f_rest", [GR, P])
        part = {w: sb(f"f_t{w}", [GR, B, P], bf16) for w in "hml"}
        sc = [ctx.enter_context(nc.psum_tensor(f"f_sc{i}", [P, 4 * P], fp32)) for i in range(2)]
        m = [ctx.enter_context(nc.psum_tensor(f"f_m{i}", [P, 512], fp32)) for i in range(4)]
        o = ctx.enter_context(nc.psum_tensor("f_o", [P, 4, P], fp32))
        ot = ctx.enter_context(nc.psum_tensor("f_ot", [P, 4, P], fp32))
        ident_done, ones_done, rel_in = sem("f_ident_done"), sem("f_ones_done"), sem("f_rel_in")
        stacks_in, guards_in, m_in, stored = ([sem(f"f_{n}{k}") for k in range(B)] for n in ("in", "guards_in", "m_in", "stored"))
        scored, exps, summed, os_done, turned, ctx_done = (sem(f"f_{n}") for n in ("scored", "exps", "summed", "os_d", "turned", "ctx_d"))
        tick_pe, tick_sp = sem("f_tick_pe"), sem("f_tick_sp")
        to_take, taken, guard_done, guard_turned, split = (
            sem(f"f_{n}") for n in ("to_take", "taken", "guard_d", "guard_turned", "split_d"))

        steps = [st for j in range(ST) for st in [("keys", j, x) for x in range(4)] + [("rel", j, 0)]]
        step_of = {st: i for i, st in enumerate(steps)}
        STEPS = len(steps)
        RING = 4
        reads_before = lambda i: i + sum(kind == "rel" for kind, *_ in steps[:i])
        READS = reads_before(STEPS)

        def heads(body):
            def passes(eng):
                body(None, 0, 0, None)
                body(None, 1, 1, 0)
                for k in range(B):
                    body(k, k, k + 2, k + 1)
                with eng.Fori(1, H - 1) as h:
                    for k in range(B):
                        body(2 * h + k, k, 2 * h + k + 2, 2 * h + k + 1)
                body(BH - 2, 0, None, BH - 1)
                body(BH - 1, 1, None, None)
            return passes

        def rounds_of(pair, k):
            return pair // 2 + 1 if isinstance(pair, int) else (pair - k) // 2 + 1

        with nc.Block() as block:

            @block.sync
            def _(sp):
                flat = lambda ap: ap.rearrange("r h t -> r (h t)")
                at = lambda n, rows, h, k: flat(hbm[n].rearrange("h r t -> r h t")[rows, ds(h, 1), k * S:(k + 1) * S])

                def load_m(h, k):
                    sp.dma_start(mq[:, k], at("q", slice(0, PR), h, k)).then_inc(m_in[k], 16)
                    sp.dma_start(mk[:, k], at("k", slice(0, PR), h, k)).then_inc(m_in[k], 16)

                def load_far(h, k):
                    sp.dma_start(kl[0:PR, k], at("k", slice(0, PR), h, k)).then_inc(stacks_in[k], 16)
                    sp.dma_start(kr[0:PR, k], at("k", slice(0, PR), h, k)).then_inc(stacks_in[k], 16)
                    sp.dma_start(q[0:PR, k], at("q", slice(0, PR), h, k)).then_inc(stacks_in[k], 16)
                    sp.dma_start(v[:, k], hbm["v"].rearrange("h p t c -> p h t c")[:, ds(h, 1), k * ST:(k + 1) * ST]
                                 .rearrange("p h t c -> p (h t) c")).then_inc(stacks_in[k], 16)

                def guards(h, k, pair):
                    wait_apart(sp, split, 4 * pair + 4, tick_sp)
                    for a, row, parts in ((0, R_LEFT, "hml"), (1, R_MAX, "hm"), (2, R_RIGHT, "hml")):
                        for y, w in enumerate(parts):
                            to = hbm["terms"][ds(h, 1), row - PR + y, k * S:(k + 1) * S].rearrange("h (t x) -> (h t) x", x=P)
                            sp.dma_start(to, part[w][a * ST:(a + 1) * ST, k]).then_inc(stored[k], 16)
                    wait_apart(sp, stored[k], 16 * GUARD_DMAS * (h + 1), tick_sp)
                    sp.dma_start(q[PR:QR, k], at("terms", slice(0, QR - PR), h, k)).then_inc(guards_in[k], 16)

                GUARD_DMAS = 8
                sp.dma_start(rel[:], hbm["rel"]).then_inc(rel_in, 16)
                load_m(0, 0)
                load_m(0, 1)
                load_far(0, 0)
                sp.wait_ge(to_take, STEPS)
                load_m(1, 0)
                guards(0, 0, 0)

                def during(h, k, m_next=True, far_next=True):
                    n = 2 * h + k
                    nk, nh = 1 - k, h + k
                    if m_next:
                        wait_apart(sp, to_take, STEPS * (n + 2), tick_sp)
                        load_m(nh + 1, nk)
                    if far_next:
                        wait_apart(sp, summed, ST * n, tick_sp)
                        load_far(nh, nk)
                        guards(nh, nk, n + 1)

                for k in range(B):
                    during(0, k)
                with sp.Fori(1, H - 2) as h:
                    for k in range(B):
                        during(h, k)
                during(H - 2, 0)
                during(H - 2, 1, m_next=False)
                during(H - 1, 0, m_next=False)
                for k in range(B):
                    sp.wait_ge(guards_in[k], 16 * H)

            @block.gpsimd
            def _(pool):
                make_ident(pool, ident, ident_done)
                pool.wait_ge(ident_done, 2)
                pool.memset(kl[PR:QR], 0.0).then_inc(ones_done, 1)
                pool.wait_ge(ones_done, 1)
                pool.memset(kr[PR:QR], 1.0).then_inc(ones_done, 1)
                pool.wait_ge(ones_done, 2)
                pool.memset(kl[PR:R_RIGHT], 1.0).then_inc(ones_done, 1)
                pool.wait_ge(ones_done, 3)
                pool.memset(kr[PR:R_RIGHT], 0.0).then_inc(ones_done, 1)
                pool.wait_ge(ones_done, 4)
                pool.memset(kr[PR:R_LEFT], 1.0).then_inc(ones_done, 1)

            @block.tensor
            def _(pe):
                pe.wait_ge(ident_done, 2)
                pe.wait_ge(rel_in, 16)

                def scores(n, k, j, x):
                    u = 4 * j + x
                    sem_wait(pe, exps, NU * n + u - 1)
                    for i, w, place in runs(row_units(j)[x], lambda i: False):
                        side = kl if j < i else kr
                        mm = pe.matmul(sc[u % 2][:, place * P:(place + w) * P], side[:, k, j * P:(j + 1) * P],
                                       q[:, k, i * P:(i + w) * P], start=True, stop=True)
                    mm.then_inc(scored, 1)

                def products(n, k, j):
                    pe.wait_ge(exps, NU * n + 4 * j + 4)
                    if j == 0:
                        sem_wait(pe, os_done, n)
                    for i, w, place in runs([i for i in range(ST) if abs(i - j) > 1], lambda i: i % 4 == 0):
                        g, c = i // 4, i % 4
                        mm = pe.matmul(o[32 * g:32 * g + 32, c:c + w], v[:, k, j], pb[j % 2][:, place * P:(place + w) * P],
                                       start=j == 0, stop=True, skip_group_check=True)
                    mm.then_inc(summed, 1)

                def turn(n):
                    pe.wait_ge(os_done, n + 1)
                    if not isinstance(n, int) or n < BH - 1:
                        sem_wait(pe, split, 4 * (n + 1) + 2)
                    sem_wait(pe, ctx_done, n)
                    for c in range(4):
                        mm = pe.transpose(ot[:, c], os[:, c], ident[:])
                    mm.then_inc(turned, 1)

                def turn_guards(g, k, n):
                    if n is not None:
                        sem_wait(pe, ctx_done, n)
                    wait_apart(pe, guard_done, 2 * g + 2, tick_pe)
                    pe.transpose(ot[0:GR, 0], terms[:, k].rearrange("p a t -> p (a t)"), ident[:])\
                        .then_inc(guard_turned, 1)

                def step(g, k, st):
                    i = step_of[st]
                    kind, t, quarter = st
                    sem_wait(pe, taken, READS * (g - 1) + reads_before(i - RING + 1 + STEPS) if i < RING else READS * g + reads_before(i - RING + 1))
                    if kind == "keys":
                        mm = pe.matmul(m[i % RING][:], mq[:, k, t * P:(t + 1) * P], mk[:, k, quarter * 512:(quarter + 1) * 512], start=True, stop=True)
                    else:
                        mm = pe.matmul(m[i % RING][:, 0:NREL], mq[:, k, t * P:(t + 1) * P],
                                       rel[:, MAXREL - 1:MAXREL - 1 + NREL], start=True, stop=True)
                    mm.then_inc(to_take, 1)

                def body(n, k, g, gs):
                    if isinstance(n, int) and n == 0:
                        pe.wait_ge(ones_done, 5)
                    if n is not None:
                        pe.wait_ge(stacks_in[k], 64 * rounds_of(n, k))
                        pe.wait_ge(guards_in[k], 16 * rounds_of(n, k))
                    if g is not None:
                        pe.wait_ge(m_in[k], 32 * rounds_of(g, k))
                    for j in range(ST):
                        def keys_steps(*quarters):
                            if g is not None:
                                for x in quarters:
                                    step(g, k, ("keys", j, x))

                        if n is not None:
                            scores(n, k, j, 0)
                            if j == 1 and not (isinstance(n, int) and n == 0):
                                turn(n - 1)
                            if j == 4 and gs is not None:
                                turn_guards(gs, 1 - k, n)
                        elif j == 4 and gs is not None:
                            turn_guards(gs, 1 - k, n)
                        keys_steps(0, 1)
                        if n is not None:
                            scores(n, k, j, 1)
                            if j:
                                products(n, k, j - 1)
                            elif not (isinstance(n, int) and n == 0):
                                products(n - 1, 1 - k, ST - 1)
                            scores(n, k, j, 2)
                        keys_steps(2, 3)
                        if n is not None:
                            scores(n, k, j, 3)
                        if g is not None:
                            step(g, k, ("rel", j, 0))

                heads(body)(pe)
                products(BH - 1, 1, ST - 1)
                turn(BH - 1)

            @block.scalar
            def _(act):
                def copy_sums(n):
                    act.wait_ge(summed, ST * n + ST)
                    sem_wait(act, turned, n)
                    act.activation(os[:], o[:], ACT.Copy).then_inc(os_done, 1)

                def body(n, k, g, gs):
                    for j in range(ST):
                        if n is not None:
                            sem_wait(act, summed, ST * n + j - 1)
                        at = 0
                        for x in range(4):
                            if n is not None:
                                u = 4 * j + x
                                w = len(row_units(j)[x]) * P
                                act.wait_ge(scored, NU * n + u + 1)
                                act.activation(pb[j % 2][:, at:at + w], sc[u % 2][:, 0:w], ACT.Exp).then_inc(exps, 1)
                                at += w
                        if j == 0 and n is not None and not (isinstance(n, int) and n == 0):
                            copy_sums(n - 1)

                heads(body)(act)
                copy_sums(BH - 1)

            @block.vector
            def _(dve):
                def step(g, k, st):
                    i = step_of[st]
                    kind, t, quarter = st
                    dve.wait_ge(to_take, STEPS * g + i + 1)
                    if kind == "keys":
                        dve.tensor_reduce(top[:, k, quarter, t:t + 1], m[i % RING][:], AX.X, ALU.max).then_inc(taken, 1)
                    else:
                        dve.tensor_reduce(top_rel[:, k, t:t + 1], m[i % RING][:, 0:NREL], AX.X, ALU.max).then_inc(taken, 1)
                        dve.tensor_copy(terms[:, k, 0:3:2, t], m[i % RING][:, 0:NREL:NREL - 1]).then_inc(taken, 1)

                def guard(g, k, stage):
                    if stage == 0:
                        dve.wait_ge(taken, READS * g + READS)
                        dve.tensor_reduce(top_all[:, k], top[:, k].rearrange("p q t -> p t q"), AX.X, ALU.max).then_inc(guard_done, 1)
                    else:
                        dve.wait_ge(guard_done, 2 * g + 1)
                        dve.scalar_tensor_tensor(out=terms[:, k, 1], in0=top_all[:, k], scalar=-1.0, in1=top_rel[:, k],
                                                 op0=ALU.mult, op1=ALU.subtract).then_inc(guard_done, 1)

                def split_guard(g, k, stage):
                    h, mid, low = (part[w][:, k] for w in "hml")
                    if stage == 0:
                        dve.wait_ge(guard_turned, g + 1)
                        sem_wait(dve, stored[k], 128 * (rounds_of(g, k) - 1))
                        dve.tensor_copy(h, ot[0:GR, 0]).then_inc(split, 1)
                        return
                    dve.wait_ge(split, 4 * g + stage)
                    if stage == 1:
                        dve.tensor_tensor(rest[:], ot[0:GR, 0], h, ALU.subtract).then_inc(split, 1)
                    elif stage == 2:
                        dve.tensor_copy(mid, rest[:]).then_inc(split, 1)
                    else:
                        dve.tensor_tensor(low, rest[:], mid, ALU.subtract).then_inc(split, 1)

                def sums(h, k, n):
                    dve.wait_ge(turned, n + 1)
                    c = ctxn[:, ds(h, 1), k].rearrange("p h (g c) x -> p (h g) c x", c=4)
                    dve.tensor_copy(c, ot[:].rearrange("p c (g x) -> p g c x", g=4)[:, :, :, 0:D + 1]).then_inc(ctx_done, 1)

                def body(n, k, g, gs):
                    if g is not None:
                        sem_wait(dve, guard_turned, g - 1)
                    for j in range(ST):
                        if g is not None:
                            for x in range(4):
                                step(g, k, ("keys", j, x))
                                if x == 1 and j == 0 and gs is not None:
                                    guard(gs, 1 - k, 0)
                            step(g, k, ("rel", j, 0))
                        elif j == 0 and gs is not None:
                            guard(gs, 1 - k, 0)
                        if j == 0 and gs is not None:
                            guard(gs, 1 - k, 1)
                        if j == 2 and n is not None and not (isinstance(n, int) and n == 0):
                            prev = (n - 1) // 2 if isinstance(n, int) else ((n - k) // 2 if k else (n - 2) // 2)
                            sums(prev, 1 - k, n - 1)
                        if gs is not None and 5 <= j <= 8:
                            split_guard(gs, 1 - k, j - 5)

                heads(body)(dve)
                sums(H - 1, 1, BH - 1)
                dve.wait_ge(ctx_done, BH)


def near(nc, hbm, ctxn):
    with ExitStack() as ctx:
        sb = lambda n, s, d=fp32: ctx.enter_context(nc.sbuf_tensor(n, s, d))
        sem = lambda n: ctx.enter_context(nc.semaphore(n))
        ident = sb("n_ident", [P, P])
        rel = sb("n_rel", [PR, EXT + 1], bf16)
        kw = [sb(f"n_k{i}", [QR, H, B, 3 * P], bf16) for i in range(2)]
        qw = [sb(f"n_q{i}", [QR, H, B, P], bf16) for i in range(2)]
        vw = [sb(f"n_v{i}", [P, H, B, 3, VC]) for i in range(2)]
        HALF = P // 2
        HB, QB = BH // 2, HALF // 2
        pb = [sb(f"n_p{i}", [P, 2, 2, 2, HB, QB]) for i in range(2)]
        G = BH // 4
        os = sb("n_os", [P, G, P])
        sc = ctx.enter_context(nc.psum_tensor("n_sc", [P, 2, 2, HB, QB], fp32))
        o = ctx.enter_context(nc.psum_tensor("n_o", [P, G, P], fp32))
        ot = ctx.enter_context(nc.psum_tensor("n_ot", [P, G, P], fp32))
        ident_done, rel_in = sem("n_ident_done"), sem("n_rel_in")
        tile_in = [sem(f"n_tile_in{i}") for i in range(2)]
        scored, exps, summed, os_done, turned, ctx_done = (sem(f"n_{n}") for n in ("scored", "exps", "summed", "os_d", "turned", "ctx_d"))
        ones_done = [sem(f"n_ones_done{i}") for i in range(2)]
        DMAS = 8
        SLOTS_OF = lambda edge: (1, 2) if edge == 0 else (0, 1) if edge == 1 else (0, 1, 2)
        first_step = lambda I: 0 if isinstance(I, int) and I == 0 else 3 * I - 1
        first_pb = lambda buf, edge: 1 if edge is None and buf == 0 else 0

        def tiles(eng, body):
            body(0, 0, 0)
            with eng.Fori(0, ST // 2 - 1) as i:
                for j in range(2):
                    body(2 * i + 1 + j, (1 + j) % 2, None)
            body(ST - 1, 1, 1)

        def keys_ones(eng, buf):
            eng.memset(kw[buf][PR:QR], 0.0).then_inc(ones_done[buf], 1)
            eng.wait_ge(ones_done[buf], 1)
            eng.memset(kw[buf][PR:R_LEFT], 1.0).then_inc(ones_done[buf], 1)

        with nc.Block() as block:

            @block.sync
            def _(sp):
                def load(I, buf, edge):
                    lo = 1 if edge == 0 else 0
                    w = 2 if edge in (0, 1) else 3
                    t0 = I - 1 + lo
                    for b in range(B):
                        sp.dma_start(kw[buf][0:PR, :, b, lo * P:(lo + w) * P],
                                     hbm["k"].rearrange("h r t -> r h t")[:, :, ds(t0 * P + b * S, w * P)]).then_inc(tile_in[buf], 16)
                        sp.dma_start(qw[buf][0:PR, :, b],
                                     hbm["q"].rearrange("h r t -> r h t")[:, :, ds(I * P + b * S, P)]).then_inc(tile_in[buf], 16)
                        sp.dma_start(qw[buf][PR:QR, :, b],
                                     hbm["terms"].rearrange("h r t -> r h t")[:, :, ds(I * P + b * S, P)]).then_inc(tile_in[buf], 16)
                        sp.dma_start(vw[buf][:, :, b, lo:lo + w],
                                     hbm["v"].rearrange("h p t c -> p h t c")[:, :, ds(t0 + b * ST, w)]).then_inc(tile_in[buf], 16)

                sp.dma_start(rel[:], hbm["rel"]).then_inc(rel_in, 16)
                load(0, 0, 0)
                load(1, 1, None)

                def next_load(I, buf, edge):
                    sp.wait_ge(summed, first_step(I - 1))
                    load(I, buf, edge)

                with sp.Fori(0, ST // 2 - 2) as i:
                    for j in range(2):
                        next_load(2 * i + 2 + j, j, None)
                next_load(ST - 2, 0, None)
                next_load(ST - 1, 1, 1)

            @block.gpsimd
            def _(pool):
                pool.memset(ident[:], 0.0).then_inc(ident_done, 1)
                pool.wait_ge(ident_done, 1)
                pool.affine_select(out=ident[:], in_=ident[:], compare_op=ALU.not_equal, fill=1.0, base=0,
                                   pattern=[[-1, P]], channel_multiplier=1).then_inc(ident_done, 1)
                pool.wait_ge(ident_done, 2)
                keys_ones(pool, 1)

            @block.tensor
            def _(pe):
                pe.wait_ge(ident_done, 2)
                pe.wait_ge(rel_in, 16)

                def scores(buf, s, slot, u):
                    kb, qb = kw[buf], qw[buf]
                    for half in range(2):
                        sem_wait(pe, exps, 2 * u - 1 + half)
                        hs = slice(half * H // 2, (half + 1) * H // 2)
                        for x in range(HB):
                            h, b = (half * HB + x) // B, x % B
                            for y in range(2):
                                i0 = s * HALF + y * QB
                                pe.matmul(sc[:, half, y, x], kb[:, h, b, slot * P:(slot + 1) * P], qb[:, h, b, i0:i0 + QB],
                                          start=x == 0, stop=False, skip_group_check=True)
                        for i in range(HALF):
                            col = (slot - 1) * P - (s * HALF + i) + 2 * MAXREL - 1
                            mm = pe.matmul(sc[:, half, i // QB, :, i % QB], rel[:, col:col + P],
                                           qb[0:PR, hs, :, s * HALF + i].rearrange("r h b -> r (h b)"),
                                           start=False, stop=True, skip_group_check=True)
                        mm.then_inc(scored, 1)

                def products(I, buf, slot, n, which, step):
                    pe.wait_ge(exps, 4 * step + 4)
                    if n == 0:
                        sem_wait(pe, os_done, I)
                    for g in range(G):
                        for x in range(4):
                            bh = 4 * g + x
                            mm = pe.matmul(o[32 * x:32 * x + 32, g], vw[buf][:, bh // B, bh % B, slot],
                                           pb[which][:, bh // HB, :, :, bh % HB, :].rearrange("p s y q -> p (s y) q"),
                                           start=(n == 0 and g % 4 == 0), stop=True, skip_group_check=True)
                    mm.then_inc(summed, 1)

                def turn(I):
                    sem_wait(pe, os_done, I + 1)
                    sem_wait(pe, ctx_done, I)
                    for g in range(G):
                        mm = pe.transpose(ot[:, g], os[:, g], ident[:])
                    mm.then_inc(turned, 1)

                def tile(I, buf, edge):
                    if isinstance(I, int) or buf == 1:
                        pe.wait_ge(ones_done[buf], 2)
                    pe.wait_ge(tile_in[buf], 16 * DMAS if isinstance(I, int) and I < 2 else (I - buf) * (8 * DMAS) + 16 * DMAS)
                    slots, step, p0 = SLOTS_OF(edge), first_step(I), first_pb(buf, edge)
                    for n, slot in enumerate(slots):
                        scores(buf, 0, slot, 2 * (step + n))
                        if n:
                            products(I, buf, slots[n - 1], n - 1, (p0 + n - 1) % 2, step + n - 1)
                        elif edge != 0:
                            products(I - 1, 1 - buf, 2, 2, (p0 + 1) % 2, step - 1)
                        if n == 1 and edge != 0:
                            turn(I - 1)
                        scores(buf, 1, slot, 2 * (step + n) + 1)

                tiles(pe, tile)

                products(ST - 1, 1, SLOTS_OF(1)[-1], 1, (first_pb(1, 1) + 1) % 2, first_step(ST - 1) + 1)
                turn(ST - 1)

            @block.scalar
            def _(act):
                def tile(I, buf, edge):
                    p0 = first_pb(buf, edge)
                    for n in range(len(SLOTS_OF(edge))):
                        step = first_step(I) + n
                        sem_wait(act, summed, step - 1)
                        for s in range(2):
                            for half in range(2):
                                act.wait_ge(scored, 4 * step + 2 * s + half + 1)
                                act.activation(pb[(p0 + n) % 2][:, half, s], sc[:, half], ACT.Exp).then_inc(exps, 1)

                tiles(act, tile)

            @block.vector
            def _(dve):
                keys_ones(dve, 0)

                def tile(I, buf, edge):
                    dve.wait_ge(summed, first_step(I) + len(SLOTS_OF(edge)))
                    sem_wait(dve, turned, I)
                    dve.tensor_copy(os[:], o[:]).then_inc(os_done, 1)
                    dve.wait_ge(turned, I + 1)
                    c = ctxn[:, :, :, ds(I, 1), :].rearrange("p h b t c -> p (h b t) c")
                    dve.tensor_tensor(c, ot[:].rearrange("p g (x c) -> p (g x) c", c=VC)[:, :, 0:D + 1], c, ALU.add).then_inc(ctx_done, 1)

                tiles(dve, tile)
                dve.wait_ge(ctx_done, ST)


WS = 64.0


def make_ident(pool, ident, done):
    pool.memset(ident[:], 0.0).then_inc(done, 1)
    pool.wait_ge(done, 1)
    pool.affine_select(out=ident[:], in_=ident[:], compare_op=ALU.not_equal, fill=1.0, base=0,
                       pattern=[[-1, P]], channel_multiplier=1).then_inc(done, 1)


def combine(nc, io, hbm, ctxn, w1, w2, logits):
    with ExitStack() as ctx:
        sb = lambda n, s, d=fp32: ctx.enter_context(nc.sbuf_tensor(n, s, d))
        sem = lambda n: ctx.enter_context(nc.semaphore(n))
        ident = sb("c_ident", [P, P])
        wo, wr = sb("c_wo", [P, 2, E]), sb("c_wr", [P, 2, NE])
        bo, br, eps = sb("c_bo", [P, E]), sb("c_br", [P, NE]), sb("c_eps", [P, 1])
        raw = [sb(f"c_raw{i}", [P, 2 * FI]) for i in range(2)]
        x = sb("c_x", [P, B, E])
        xb = sb("c_xb", [P, B, E])
        rden = sb("c_rden", [P, B, H])
        c = sb("c_c", [P, B, E])
        ct = sb("c_ct", [P, B, 2, P])
        x1 = sb("c_x1", [P, B, E])
        stats, mv, sd, rs = sb("c_stats", [P, B, 6]), sb("c_mv", [P, B, 2]), sb("c_sd", [P, B]), sb("c_rs", [P, B])
        xn = sb("c_xn", [P, B, E])
        xnt = sb("c_xnt", [P, B, 2, P])
        ps = lambda n, s: ctx.enter_context(nc.psum_tensor(n, s, fp32))
        pc = [ps(f"c_pc{b}", [P, 2, P]) for b in range(B)]
        po = [ps(f"c_po{b}", [P, E]) for b in range(B)]
        pn = [ps(f"c_pn{b}", [P, 2, P]) for b in range(B)]
        pl = [ps(f"c_pl{b}", [P, NE]) for b in range(B)]
        ident_done, consts_in, eps_done = sem("c_ident_done"), sem("c_consts_in"), sem("c_eps_done")
        raw_in, hi_done, lo_done = [sem(f"c_raw_in{i}") for i in range(2)], sem("c_hi_done"), sem("c_lo_done")
        x_in, stored = [sem(f"c_x_in{b}") for b in range(B)], [sem(f"c_stored{b}") for b in range(B)]
        names = ("xb", "rden", "c", "ctp", "ct", "o", "x1", "stats", "mv", "sd", "rs", "xn", "xnp", "xnt", "lp", "l", "tick")
        done = {n: sem(f"c_{n}_done") for n in names}
        tick_sp = sem("c_tick_sp")
        count = lambda i, b: B * i + b + 1

        def stages(tile, weights=None, load=None):
            def passes(eng):
                def both(e, first=False):
                    if load and not first:
                        load(e)
                    for k in range(2):
                        i = 2 * e + k
                        tile(i, True, not isinstance(i, int) or i >= 1, not isinstance(i, int) or i >= 2)
                        if weights:
                            weights(e, k)
                both(0, True)
                both(1)
                with eng.Fori(2, NE) as e:
                    both(e)
                tile(ST, False, True, True)
                tile(ST + 1, False, False, True)
            return passes

        x_h = io["L0_attn_q"].rearrange("b (t p) e -> p b t e", p=P)

        with nc.Block() as block:

            @block.sync
            def _(sp):
                sp.dma_start(wo[:], io["L0_attn_Wo"].rearrange("(c p) n -> p c n", p=P)).then_inc(consts_in, 16)
                sp.dma_start(wr[:], io["L0_ffn_wr"].rearrange("(c p) n -> p c n", p=P)).then_inc(consts_in, 16)
                sp.dma_start(bo[:], io["L0_attn_bo"].rearrange("(a n) -> a n", a=1).to_broadcast([P, E])).then_inc(consts_in, 16)
                sp.dma_start(br[:], io["L0_ffn_br"].rearrange("(a n) -> a n", a=1).to_broadcast([P, NE])).then_inc(consts_in, 16)

                def load(i):
                    for b in range(B):
                        if not isinstance(i, int):
                            wait_apart(sp, done["xb"], count(i - 1, b), tick_sp)
                        sp.dma_start(x[:, b], x_h[:, b, ds(i, 1)].rearrange("p t e -> p (t e)")).then_inc(x_in[b], 16)

                def stores(i):
                    for b in range(B):
                        sp.wait_ge(done["x1"], count(i, b))
                        sp.dma_start(hbm["x1"].rearrange("(b t p) e -> p b t e", p=P, b=B)[:, b, ds(i, 1)].rearrange("p t e -> p (t e)"),
                                     x1[:, b]).then_inc(stored[b], 16)
                        sp.wait_ge(done["xn"], count(i, b))
                        sp.dma_start(hbm["xn"].rearrange("(b t p) e -> p b t e", p=P, b=B)[:, b, ds(i, 1)].rearrange("p t e -> p (t e)"),
                                     xn[:, b]).then_inc(stored[b], 16)

                load(0)
                with sp.Fori(0, ST - 1) as i:
                    load(i + 1)
                    stores(i)
                stores(ST - 1)
                for b in range(B):
                    sp.wait_ge(stored[b], 32 * ST)

            @block.gpsimd
            def _(pool):
                make_ident(pool, ident, ident_done)
                pool.wait_ge(ident_done, 2)

                pool.wait_ge(consts_in, 64)

                def tile(i):
                    for b in range(B):
                        pool.wait_ge(x_in[b], 16 * i + 16)
                        sem_wait(pool, done["x1"], B * i + b - 1 if not isinstance(i, int) else 0)
                        pool.tensor_tensor(xb[:, b], x[:, b], bo[:], ALU.add).then_inc(done["xb"], 1)

                rounds(pool, ST, tile)

            @block.scalar
            def _(act):
                act.wait_ge(eps_done, 1)

                def load(e, k):
                    act.dma_start(raw[0][:].rearrange("p (c n) -> p c n", c=2) if k == 0 else raw[1][:].rearrange("p (c n) -> p c n", c=8),
                                  io["L0_ffn_w1" if k == 0 else "L0_ffn_w2"][ds(e, 1)].rearrange("a (c p) n -> p (a c) n", p=P))\
                       .then_inc(raw_in[k], 16)

                act.wait_ge(consts_in, 64)
                for k in range(2):
                    load(0, k)

                def tile(i, stage_a, stage_b, stage_c):
                    for b in range(B) if stage_c else ():
                        act.wait_ge(done["xnp"], count(i - 2, b))
                        sem_wait(act, done["lp"], count(i - 3, b))
                        act.activation(xnt[:, b], pn[b][:], ACT.Copy).then_inc(done["xnt"], 1)
                    for b in range(B) if stage_a else ():
                        act.wait_ge(done["ctp"], count(i, b))
                        sem_wait(act, done["o"], count(i - 1, b))
                        act.activation(ct[:, b], pc[b][:], ACT.Copy).then_inc(done["ct"], 1)
                    for b in range(B) if stage_b else ():
                        act.wait_ge(done["mv"], count(i - 1, b))
                        sem_wait(act, done["rs"], count(i - 2, b))
                        act.activation(sd[:, b:b + 1], mv[:, b, 1:2], ACT.Sqrt, bias=eps[:]).then_inc(done["sd"], 1)

                def weights(e, k):
                    act.wait_ge(raw_in[k], 16 * e + 16)
                    w = (w1, w2)[k][0]
                    act.activation(w[:, ds(e, 1)].rearrange("p a n -> p (a n)"), raw[k][:], ACT.Copy, scale=WS).then_inc(hi_done, 1)

                def next_load(e):
                    for k in range(2):
                        act.wait_ge(lo_done, 2 * e - 1 + k)
                        load(e, k)

                stages(tile, weights, next_load)(act)

            @block.tensor
            def _(pe):
                pe.wait_ge(ident_done, 2)
                pe.wait_ge(consts_in, 64)

                def tile(i, stage_a, stage_b, stage_c):
                    for b in range(B) if stage_b else ():
                        pe.wait_ge(done["ct"], count(i - 1, b))
                        sem_wait(pe, done["x1"], count(i - 2, b))
                        for e in range(2):
                            mm = pe.matmul(po[b][:], ct[:, b, e], wo[:, e], start=e == 0, stop=e == 1)
                        mm.then_inc(done["o"], 1)
                    for b in range(B) if stage_c else ():
                        pe.wait_ge(done["xn"], count(i - 2, b))
                        sem_wait(pe, done["xnt"], count(i - 3, b))
                        for e in range(2):
                            mm = pe.transpose(pn[b][:, e], xn[:, b, e * P:(e + 1) * P], ident[:])
                        mm.then_inc(done["xnp"], 1)
                    for b in range(B) if stage_a else ():
                        pe.wait_ge(done["c"], count(i, b))
                        sem_wait(pe, done["ct"], count(i - 1, b))
                        for e in range(2):
                            mm = pe.transpose(pc[b][:, e], c[:, b, e * P:(e + 1) * P], ident[:])
                        mm.then_inc(done["ctp"], 1)
                    for b in range(B) if stage_c else ():
                        pe.wait_ge(done["xnt"], count(i - 2, b))
                        sem_wait(pe, done["l"], count(i - 3, b))
                        for e in range(2):
                            mm = pe.matmul(pl[b][:], xnt[:, b, e], wr[:, e], start=e == 0, stop=e == 1)
                        mm.then_inc(done["lp"], 1)

                stages(tile)(pe)

            @block.vector
            def _(dve):
                dve.memset(eps[:], EPS).then_inc(eps_done, 1)
                dve.wait_ge(consts_in, 64)

                def tile(i, stage_a, stage_b, stage_c):
                    for b in range(B) if stage_a else ():
                        dve.reciprocal(rden[:, b], ctxn[:, :, b, ds(i, 1), D].rearrange("p h t -> p (h t)")).then_inc(done["rden"], 1)
                    for b in range(B) if stage_a else ():
                        sem_wait(dve, done["ctp"], count(i - 1, b))
                        dve.wait_ge(done["rden"], count(i, b))
                        dve.tensor_tensor(c[:, b].rearrange("p (h d) -> p h d", d=D),
                                          ctxn[:, :, b, ds(i, 1), 0:D].rearrange("p h t d -> p (h t) d"),
                                          rden[:, b].rearrange("p (h a) -> p h a", a=1).to_broadcast([P, H, D]), ALU.mult)\
                           .then_inc(done["c"], 1)
                    for b in range(B) if stage_b else ():
                        dve.wait_ge(done["o"], count(i - 1, b))
                        sem_wait(dve, stored[b], 32 * (i - 1))
                        dve.wait_ge(done["xb"], count(i - 1, b))
                        dve.tensor_tensor(x1[:, b], po[b][:], xb[:, b], ALU.add).then_inc(done["x1"], 1)
                    for b in range(B) if stage_b else ():
                        dve.wait_ge(done["x1"], count(i - 1, b))
                        dve.bn_stats(stats[:, b], x1[:, b]).then_inc(done["stats"], 1)
                    for b in range(B) if stage_b else ():
                        sem_wait(dve, done["sd"], count(i - 2, b))
                        wait_apart(dve, done["stats"], count(i - 1, b), done["tick"])
                        dve.bn_aggr(mv[:, b], stats[:, b]).then_inc(done["mv"], 1)
                    for b in range(B) if stage_b else ():
                        dve.wait_ge(done["sd"], count(i - 1, b))
                        dve.reciprocal(rs[:, b:b + 1], sd[:, b:b + 1]).then_inc(done["rs"], 1)
                    for b in range(B) if stage_b else ():
                        sem_wait(dve, done["xnp"], count(i - 2, b))
                        dve.wait_ge(done["rs"], count(i - 1, b))
                        dve.tensor_scalar(xn[:, b], x1[:, b], mv[:, b, 0:1], rs[:, b:b + 1], ALU.subtract, ALU.mult)\
                           .then_inc(done["xn"], 1)
                    for b in range(B) if stage_c else ():
                        dve.wait_ge(done["lp"], count(i - 2, b))
                        dve.tensor_tensor(logits[:, b, ds(i - 2, 1)].rearrange("p t e -> p (t e)"), pl[b][:], br[:], ALU.add)\
                           .then_inc(done["l"], 1)

                def weights(e, k):
                    hi, lo = (w1, w2)[k]
                    dve.wait_ge(hi_done, 2 * e + k + 1)
                    dve.scalar_tensor_tensor(out=lo[:, ds(e, 1)].rearrange("p a n -> p (a n)"), in0=raw[k][:], scalar=WS,
                                             in1=hi[:, ds(e, 1)].rearrange("p a n -> p (a n)"), op0=ALU.mult, op1=ALU.subtract)\
                       .then_inc(lo_done, 1)

                stages(tile, weights)(dve)
                dve.wait_ge(done["l"], NT)
                dve.wait_ge(lo_done, 2 * NE)


def route(nc, io, hbm, logits, gate, slot, owner):
    with ExitStack() as ctx:
        sb = lambda n, s, d=fp32: ctx.enter_context(nc.sbuf_tensor(n, s, d))
        sem = lambda n: ctx.enter_context(nc.semaphore(n))
        xn = sb("r_xn", [P, NT, E])
        ones, below = sb("r_ones", [P, P], bf16), sb("r_below", [P, P], bf16)
        e_of, e_less, starts_at = sb("r_e_of", [P, NT, NE]), sb("r_e_less", [P, NT, NE]), sb("r_starts", [P, SLOT_TILES + 1, NE])
        ione = sb("r_ione", [P, NT])
        best, second, gap, ex = (sb(f"r_{n}", [P, NT]) for n in ("best", "second", "gap", "ex"))
        top = sb("r_top", [P, NT])
        a = [sb(f"r_a{i}", [P, NT, NE]) for i in range(4)]
        oh, ohb = sb("r_oh", [P, NT, NE]), sb("r_ohb", [P, NT, NE], bf16)
        tot, inc, base = (sb(f"r_{n}", [P, NE, NT]) for n in ("tot", "inc", "base"))
        cnt, rem, room, end, start = (sb(f"r_{n}", [P, NE]) for n in ("cnt", "rem", "room", "end", "start"))
        cnti, remi = sb("r_cnti", [P, NE], i32), sb("r_remi", [P, NE], i32)
        slotf = sb("r_slotf", [P, NT])
        own, ownf = sb("r_own", [P, SLOT_TILES + 1, NE]), sb("r_ownf", [P, SLOT_TILES + 1])
        pp = ctx.enter_context(nc.psum_tensor("r_pp", [P, NT * NE], fp32))
        pt = ctx.enter_context(nc.psum_tensor("r_pt", [P, NT * NE], fp32))
        consts, ones_done, below_done, oh_done, ranked = (sem(f"r_{n}") for n in ("consts", "ones_done", "below_done", "oh_done", "ranked"))
        step, gap_done, ex_done, slot_done, xn_in, sent = (sem(f"r_{n}") for n in ("step", "gap_done", "ex_done", "slot_done", "xn_in", "sent"))

        with nc.Block() as block:

            @block.sync
            def _(sp):
                sp.dma_start(xn[:], hbm["xn"].rearrange("(t p) e -> p t e", p=P)).then_inc(xn_in, 16)
                sp.wait_ge(xn_in, 16)

            @block.gpsimd
            def _(pool):
                pool.iota(e_of[:], pattern=[[0, NT], [1, NE]], base=0, channel_multiplier=0, allow_small_or_imprecise_dtypes=True).then_inc(consts, 1)
                pool.iota(e_less[:], pattern=[[0, NT], [1, NE]], base=-NE, channel_multiplier=0, allow_small_or_imprecise_dtypes=True).then_inc(consts, 1)
                pool.iota(starts_at[:], pattern=[[P, SLOT_TILES + 1], [0, NE]], base=0, channel_multiplier=0, allow_small_or_imprecise_dtypes=True).then_inc(consts, 1)
                pool.memset(ione[:], 1.0).then_inc(consts, 1)
                pool.memset(ones[:], 1.0).then_inc(ones_done, 1)
                pool.wait_ge(ones_done, 1)
                pool.affine_select(out=below[:], in_=ones[:], compare_op=ALU.is_gt, fill=0.0, base=0,
                                   pattern=[[1, P]], channel_multiplier=-1).then_inc(below_done, 1)
                pool.wait_ge(below_done, 1)
                pool.wait_ge(slot_done, 1)
                pool.wait_ge(xn_in, 16)
                for t in range(NT):
                    pool.indirect_dma_start(out=hbm["xs"], out_offset=bass.IndirectOffsetOnAxis(ap=slot[:, t:t + 1], axis=0),
                                            in_=xn[:, t], in_offset=None, bounds_check=SLOTS - 1, oob_is_err=True).then_inc(sent, 16)
                pool.wait_ge(sent, 16 * NT)

            @block.scalar
            def _(act):
                act.wait_ge(gap_done, 1)
                act.activation(ex[:], gap[:], ACT.Exp).then_inc(ex_done, 1)

            @block.tensor
            def _(pe):
                pe.wait_ge(below_done, 1)
                pe.wait_ge(oh_done, 1)
                flat = ohb[:].rearrange("p t e -> p (t e)")
                pe.matmul(pp[:], below[:], flat, start=True, stop=True).then_inc(ranked, 1)
                pe.matmul(pt[:], ones[:], flat, start=True, stop=True).then_inc(ranked, 1)

            @block.vector
            def _(dve):
                n = [0]

                def then(ins):
                    n[0] += 1
                    ins.then_inc(step, 1)
                    dve.wait_ge(step, n[0])

                wide = lambda ap, m=NE: ap.rearrange("p (t a) -> p t a", a=1).to_broadcast([P, ap.shape[1], m])
                l = logits[:].rearrange("p b t e -> p (b t) e")
                dve.wait_ge(consts, 4)
                then(dve.tensor_reduce(best[:], l, AX.X, ALU.max))
                then(dve.tensor_tensor(a[0][:], l, wide(best[:]), ALU.is_equal))
                then(dve.tensor_tensor(a[1][:], a[0][:], e_less[:], ALU.mult))
                then(dve.tensor_reduce(top[:], a[1][:], AX.X, ALU.min))
                then(dve.tensor_tensor(oh[:], e_less[:], wide(top[:]), ALU.is_equal))
                dve.tensor_copy(ohb[:], oh[:]).then_inc(oh_done, 1)
                then(dve.scalar_tensor_tensor(out=a[2][:], in0=oh[:], scalar=-3.0e38, in1=l, op0=ALU.mult, op1=ALU.add))
                then(dve.tensor_reduce(second[:], a[2][:], AX.X, ALU.max))
                dve.tensor_tensor(gap[:], second[:], best[:], ALU.subtract).then_inc(gap_done, 1)
                dve.wait_ge(ranked, 2)
                then(dve.tensor_copy(tot[:], pt[:].rearrange("p (t e) -> p e t", e=NE)))
                for e in range(NE):
                    ins = dve.tensor_tensor_scan(inc[:, e], ione[:], tot[:, e], 0.0, ALU.mult, ALU.add)
                    n[0] += 1
                    ins.then_inc(step, 1)
                dve.wait_ge(step, n[0])
                then(dve.tensor_scalar(cnt[:], inc[:, :, NT - 1], float(P - 1), None, ALU.add))
                then(dve.tensor_copy(cnti[:], cnt[:]))
                then(dve.tensor_scalar(remi[:], cnti[:], P - 1, None, ALU.bitwise_and))
                then(dve.tensor_copy(rem[:], remi[:]))
                then(dve.tensor_tensor(room[:], cnt[:], rem[:], ALU.subtract))
                then(dve.tensor_tensor_scan(end[:], ione[:, 0:NE], room[:], 0.0, ALU.mult, ALU.add))
                then(dve.tensor_tensor(start[:], end[:], room[:], ALU.subtract))
                then(dve.tensor_tensor(base[:], inc[:], tot[:], ALU.subtract))
                then(dve.tensor_tensor(tot[:], base[:], wide(start[:], NT), ALU.add))
                then(dve.tensor_tensor(a[3][:], pp[:].rearrange("p (t e) -> p t e", e=NE), tot[:].rearrange("p e t -> p t e"), ALU.add))
                then(dve.tensor_tensor(a[0][:], a[3][:], oh[:], ALU.mult))
                then(dve.tensor_reduce(slotf[:], a[0][:], AX.X, ALU.add))
                dve.tensor_copy(slot[:], slotf[:]).then_inc(slot_done, 1)
                then(dve.tensor_tensor(own[:], starts_at[:], end[:].rearrange("p (a e) -> p a e", a=1).to_broadcast([P, SLOT_TILES + 1, NE]), ALU.is_ge))
                then(dve.tensor_reduce(ownf[:], own[:], AX.X, ALU.add))
                then(dve.tensor_scalar(ownf[:], ownf[:], float(NE - 1), None, ALU.min))
                then(dve.tensor_copy(owner[:], ownf[:]))
                dve.wait_ge(ex_done, 1)
                then(dve.tensor_scalar(ex[:], ex[:], 1.0, None, ALU.add))
                then(dve.reciprocal(gate[:], ex[:]))


def experts(nc, io, hbm, w1, w2, owner):
    with ExitStack() as ctx:
        sb = lambda n, s, d=fp32: ctx.enter_context(nc.sbuf_tensor(n, s, d))
        sem = lambda n: ctx.enter_context(nc.semaphore(n))
        (w1h, w1l), (w2h, w2l) = w1, w2
        KC, IC = E // P, FI // P
        HC = IC // 2
        ident = sb("e_ident", [P, P])
        b1r, b1 = sb("e_b1r", [NE * IC, P]), sb("e_b1", [P, NE * IC])
        b2 = sb("e_b2", [P, NE, E])
        xs = sb("e_xs", [P, 2, E])
        xh, xl = sb("e_xh", [P, 2, KC, P], fp16), sb("e_xl", [P, 2, KC, P], fp16)
        g = sb("e_g", [P, 2, IC, P])
        gh, gl = sb("e_gh", [P, 2, IC, P], fp16), sb("e_gl", [P, 2, IC, P], fp16)
        ys = sb("e_ys", [P, 2, E])
        px = [ctx.enter_context(nc.psum_tensor(f"e_px{k}", [P, KC, P], fp32)) for k in range(2)]
        ph = [ctx.enter_context(nc.psum_tensor(f"e_ph{k}", [P, IC, P], fp32)) for k in range(2)]
        py = [ctx.enter_context(nc.psum_tensor(f"e_py{k}", [P, E], fp32)) for k in range(2)]
        ident_done, b_in, b1_done = sem("e_ident_done"), sem("e_b_in"), sem("e_b1_done")
        b1_turned = sem("e_b1_turned")
        x_in, stored = [sem(f"e_x_in{k}") for k in range(2)], [sem(f"e_stored{k}") for k in range(2)]
        xt_done, xh_done, xl_done, h_done, g_done, gh_done, gl_done, y_done, ys_done = (
            sem(f"e_{n}_done") for n in ("xt", "xh", "xl", "h", "g", "gh", "gl", "y", "ys"))
        xs_h = hbm["xs"].rearrange("(t p) e -> p t e", p=P)
        y_h = hbm["y"].rearrange("(t p) e -> p t e", p=P)
        T2 = (SLOT_TILES + 1) // 2

        def tile_pairs(eng, body):
            body(0, True)
            with eng.Fori(1, T2 - 1) as i:
                body(i, True)
            body(T2 - 1, False)


        with nc.Block() as block:

            @block.sync
            def _(sp):
                sp.dma_start(b1r[:], io["L0_ffn_b1"].rearrange("e (c p) -> (e c) p", p=P)).then_inc(b_in, 16)
                sp.dma_start(b2[:], io["L0_ffn_b2"].rearrange("(a e) n -> a e n", a=1).to_broadcast([P, NE, E])).then_inc(b_in, 16)

                def load(t, k):
                    sp.dma_start(xs[:, k], xs_h[:, ds(t, 1)].rearrange("p t e -> p (t e)")).then_inc(x_in[k], 16)

                def store(t, k):
                    sp.wait_ge(ys_done, t + 1)
                    sp.dma_start(y_h[:, ds(t, 1)].rearrange("p t e -> p (t e)"), ys[:, k]).then_inc(stored[k], 16)

                for k in range(2):
                    load(k, k)
                with sp.Fori(0, T2 - 1) as i:
                    for k in range(2):
                        sp.wait_ge(xt_done, 2 * i + k + 1)
                        load(2 * i + k + 2, k)
                    for k in range(2):
                        store(2 * i + k, k)
                for k in range(2):
                    store(2 * T2 - 2 + k, k)
                for k in range(2):
                    sp.wait_ge(stored[k], 16 * T2)

            @block.gpsimd
            def _(pool):
                make_ident(pool, ident, ident_done)

            @block.tensor
            def _(pe):
                pe.wait_ge(ident_done, 2)
                pe.wait_ge(b_in, 32)
                pe.transpose(px[0][:, 0, 0:NE * IC], b1r[:], ident[0:NE * IC, 0:NE * IC]).then_inc(b1_turned, 1)
                pe.wait_ge(b1_done, 1)

                def turn(i, k):
                    t = 2 * i + k
                    pe.wait_ge(x_in[k], 16 * i + 16)
                    sem_wait(pe, xl_done, t - 1)
                    for c in range(KC):
                        mm = pe.transpose(px[k][:, c], xs[:, k, c * P:(c + 1) * P], ident[:])
                    mm.then_inc(xt_done, 1)

                def up(i, k, e):
                    t = 2 * i + k
                    pe.wait_ge(xl_done, t + 1)
                    sem_wait(pe, g_done, IC * (t - 1))
                    for n in range(IC):
                        terms = [(w, x, c) for w, x in ((w1h, xh), (w1h, xl), (w1l, xh)) for c in range(KC)]
                        for m, (w, x, c) in enumerate(terms):
                            mm = pe.matmul(ph[k][:, n], w[:, ds(e, 1), c * FI + n * P:c * FI + (n + 1) * P].rearrange("p a n -> p (a n)"),
                                           x[:, k, c], start=m == 0, stop=m == len(terms) - 1)
                        if n % HC == HC - 1:
                            mm.then_inc(h_done, 1)

                def down(i, k, e):
                    t = 2 * i + k
                    pe.wait_ge(gl_done, t + 1)
                    sem_wait(pe, ys_done, t - 1)
                    terms = [(x, w, n) for n in range(IC) for x, w in ((gh, w2h), (gl, w2h), (gh, w2l))]
                    for m, (x, w, n) in enumerate(terms):
                        mm = pe.matmul(py[k][:], x[:, k, n], w[:, ds(e, 1), n * E:(n + 1) * E].rearrange("p a n -> p (a n)"),
                                       start=m == 0, stop=m == len(terms) - 1)
                    mm.then_inc(y_done, 1)

                def tiles(i, more):
                    e = [pe.value_load(owner[0:1, ds(2 * i + k, 1)], min_val=0, max_val=NE - 1) for k in range(2)]
                    for k in range(2):
                        up(i, k, e[k])
                    for k in range(2) if more else ():
                        turn(i + 1, k)
                    for k in range(2):
                        down(i, k, e[k])

                for k in range(2):
                    turn(0, k)
                tile_pairs(pe, tiles)

            @block.scalar
            def _(act):
                act.wait_ge(b1_turned, 1)
                act.activation(b1[:], px[0][:, 0, 0:NE * IC], ACT.Copy).then_inc(b1_done, 1)
                act.wait_ge(b1_done, 1)

                def high(i, k):
                    t = 2 * i + k
                    act.wait_ge(xt_done, t + 1)
                    sem_wait(act, h_done, 2 * (t - 1))
                    act.activation(xh[:, k], px[k][:], ACT.Copy).then_inc(xh_done, 1)

                def tiles(i, more):
                    e = [act.value_load(owner[0:1, ds(2 * i + k, 1)], min_val=0, max_val=NE - 1) for k in range(2)]
                    for k in range(2):
                        t = 2 * i + k
                        sem_wait(act, gl_done, t - 1)
                        for n in range(IC):
                            if n % HC == 0:
                                act.wait_ge(h_done, 2 * t + n // HC + 1)
                            act.activation(g[:, k, n], ph[k][:, n], ACT.Gelu, bias=b1[:, ds(e[k] * IC + n, 1)], scale=1.0 / WS)\
                               .then_inc(g_done, 1)
                    for k in range(2) if more else ():
                        high(i + 1, k)

                for k in range(2):
                    high(0, k)
                tile_pairs(act, tiles)

            @block.vector
            def _(dve):
                def low(i, k):
                    dve.wait_ge(xh_done, 2 * i + k + 1)
                    dve.tensor_tensor(xl[:, k], px[k][:], xh[:, k], ALU.subtract).then_inc(xl_done, 1)

                def tiles(i, more):
                    e = [dve.value_load(owner[0:1, ds(2 * i + k, 1)], min_val=0, max_val=NE - 1) for k in range(2)]
                    for k in range(2):
                        t = 2 * i + k
                        dve.wait_ge(g_done, IC * (t + 1))
                        sem_wait(dve, y_done, t - 1)
                        dve.tensor_copy(gh[:, k], g[:, k]).then_inc(gh_done, 1)
                        dve.wait_ge(gh_done, t + 1)
                        dve.tensor_tensor(gl[:, k], g[:, k], gh[:, k], ALU.subtract).then_inc(gl_done, 1)
                    for k in range(2) if more else ():
                        low(i + 1, k)
                    for k in range(2):
                        t = 2 * i + k
                        dve.wait_ge(y_done, t + 1)
                        sem_wait(dve, stored[k], 16 * i)
                        dve.scalar_tensor_tensor(out=ys[:, k], in0=py[k][:], scalar=1.0 / WS,
                                                 in1=b2[:, ds(e[k], 1)].rearrange("p a n -> p (a n)"), op0=ALU.mult, op1=ALU.add)\
                           .then_inc(ys_done, 1)

                dve.wait_ge(b_in, 32)
                for k in range(2):
                    low(0, k)
                tile_pairs(dve, tiles)


def gather(nc, hbm, out, gate, slot):
    with ExitStack() as ctx:
        sb = lambda n, s, d=fp32: ctx.enter_context(nc.sbuf_tensor(n, s, d))
        sem = lambda n: ctx.enter_context(nc.semaphore(n))
        CH = 8
        y, x1 = sb("g_y", [P, NT, E]), sb("g_x1", [P, NT, E])
        y_in = [sem(f"g_y_in{i}") for i in range(NT // CH)]
        x_in, done, stored = sem("g_x_in"), sem("g_done"), sem("g_stored")
        out_h = out.rearrange("b (t p) e -> p (b t) e", p=P)

        with nc.Block() as block:

            @block.gpsimd
            def _(pool):
                for t in range(NT):
                    pool.indirect_dma_start(out=y[:, t], out_offset=None, in_=hbm["y"],
                                            in_offset=bass.IndirectOffsetOnAxis(ap=slot[:, t:t + 1], axis=0),
                                            bounds_check=SLOTS - 1, oob_is_err=True).then_inc(y_in[t // CH], 16)

            @block.vector
            def _(dve):
                dve.wait_ge(x_in, 16)
                for t in range(NT):
                    dve.wait_ge(y_in[t // CH], 16 * CH)
                    dve.scalar_tensor_tensor(out=x1[:, t], in0=y[:, t], scalar=gate[:, t:t + 1], in1=x1[:, t], op0=ALU.mult, op1=ALU.add)\
                       .then_inc(done, 1)

            @block.sync
            def _(sp):
                sp.dma_start(x1[:], hbm["x1"].rearrange("(t p) e -> p t e", p=P)).then_inc(x_in, 16)
                for c in range(NT // CH):
                    sp.wait_ge(done, CH * (c + 1))
                    sp.dma_start(out_h[:, c * CH:(c + 1) * CH], x1[:, c * CH:(c + 1) * CH]).then_inc(stored, 16)
                sp.wait_ge(stored, 16 * (NT // CH))


def build(nc, io, out):
    hbm = scratch(nc)
    project(nc, io, hbm)
    with ExitStack() as ctx:
        sb = lambda n, s, d=fp32: ctx.enter_context(nc.sbuf_tensor(n, s, d))
        logits = sb("logits", [P, B, ST, NE])
        gate, slot, owner = sb("gate", [P, NT]), sb("slot", [P, NT], u32), sb("owner", [P, SLOT_TILES + 1], i32)
        with ExitStack() as attention:
            ctxn = attention.enter_context(nc.sbuf_tensor("ctxn", [P, H, B, ST, D + 1], fp32, side="right"))
            far(nc, hbm, ctxn)
            near(nc, hbm, ctxn)
            w1 = [sb(f"w1{n}", [P, NE, 2 * FI], fp16) for n in "hl"]
            w2 = [sb(f"w2{n}", [P, NE, 2 * FI], fp16) for n in "hl"]
            combine(nc, io, hbm, ctxn, w1, w2, logits)
        route(nc, io, hbm, logits, gate, slot, owner)
        experts(nc, io, hbm, w1, w2, owner)
        gather(nc, hbm, out, gate, slot)


def kernel(**inputs):
    import numpy as np
    import concourse.bacc as bacc
    from concourse.bass_utils import run_bass_kernel_spmd

    nc = bacc.Bacc("TRN2", target_bir_lowering=False, num_devices=1)
    arrays, io = {}, {}
    for name, value in inputs.items():
        a = np.ascontiguousarray(value)
        arrays[f"in_{name}"] = a
        io[name] = nc.dram_tensor(f"in_{name}", a.shape, mybir.dt.from_np(a.dtype), kind="ExternalInput").ap()
    out = nc.dram_tensor("out", (B, S, E), fp32, kind="ExternalOutput").ap()
    build(nc, io, out)
    r = run_bass_kernel_spmd(nc, [arrays], core_ids=[0])
    return r.results[0]["out"]
```
